# Optimizing a Trainium2 kernel written in Bass

```python
import numpy as np
import jax
import jax.numpy as jnp

def _softmax(x, axis=-1):
    return jax.nn.softmax(x, axis=axis)

def _gelu(x):
    return jax.nn.gelu(x, approximate=True)

def _silu(x):
    return jax.nn.silu(x)

def _sigmoid(x):
    return jax.nn.sigmoid(x)

def _layernorm(x, axis=-1, eps=1e-05):
    m = jnp.mean(x, axis=axis, keepdims=True)
    v = jnp.var(x, axis=axis, keepdims=True)
    return (x - m) / jnp.sqrt(v + eps)

def _scatter_add(tgt, idx, src, axis=0):
    return tgt.at[idx].add(src)

def _segment_sum(src, seg, n):
    return jax.ops.segment_sum(src, seg, n)
kernel_name = 'mk_lm_tower_d1_tok_ids2048_r4_4705dd'

def setup_inputs(seed: int=0):
    np.random.seed(seed)
    _w = jnp.asarray

    def _rec_inputs():
        import jax
        import jax.numpy as jnp
        _rk = jax.random.key(seed)
        x = jax.random.randint(jax.random.fold_in(_rk, 1), (8, 256), 0, 127998, jnp.int32)
        return x
    x = _rec_inputs()

    def _L0_tok_setup():
        import jax, jax.numpy as jnp
        import numpy as np
        VOCAB = 32000
        D_MODEL = 512
        LATENT = 128
        NUM_HOT = 8000

        def _maps(hot_token_ids, vocab):
            hot_mask = jnp.zeros((vocab,), dtype=bool).at[hot_token_ids].set(True)
            tok2hot = jnp.full((vocab,), 0, dtype=jnp.int32).at[hot_token_ids].set(jnp.arange(hot_token_ids.shape[0], dtype=jnp.int32))
            tok2cold = jnp.cumsum((~hot_mask).astype(jnp.int32)) - 1
            tok2cold = jnp.clip(tok2cold, 0, None)
            return (hot_mask, tok2hot, tok2cold)
        key = jax.random.key(seed)
        k1, k2, k3, k4 = jax.random.split(key, 4)
        input_ids = jax.random.randint(k1, (4, 1024), 0, VOCAB, dtype=jnp.int64 if jax.config.jax_enable_x64 else jnp.int32)
        hot_token_ids = jnp.arange(NUM_HOT, dtype=jnp.int32)
        hot_emb_w = jax.random.normal(k2, (NUM_HOT, D_MODEL), dtype=jnp.float32)
        cold_emb_w = jax.random.normal(k3, (VOCAB - NUM_HOT, LATENT), dtype=jnp.float32)
        proj_w = jax.random.normal(k4, (D_MODEL, LATENT), dtype=jnp.float32) / np.sqrt(LATENT)
        return {'input_ids': input_ids, 'hot_token_ids': hot_token_ids, 'hot_emb_w': hot_emb_w, 'cold_emb_w': cold_emb_w, 'proj_w': proj_w}
    _L0_tok_all = _L0_tok_setup()
    _L0_tok_in = {k: v for k, v in _L0_tok_all.items() if k in ('hot_token_ids', 'hot_emb_w', 'cold_emb_w', 'proj_w')}
    del _L0_tok_all

    def _L0_attn_setup():
        import jax, jax.numpy as jnp
        import numpy as np
        D_MODEL = 512
        N_HEADS = 32
        N_KV_HEADS = 8
        HEAD_DIM = D_MODEL // N_HEADS
        N_REP = N_HEADS // N_KV_HEADS
        SCALE = HEAD_DIM ** (-0.5)

        def _rope_tables(seq_len):
            inv_freq = 1.0 / 10000.0 ** (jnp.arange(0, HEAD_DIM, 2, dtype=jnp.float32) / HEAD_DIM)
            t = jnp.arange(seq_len, dtype=jnp.float32)
            freqs = jnp.outer(t, inv_freq)
            return (jnp.cos(freqs), jnp.sin(freqs))

        def _apply_rope(x, cos, sin):
            x_r, x_i = (x[..., ::2], x[..., 1::2])
            out_r = x_r * cos - x_i * sin
            out_i = x_r * sin + x_i * cos
            out = jnp.stack([out_r, out_i], axis=-1)
            return out.reshape(x.shape)
        key = jax.random.key(seed)
        ks = jax.random.split(key, 5)
        bs, seq_len = (2, 512)
        std = D_MODEL ** (-0.5)
        x = jax.random.normal(ks[0], (bs, seq_len, D_MODEL), dtype=jnp.float32)
        wq = jax.random.normal(ks[1], (N_HEADS * HEAD_DIM, D_MODEL), dtype=jnp.float32) * std
        wk = jax.random.normal(ks[2], (N_KV_HEADS * HEAD_DIM, D_MODEL), dtype=jnp.float32) * std
        wv = jax.random.normal(ks[3], (N_KV_HEADS * HEAD_DIM, D_MODEL), dtype=jnp.float32) * std
        wo = jax.random.normal(ks[4], (D_MODEL, N_HEADS * HEAD_DIM), dtype=jnp.float32) * std
        return {'x': x, 'wq': wq, 'wk': wk, 'wv': wv, 'wo': wo}
    _L0_attn_all = _L0_attn_setup()
    _L0_attn_in = {k: v for k, v in _L0_attn_all.items() if k in ('wq', 'wk', 'wv', 'wo')}
    del _L0_attn_all

    def _L0_ffn_setup():
        import jax, jax.numpy as jnp
        import numpy as np
        NUM_EXPERTS = 32
        TOP_K = 8
        THRESHOLD = 0.8
        HIDDEN = 512
        INTER = 192
        key = jax.random.key(seed)
        k1, k2, k3, k4 = jax.random.split(key, 4)
        hidden_states = jax.random.normal(k1, (2, 256, HIDDEN), jnp.float32)
        gate_weight = jax.random.normal(k2, (NUM_EXPERTS, HIDDEN), jnp.float32) * 0.02
        gate_up_proj = jax.random.normal(k3, (NUM_EXPERTS, 2 * INTER, HIDDEN), jnp.float32) * 0.02
        down_proj = jax.random.normal(k4, (NUM_EXPERTS, HIDDEN, INTER), jnp.float32) * 0.02
        return {'hidden_states': hidden_states, 'gate_weight': gate_weight, 'gate_up_proj': gate_up_proj, 'down_proj': down_proj}
    _L0_ffn_all = _L0_ffn_setup()
    _L0_ffn_in = {k: v for k, v in _L0_ffn_all.items() if k in ('gate_weight', 'gate_up_proj', 'down_proj')}
    del _L0_ffn_all
    return {'x': x, 'L0_tok_hot_token_ids': _L0_tok_in['hot_token_ids'], 'L0_tok_hot_emb_w': _L0_tok_in['hot_emb_w'], 'L0_tok_cold_emb_w': _L0_tok_in['cold_emb_w'], 'L0_tok_proj_w': _L0_tok_in['proj_w'], 'L0_attn_wq': _L0_attn_in['wq'], 'L0_attn_wk': _L0_attn_in['wk'], 'L0_attn_wv': _L0_attn_in['wv'], 'L0_attn_wo': _L0_attn_in['wo'], 'L0_ffn_gate_weight': _L0_ffn_in['gate_weight'], 'L0_ffn_gate_up_proj': _L0_ffn_in['gate_up_proj'], 'L0_ffn_down_proj': _L0_ffn_in['down_proj']}

def reference(x, L0_tok_hot_token_ids, L0_tok_hot_emb_w, L0_tok_cold_emb_w, L0_tok_proj_w, L0_attn_wq, L0_attn_wk, L0_attn_wv, L0_attn_wo, L0_ffn_gate_weight, L0_ffn_gate_up_proj, L0_ffn_down_proj):
    import jax
    import jax.numpy as jnp

    def _L0_tok_ref(input_ids, hot_token_ids, hot_emb_w, cold_emb_w, proj_w):
        import jax, jax.numpy as jnp
        import numpy as np
        VOCAB = 32000
        D_MODEL = 512
        LATENT = 128
        NUM_HOT = 8000

        def _maps(hot_token_ids, vocab):
            hot_mask = jnp.zeros((vocab,), dtype=bool).at[hot_token_ids].set(True)
            tok2hot = jnp.full((vocab,), 0, dtype=jnp.int32).at[hot_token_ids].set(jnp.arange(hot_token_ids.shape[0], dtype=jnp.int32))
            tok2cold = jnp.cumsum((~hot_mask).astype(jnp.int32)) - 1
            tok2cold = jnp.clip(tok2cold, 0, None)
            return (hot_mask, tok2hot, tok2cold)
        hot_mask, tok2hot, tok2cold = _maps(hot_token_ids, VOCAB)
        flat = input_ids.reshape(-1)
        is_hot = hot_mask[flat]
        hot_vec = hot_emb_w[tok2hot[flat]]
        cold_lat = cold_emb_w[tok2cold[flat]]
        cold_vec = cold_lat @ proj_w.T
        out = jnp.where(is_hot[:, None], hot_vec, cold_vec)
        return out.reshape(*input_ids.shape, D_MODEL)

    def _L0_attn_ref(x, wq, wk, wv, wo):
        import jax, jax.numpy as jnp
        import numpy as np
        D_MODEL = 512
        N_HEADS = 32
        N_KV_HEADS = 8
        HEAD_DIM = D_MODEL // N_HEADS
        N_REP = N_HEADS // N_KV_HEADS
        SCALE = HEAD_DIM ** (-0.5)

        def _rope_tables(seq_len):
            inv_freq = 1.0 / 10000.0 ** (jnp.arange(0, HEAD_DIM, 2, dtype=jnp.float32) / HEAD_DIM)
            t = jnp.arange(seq_len, dtype=jnp.float32)
            freqs = jnp.outer(t, inv_freq)
            return (jnp.cos(freqs), jnp.sin(freqs))

        def _apply_rope(x, cos, sin):
            x_r, x_i = (x[..., ::2], x[..., 1::2])
            out_r = x_r * cos - x_i * sin
            out_i = x_r * sin + x_i * cos
            out = jnp.stack([out_r, out_i], axis=-1)
            return out.reshape(x.shape)
        bs, seq_len, _ = x.shape
        q = (x @ wq.T).reshape(bs, seq_len, N_HEADS, HEAD_DIM).transpose(0, 2, 1, 3)
        k = (x @ wk.T).reshape(bs, seq_len, N_KV_HEADS, HEAD_DIM).transpose(0, 2, 1, 3)
        v = (x @ wv.T).reshape(bs, seq_len, N_KV_HEADS, HEAD_DIM).transpose(0, 2, 1, 3)
        cos, sin = _rope_tables(seq_len)
        q = _apply_rope(q, cos, sin)
        k = _apply_rope(k, cos, sin)
        k = jnp.repeat(k, N_REP, axis=1)
        v = jnp.repeat(v, N_REP, axis=1)
        attn = jnp.einsum('bhqd,bhkd->bhqk', q, k) * SCALE
        causal = jnp.triu(jnp.ones((seq_len, seq_len), dtype=bool), k=1)
        attn = jnp.where(causal, -jnp.inf, attn)
        attn = jax.nn.softmax(attn, axis=-1)
        out = jnp.einsum('bhqk,bhkd->bhqd', attn, v)
        out = out.transpose(0, 2, 1, 3).reshape(bs, seq_len, D_MODEL)
        return out @ wo.T

    def _L0_ffn_ref(hidden_states, gate_weight, gate_up_proj, down_proj):
        import jax, jax.numpy as jnp
        import numpy as np
        NUM_EXPERTS = 32
        TOP_K = 8
        THRESHOLD = 0.8
        HIDDEN = 512
        INTER = 192
        B, S, H = hidden_states.shape
        x = hidden_states.reshape(-1, H)
        logits = x @ gate_weight.T
        probs = jax.nn.softmax(logits.astype(jnp.float32), axis=-1).astype(logits.dtype)
        top_vals, top_idx = jax.lax.top_k(probs, TOP_K)
        renorm = top_vals / jnp.clip(jnp.sum(top_vals, axis=-1, keepdims=True), 1e-12)
        cum = jnp.cumsum(renorm, axis=-1)
        num_keep = jnp.minimum(jnp.sum((cum < THRESHOLD).astype(jnp.int32), axis=-1) + 1, TOP_K)
        active = jnp.arange(TOP_K)[None, :] < num_keep[:, None]
        rw = top_vals * active.astype(top_vals.dtype)
        rw = rw / jnp.clip(jnp.sum(rw, axis=-1, keepdims=True), 1e-12)
        combine = jnp.sum(jax.nn.one_hot(top_idx, NUM_EXPERTS, dtype=rw.dtype) * rw[..., None], axis=1)

        def body(acc, params):
            w_gu, w_d, ce = params
            gu = x @ w_gu.T
            g, u = jnp.split(gu, 2, axis=-1)
            h = jax.nn.silu(g) * u
            return (acc + h @ w_d.T * ce[:, None], None)
        out, _ = jax.lax.scan(body, jnp.zeros_like(x), (gate_up_proj, down_proj, combine.T))
        return out.reshape(B, S, H)
    h = _L0_tok_ref(x, L0_tok_hot_token_ids, L0_tok_hot_emb_w, L0_tok_cold_emb_w, L0_tok_proj_w)
    h = h + _L0_attn_ref(_layernorm(h, axis=-1), L0_attn_wq, L0_attn_wk, L0_attn_wv, L0_attn_wo)
    h = h + _L0_ffn_ref(_layernorm(h, axis=-1), L0_ffn_gate_weight, L0_ffn_gate_up_proj, L0_ffn_down_proj)
    return h

_drawn_inputs = setup_inputs


def setup_inputs(seed=0):
    import zlib

    import numpy as np

    out = dict(_drawn_inputs(seed))
    spreads = {}
    factors = {'L0_ffn_gate_weight': 6.548, 'L0_ffn_gate_up_proj': 5.516, 'L0_ffn_down_proj': 5.627}
    for name, (base, spread) in spreads.items():
        noise = np.random.default_rng([zlib.crc32(name.encode()), seed]).standard_normal(out[name].shape)
        drawn = base * np.exp(spread * noise) if base else spread * noise
        out[name] = jnp.asarray(drawn.astype(out[name].dtype))
    for name, factor in factors.items():
        out[name] = (out[name] * factor).astype(out[name].dtype)
    return out
```

```python
from contextlib import ExitStack

import numpy as np
import concourse.bass as bass
from concourse import mybir

F32 = mybir.dt.float32
F32R = mybir.dt.float32r
BF16 = mybir.dt.bfloat16
I32 = mybir.dt.int32
ALU = mybir.AluOpType
ACT = mybir.ActivationFunctionType
AX = mybir.AxisListType

P = 128
BATCH, SEQ = 8, 256
TOK = BATCH * SEQ
NT = TOK // P
D = 512
KC = D // P
VOCAB, HOT, LATENT = 32000, 8000, 128
COLD = VOCAB - HOT
VR, VC = 125, 256
HR, HC = 125, 64
HOT_UNIT = 8192.0
EPS = 1e-5

CI, CT, CN, CP = 0, 128, 256, 512
CST_COLS = CP + 5


def constants():
    c = np.zeros((P, CST_COLS), np.float32)
    p = np.arange(P)
    c[:, CI:CI + P] = np.eye(P)
    c[:, CT:CT + P] = p[:, None] < p[None, :]
    c[:, CN:CN + VC] = np.arange(VC)
    c[:, CP] = p
    c[:, CP + 1] = HC * (HOT_UNIT / HC + p)
    c[:, CP + 2] = VC * p
    c[:, CP + 3] = p % 32 < 16
    c[:, CP + 4] = p % 32 >= 16
    return c


class Chip:
    pass


def linker(eng, sem):
    count = [0]

    def link(ins, base=0):
        count[0] += 1
        ins.then_inc(sem, 1)
        eng.wait_ge(sem, base + count[0])

    return link


def rsqrt(dve, sem, at, out, var, root):
    y = out
    dve.reciprocal(y, root).then_inc(sem, 1)
    dve.wait_ge(sem, at + 1)
    dve.tensor_tensor(root, y, y, ALU.mult).then_inc(sem, 1)
    dve.wait_ge(sem, at + 2)
    dve.tensor_tensor(root, root, var, ALU.mult).then_inc(sem, 1)
    dve.wait_ge(sem, at + 3)
    dve.tensor_scalar(root, root, -0.5, 1.5, ALU.mult, ALU.add).then_inc(sem, 1)
    dve.wait_ge(sem, at + 4)
    dve.tensor_tensor(out, y, root, ALU.mult).then_inc(sem, 1)
    dve.wait_ge(sem, at + 5)


def moments(dve, sem, at, stats, mean, var, calc):
    dve.tensor_tensor(mean, stats[:, :, 1], stats[:, :, 4], ALU.add)
    dve.tensor_tensor(calc, stats[:, :, 1], stats[:, :, 4], ALU.subtract).then_inc(sem, 1)
    dve.wait_ge(sem, at + 1)
    dve.tensor_scalar(mean, mean, 0.5, None, ALU.mult)
    dve.scalar_tensor_tensor(calc, calc, 0.25, calc, ALU.mult, ALU.mult)
    dve.tensor_tensor(var, stats[:, :, 2], stats[:, :, 5], ALU.add).then_inc(sem, 1)
    dve.wait_ge(sem, at + 2)
    dve.scalar_tensor_tensor(calc, var, 1.0 / D, calc, ALU.mult, ALU.add).then_inc(sem, 1)
    dve.wait_ge(sem, at + 3)
    dve.tensor_scalar(var, calc, EPS, None, ALU.add).then_inc(sem, 1)
    dve.wait_ge(sem, at + 4)


def embed(nc, t, ids, hot_ids, hot_w, cold_w, proj, cst, table):
    NB = 4
    with ExitStack() as ctx:
        sb = lambda n, s, d: ctx.enter_context(nc.sbuf_tensor(n, s, d))
        pb = lambda n, s, d: ctx.enter_context(nc.psum_tensor(n, s, d))
        sem = lambda n: ctx.enter_context(nc.semaphore(n))
        tok = sb("tok", [P, NT], I32)
        tok_neg = sb("tok_neg", [P, NT], I32)
        tokf = sb("tokf", [P, NT], F32)
        hid = sb("hid", [HR, HC], I32)
        hneg = sb("hneg", [HR, HC], I32)
        hi = sb("hi", [HR, 2, HC], I32)
        hf = sb("hf", [HR, 2, HC], F32)
        count_row = sb("count_row", [P, VC], BF16)
        row_hot = sb("row_hot", [HR, NB, 2, VR], BF16)
        col_hot = sb("col_hot", [HR, NB, VC], BF16)
        zero = sb("zero", [HR, VC], BF16)
        ones = sb("ones", [P, VC], F32)
        hits = sb("hits", [VR, VC], F32)
        is_hot = sb("is_hot", [VR, VC], F32)
        run = sb("run", [VR, VC], F32)
        calc = sb("calc", [VR, VC], F32)
        side = sb("side", [VR, 4], F32)
        flag = sb("flag", [1, 1], I32)
        rows = sb("rows", [VR, VC, 4], I32)
        look = sb("look", [P, NT, 4], I32)
        hot_at = sb("hot_at", [P, NT], I32)
        cold = sb("cold", [P, NT], I32)
        lat = sb("lat", [P, NB, LATENT], F32)
        row = sb("row", [P, NB, D], F32)
        stats = sb("stats", [P, NT, 6], F32)
        take = sb("take", [P, NB], I32)
        ln_calc = sb("ln_calc", [P, 2, NT], F32)
        latT = sb("latT", [P, 2, P], F32)
        pj = sb("proj_sb", [P, D], F32)
        all_i = sb("all_i", [P, HOT], I32)
        all_f = sb("all_f", [P, HOT], F32)
        order = sb("order", [P, HOT], F32)
        best = sb("best", [P, 2], F32)

        count = pb("count", [P, 512], F32)
        small = pb("small", [P, 512], F32)
        turned = pb("turned", [P, 2, 512], F32)
        projected = pb("projected", [P, 2, 512], F32)

        s_ids = sem("s_ids")
        s_hid = sem("s_hid")
        s_cst = sem("s_cst")
        s_pj = sem("s_pj")
        s_v = sem("s_v")
        s_onehot = sem("s_onehot")
        s_counted = sem("s_counted")
        s_total = sem("s_total")
        s_scan = sem("s_scan")
        s_inputs = sem("s_inputs")
        s_prefix = sem("s_prefix")
        s_rows = sem("s_rows")
        s_flag = sem("s_flag")
        s_tok = sem("s_tok")
        s_table = sem("s_table")
        s_look = sem("s_look")
        s_index = sem("s_index")
        s_hot = [sem(f"s_hot{b}") for b in range(NB)]
        s_lat = [sem(f"s_lat{b}") for b in range(NB)]
        s_turned = sem("s_turned")
        s_latT = sem("s_latT")
        s_proj = sem("s_proj")
        s_token = sem("s_token")
        s_all = sem("s_all")
        s_done = sem("s_done")
        s_kept = sem("s_kept")
        s_take = sem("s_take")
        s_stat = sem("s_stat")
        s_var = sem("s_var")
        s_sqrt = sem("s_sqrt")
        block = ctx.enter_context(nc.Block())

        iota = t.cst[:, CN:CN + VC]

        @block.sync
        def _(sp):
            sp.dma_start(hid[:], hot_ids.rearrange("(p c) -> p c", c=HC)).then_inc(s_hid, 16)
            sp.dma_start(t.cst[:], cst).then_inc(s_cst, 16)
            sp.dma_start(tok[:], ids).then_inc(s_ids, 16)
            sp.dma_start(pj[:], proj).then_inc(s_pj, 16)
            sp.wait_ge(s_rows, 1)
            sp.dma_start(table.rearrange("(p c) k -> p c k", c=VC), rows[:]).then_inc(s_table, 16)
            sp.wait_ge(s_flag, 1)
            twice = sp.value_load(flag[0:1, 0:1], min_val=0, max_val=1)
            with sp.If(twice > 0):
                sp.dma_start(all_i[:], hot_ids.rearrange("(a c) -> a c", a=1).broadcast_to([P, HOT])).then_inc(s_all, 16)
            sp.wait_ge(s_table, 16)

        @block.gpsimd
        def _(pool):
            pool.wait_ge(s_table, 16)
            pool.wait_ge(s_tok, 1)
            for j in range(NT):
                pool.indirect_dma_start(look[:, j, :], None, table, bass.IndirectOffsetOnAxis(ap=tok[:, j:j + 1], axis=0),
                                        bounds_check=VOCAB - 1, oob_is_err=False).then_inc(s_look, 16)
            pool.wait_ge(s_index, 1)
            for j in range(NT):
                b, k = j % NB, j // NB
                if k:
                    pool.wait_ge(s_hot[b], 16 * k)
                    pool.wait_ge(s_turned, NB * (k - 1) + b + 1)
                    pool.wait_ge(s_kept, NB * (k - 1) + b + 1)
                    pool.wait_ge(s_stat, NB * (k - 1) + b + 1)
                pool.indirect_dma_start(lat[:, b, :], None, cold_w, bass.IndirectOffsetOnAxis(ap=cold[:, j:j + 1], axis=0),
                                        bounds_check=COLD - 1, oob_is_err=False).then_inc(s_lat[b], 16)
                pool.indirect_dma_start(row[:, b, :], None, hot_w, bass.IndirectOffsetOnAxis(ap=hot_at[:, j:j + 1], axis=0),
                                        bounds_check=HOT - 1, oob_is_err=False).then_inc(s_hot[b], 16)

        @block.tensor
        def _(pe):
            pe.wait_ge(s_v, 1)
            pe.matmul(count[0:VR, 0:VC], zero[:, 0:VR], zero[:], start=True, stop=False)
            with pe.Fori(0, HC // NB) as i:
                for b in range(NB):
                    pe.wait_ge(s_onehot, i * NB + (b + 1))
                    pe.matmul(count[0:VR, 0:VC], row_hot[:, b, 0, :], col_hot[:, b, :], start=False, stop=False)
                    pe.matmul(count[0:VR, 0:VC], row_hot[:, b, 1, :], col_hot[:, b, :], start=False,
                              stop=False).then_inc(s_counted, 1)
            pe.matmul(count[0:VR, 0:VC], zero[:, 0:VR], zero[:], start=False, stop=True).then_inc(s_total, 1)
            pe.wait_ge(s_scan, 1)
            pe.matmul(small[0:VR, 0:1], t.cst[0:VR, CT:CT + VR], run[:, VC - 1:VC], start=True, stop=True)
            pe.matmul(small[0:1, 1:2], ones[0:VR, 0:1], side[:, 1:2], start=True, stop=True).then_inc(s_prefix, 1)
            pe.wait_ge(s_pj, 16)
            with pe.Fori(0, NT // NB) as i:
                for b in range(NB):
                    o = b % 2
                    pe.wait_ge(s_lat[b], i * 16 + 16)
                    pe.transpose(turned[:, o, 0:P], lat[:, b, :], t.cst[:, CI:CI + P]).then_inc(s_turned, 1)
                    pe.wait_ge(s_latT, i * NB + (b + 1))
                    pe.wait_ge(s_token, i * NB + b)
                    pe.matmul(projected[:, o, :], latT[:, o, :], pj[:], start=True, stop=True).then_inc(s_proj, 1)

        @block.scalar
        def _(act):
            with act.Fori(0, NT // NB) as i:
                for b in range(NB):
                    o = b % 2
                    act.wait_ge(s_turned, i * NB + (b + 1))
                    act.copy(latT[:, o, :], turned[:, o, 0:P]).then_inc(s_latT, 1)
                    act.wait_ge(s_token, i * NB + (b + 1))
                    act.copy(t.h[:, bass.ds(i * NB + b, 1), :].rearrange("p a d -> p (a d)"), row[:, b, :]).then_inc(s_kept, 1)
            act.wait_ge(s_var, 1)
            act.activation(ln_calc[:, 0, :], ln_calc[:, 1, :], ACT.Sqrt).then_inc(s_sqrt, 1)

        @block.vector
        def _(dve):
            link = linker(dve, s_v)
            link(dve.memset(zero[:], 0.0))
            dve.memset(ones[:], 1.0).then_inc(s_done, 1)
            dve.wait_ge(s_hid, 16)
            link(dve.tensor_scalar(hneg[:], hid[:], 0, VOCAB, ALU.is_lt, ALU.mult))
            link(dve.tensor_tensor(hid[:], hid[:], hneg[:], ALU.add))
            dve.tensor_scalar(hi[:, 0, :], hid[:], 8, None, ALU.arith_shift_right).then_inc(s_done, 1)
            link(dve.tensor_scalar(hi[:, 1, :], hid[:], VC - 1, None, ALU.bitwise_and))
            dve.wait_ge(s_done, 2)
            link(dve.tensor_copy(hf[:], hi[:]))
            dve.wait_ge(s_cst, 16)
            link(dve.tensor_copy(count_row[:], iota))
            with dve.Fori(0, HC // NB) as i:
                for b in range(NB):
                    c = i * NB + b
                    if b == 0:
                        dve.wait_ge(s_counted, i * NB)
                    row_id, col_id = hf[:, 0, bass.ds(c, 1)], hf[:, 1, bass.ds(c, 1)]
                    dve.tensor_scalar(row_hot[:, b, 0, :], count_row[0:HR, 0:VR], row_id, t.cst[0:HR, CP + 1:CP + 2],
                                      ALU.is_equal, ALU.mult)
                    dve.tensor_scalar(row_hot[:, b, 1, :], count_row[0:HR, 0:VR], row_id, t.cst[0:HR, bass.ds(c + CN, 1)],
                                      ALU.is_equal, ALU.mult)
                    dve.tensor_scalar(col_hot[:, b, :], count_row[0:HR, :], col_id, None, ALU.is_equal).then_inc(s_onehot, 1)
            dve.wait_ge(s_ids, 16)
            link(dve.tensor_scalar(tok_neg[:], tok[:], 0, VOCAB, ALU.is_lt, ALU.mult))
            link(dve.tensor_tensor(tok[:], tok[:], tok_neg[:], ALU.add))
            link(dve.tensor_scalar(tok[:], tok[:], 0, VOCAB - 1, ALU.max, ALU.min))
            dve.tensor_copy(tokf[:], tok[:]).then_inc(s_tok, 1)
            dve.wait_ge(s_total, 1)
            link(dve.tensor_copy(hits[:], count[0:VR, 0:VC]))
            dve.memset(rows[:], 0).then_inc(s_done, 1)
            dve.tensor_reduce(side[:, 0:1], hits[:], AX.X, ALU.max).then_inc(s_done, 1)
            link(dve.tensor_scalar(is_hot[:], hits[:], HOT_UNIT, None, ALU.is_ge))
            dve.wait_ge(s_done, 4)
            dve.tensor_scalar(side[:, 1:2], side[:, 0:1], 2 * HOT_UNIT, None, ALU.is_ge).then_inc(s_done, 1)
            link(dve.tensor_tensor_scan(run[:], ones[0:VR, :], is_hot[:], 0.0, ALU.mult, ALU.add))
            dve.wait_ge(s_done, 5)
            dve.nop().then_inc(s_scan, 1)
            link(dve.scalar_tensor_tensor(calc[:], is_hot[:], -HOT_UNIT, hits[:], ALU.mult, ALU.add))
            link(dve.tensor_scalar(rows[:, :, 0], calc[:], float(HOT - 1), None, ALU.min))
            link(dve.scalar_tensor_tensor(calc[:], iota[0:VR, :], t.cst[0:VR, CP + 2:CP + 3], run[:], ALU.add, ALU.subtract))
            dve.wait_ge(s_prefix, 1)
            dve.tensor_scalar(flag[:], small[0:1, 1:2], 0.0, None, ALU.is_gt).then_inc(s_flag, 1)
            link(dve.tensor_copy(side[:, 2:3], small[0:VR, 0:1]))
            link(dve.tensor_scalar(calc[:], calc[:], side[:, 2:3], 0.0, ALU.subtract, ALU.max))
            link(dve.tensor_scalar(rows[:, :, 1], calc[:], float(COLD - 1), None, ALU.min))
            dve.tensor_scalar(rows[:, :, 2], is_hot[:], -1.0, 1.0, ALU.mult, ALU.add).then_inc(s_rows, 1)
            dve.wait_ge(s_look, 16 * NT)
            link(dve.tensor_copy(hot_at[:], look[:, :, 0]))
            dve.wait_ge(s_flag, 1)
            twice = dve.value_load(flag[0:1, 0:1], min_val=0, max_val=1)
            with dve.If(twice > 0):
                dve.wait_ge(s_all, 16)
                dve.memset(all_f[:], 1.0).then_inc(s_done, 1)
                dve.wait_ge(s_done, 6)
                dve.tensor_tensor_scan(order[:], all_f[:], all_f[:], 0.0, ALU.mult, ALU.add).then_inc(s_done, 1)
                dve.wait_ge(s_done, 7)
                dve.tensor_scalar(all_f[:], all_i[:], 0, float(VOCAB), ALU.is_lt, ALU.mult).then_inc(s_done, 1)
                dve.wait_ge(s_done, 8)
                dve.tensor_tensor(all_f[:], all_f[:], all_i[:], ALU.add).then_inc(s_done, 1)
                dve.wait_ge(s_done, 9)
                scratch = all_i[:].bitcast(F32)
                with dve.Fori(0, NT) as j:
                    dve.scalar_tensor_tensor(scratch, all_f[:], tokf[:, bass.ds(j, 1)], order[:], ALU.is_equal,
                                             ALU.mult).then_inc(s_done, 1)
                    dve.wait_ge(s_done, j * 3 + 10)
                    dve.tensor_reduce(best[:, 0:1], scratch, AX.X, ALU.max).then_inc(s_done, 1)
                    dve.wait_ge(s_done, j * 3 + 11)
                    dve.tensor_scalar(hot_at[:, bass.ds(j, 1)], best[:, 0:1], 1.0, 0.0, ALU.subtract,
                                      ALU.max).then_inc(s_done, 1)
                    dve.wait_ge(s_done, j * 3 + 12)
            dve.tensor_copy(cold[:], look[:, :, 1]).then_inc(s_index, 1)
            with dve.Fori(0, NT // NB) as i:
                for b in range(NB):
                    j = i * NB + b
                    dve.tensor_copy(take[:, b:b + 1], look[:, bass.ds(j, 1), 2]).then_inc(s_take, 1)
                    dve.wait_ge(s_proj, j + 1)
                    dve.wait_ge(s_hot[b], i * 16 + 16)
                    dve.wait_ge(s_take, j + 1)
                    dve.nop().then_inc(s_inputs, 1)
                    dve.copy_predicated(row[:, b, :], take[:, b:b + 1].broadcast_to([P, D]),
                                        projected[:, b % 2, :]).then_inc(s_token, 1)
                    dve.wait_ge(s_token, j + 1)
                    dve.bn_stats(stats[:, bass.ds(j, 1), :].rearrange("p a d -> p (a d)"), row[:, b, :]).then_inc(s_stat, 1)
            dve.memset(t.h[:, NT:, :], 0.0).then_inc(s_stat, 1)
            dve.memset(t.ln[:, NT:, :], 0.0).then_inc(s_stat, 1)
            dve.wait_ge(s_stat, NT + 2)
            moments(dve, s_stat, NT + 2, stats, t.ln[:, 0:NT, 0], ln_calc[:, 1, :], ln_calc[:, 0, :])
            dve.nop().then_inc(s_var, 1)
            dve.wait_ge(s_sqrt, 1)
            rsqrt(dve, s_stat, NT + 6, t.ln[:, 0:NT, 1], ln_calc[:, 1, :], ln_calc[:, 0, :])


HEADS, KV, HD = 32, 8, 16
GROUP = HEADS // KV
QKV = (HEADS + 2 * KV) * HD
KF = KV * HD
NG = 20
MASKED = -1e30
STEPS = 24


def attention_units():
    return ([(1, i, m, 1) for i in range(GROUP) for m in range(KV // 2)]
            + [(0, i, m, 2) for i in range(GROUP) for m in (0, 2)])


UNITS = attention_units()
FRONT = [("x", 0), ("q", 1), ("kv", 2), ("g0", 4), ("g1", 5), ("g2", 6), ("g3", 7), ("k", 8)]
TURNS = ([(s, (w, 0)) for w, s in FRONT] + [(s + 10, (w, 1)) for w, s in FRONT]
         + [(19, ("o", 1)), (20, ("w", 1)), (25, ("o", 0)), (26, ("w", 0))])
NF = len(FRONT) * 2
ON_ACT = {"x", "g0", "g1", "k", "o"}
ON_DVE = {"x", "q", "kv", "g2", "g3", "o", "w"}
PT_ON_ACT = [n for n in range(STEPS) if n % 5 in (1, 3)]


def attend(nc, t, wqkv, wo, rope):
    NB2 = BATCH // 2
    with ExitStack() as ctx:
        sb = lambda n, s, d: ctx.enter_context(nc.sbuf_tensor(n, s, d))
        pb = lambda n, s, d: ctx.enter_context(nc.psum_tensor(n, s, d))
        sem = lambda n: ctx.enter_context(nc.semaphore(n))
        raw = sb("w_raw", [P, 2, QKV], F32)
        wq_hi = sb("wq_hi", [P, KC, QKV], F32R)
        wq_lo = sb("wq_lo", [P, KC, QKV], F32R)
        wo_hi = sb("wo_hi", [P, KC, D], F32R)
        wo_lo = sb("wo_lo", [P, KC, D], F32R)
        rot = sb("rot", [P, 2, 4, HD], F32)
        hide = sb("hide", [P, P], BF16)
        eye = sb("eye", [P, P], BF16)
        xn = sb("xn", [P, D], F32)
        x_hi = sb("x_hi", [P, D], F32R)
        x_lo = sb("x_lo", [P, D], F32R)
        r1 = sb("r1", [P, NG * 32], F32)
        r2 = sb("r2", [P, NG * 32], F32)
        parts = sb("parts", [P, NG, 96], F32R)
        q_sb = sb("q_sb", [96, 2, 16, SEQ], F32R)
        k_sb = sb("k_sb", [96, 2, 4, 2, SEQ], F32R)
        v_sb = sb("v_sb", [P, 2, 2, KF], F32)
        nmax = sb("nmax", [P, 3, 4], F32)
        sums = sb("sums", [P, 2, HEADS], F32)
        inv = sb("inv", [P, 2, HEADS], F32)
        prob = sb("prob", [P, 2, 512], F32)
        probT = sb("probT", [P, 2, 512], F32)
        on = sb("on", [P, D], F32)
        o_hi = sb("o_hi", [P, D], F32R)
        o_lo = sb("o_lo", [P, D], F32R)

        score = pb("score", [P, 3, 512], F32)
        turned = pb("p_turned", [P, 2, 512], F32)
        mixed = pb("mixed", [P, 512], F32)
        work = pb("work", [P, 2, 512], F32)

        s_raw = [sem("s_raw0"), sem("s_raw1")]
        s_tab = sem("s_tab")
        s_split_hi = sem("s_split_hi")
        s_split = sem("s_split")
        s_eye = sem("s_eye")
        s_xn = sem("s_xn")
        s_work = sem("s_work")
        s_work_act = sem("s_work_act")
        s_work_dve = sem("s_work_dve")
        s_pool = sem("s_pool")
        s_score = sem("s_score")
        s_max = sem("s_max")
        s_prob = sem("s_prob")
        s_turned = sem("s_pturned")
        s_pt_act = sem("s_pt_act")
        s_pt_dve = sem("s_pt_dve")
        s_pv = sem("s_pv")
        s_inv = sem("s_inv")
        s_on = sem("s_on")
        block = ctx.enter_context(nc.Block())

        ident = t.cst[:, CI:CI + P]

        class At:

            def __init__(self, it, half):
                self.it, self.half = it, half

            def __call__(self, per_batch, k, before=0):
                if self.it is None:
                    return k
                return self.it * (2 * per_batch) + (before + self.half * per_batch + k)

        FIRST = At(None, 1)

        def taken(at, names, n):
            per = sum(w in names for _, (w, _) in TURNS)
            return at(per, sum(w in names for _, (w, _) in TURNS[:n + 1]), per)

        def index(name, u):
            return [w for _, w in TURNS].index((name, u))

        def count_copies(eng, at, n):
            if n in PT_ON_ACT:
                eng.wait_ge(s_pt_act, at(len(PT_ON_ACT), sum(m <= n for m in PT_ON_ACT)))
            else:
                eng.wait_ge(s_pt_dve, at(STEPS - len(PT_ON_ACT), sum(m <= n for m in range(STEPS) if m not in PT_ON_ACT)))

        @block.sync
        def _(sp):
            sp.dma_start(rot[:], rope).then_inc(s_tab, 16)
            for n in range(2 * KC):
                if n >= 2:
                    sp.wait_ge(s_split, n - 1)
                src = wqkv[:, n, :] if n < KC else wo[:, n - KC, :]
                sp.dma_start(raw[:, n % 2, 0:src.shape[1]], src).then_inc(s_raw[n % 2], 16)

        @block.gpsimd
        def _(pool):
            def halves(at, u):
                for w, (g0, g1) in enumerate(((0, 16), (16, NG))):
                    pool.wait_ge(s_work_dve, taken(at, ON_DVE, index(("q", "kv")[w], u)))
                    if w == 0 and not (at.it is None and u == 0):
                        prev = (at, index("k", 0)) if u else (At(at.it, at.half - 1), index("k", 1))
                        pool.wait_ge(s_work, prev[0](len(TURNS), prev[1] + 1, len(TURNS)))
                    base = 4 * (2 * u + w)
                    a = r1[:, g0 * 32:g1 * 32].rearrange("p (g c) -> p g c", c=32)
                    b = r2[:, g0 * 32:g1 * 32].rearrange("p (g c) -> p g c", c=32)
                    hi, lo, other = (0, 32, 64) if w == 0 else (0, 64, 32)
                    pool.tensor_tensor(parts[:, g0:g1, hi:hi + 32], a, b, ALU.add).then_inc(s_pool, 1)
                    pool.tensor_tensor(parts[:, g0:g1, other:other + 32], a, b, ALU.add).then_inc(s_pool, 1)
                    pool.tensor_tensor(a, a, b, ALU.add).then_inc(s_pool, 1)
                    pool.wait_ge(s_pool, at(16, base + 3, 16))
                    pool.tensor_tensor(parts[:, g0:g1, lo:lo + 32], a, parts[:, g0:g1, hi:hi + 32].bitcast(F32),
                                       ALU.subtract).then_inc(s_pool, 1)

            for u in range(2):
                halves(FIRST, u)
            with pool.Fori(0, NB2) as it:
                for half in range(2):
                    for u in range(2):
                        halves(At(it, half), u)

        @block.tensor
        def _(pe):
            def three(out, hi, lo, w_hi, w_lo):
                for c in range(KC):
                    cut = slice(c * P, (c + 1) * P)
                    pe.matmul(out, hi[:, cut], w_hi(c), start=(c == 0), stop=False)
                    pe.matmul(out, hi[:, cut], w_lo(c), start=False, stop=False)
                    last = pe.matmul(out, lo[:, cut], w_hi(c), start=False, stop=(c == KC - 1))
                return last

            def turn(at, n):
                name, u = TURNS[n][1]
                bank = work[:, n % 2, :]
                if not (at.it is None and n < 2):
                    prev, m = (at, n - 2) if n >= 2 else (At(at.it, at.half - 1), n - 2 + len(TURNS))
                    pe.wait_ge(s_work_act, taken(prev, ON_ACT, m))
                    pe.wait_ge(s_work_dve, taken(prev, ON_DVE, m))
                if name == "x":
                    pe.wait_ge(s_xn, at(2, u + 1, 2))
                    for c in range(KC):
                        last = pe.transpose(bank[:, c * P:(c + 1) * P], xn[:, c * P:(c + 1) * P], ident)
                elif name in ("q", "kv"):
                    if name == "q":
                        pe.wait_ge(s_work_act, taken(at, ON_ACT, index("x", u)))
                        pe.wait_ge(s_work_dve, taken(at, ON_DVE, index("x", u)))
                    a, b = (0, 512) if name == "q" else (512, QKV)
                    last = three(bank[:, 0:b - a], x_hi, x_lo, lambda c: wq_hi[:, c, a:b], lambda c: wq_lo[:, c, a:b])
                elif name in ("g0", "g1", "g2", "g3", "k"):
                    g = 4 * int(name[1]) if name != "k" else 16
                    pe.wait_ge(s_pool, at(16, 8 * u + (8 if name == "k" else 4), 16))
                    for m in range(4):
                        last = pe.transpose(bank[0:96, m * P:(m + 1) * P], parts[:, g + m, :].bitcast(F32), ident)
                elif name == "o":
                    pe.wait_ge(s_on, at(2, 1 if u else 2))
                    for c in range(KC):
                        last = pe.transpose(bank[:, c * P:(c + 1) * P], on[:, c * P:(c + 1) * P], ident)
                else:
                    pe.wait_ge(s_work_act, taken(at, ON_ACT, index("o", u)))
                    pe.wait_ge(s_work_dve, taken(at, ON_DVE, index("o", u)))
                    last = three(bank, o_hi, o_lo, lambda c: wo_hi[:, c, :], lambda c: wo_lo[:, c, :])
                last.then_inc(s_work, 1)

            def scores(at, n):
                qt, i, m0, pairs = UNITS[n]
                keys = (qt + 1) * P
                if n == 0:
                    last = At(at.it, at.half - 1)
                    pe.wait_ge(s_work_act, taken(last, ON_ACT, len(TURNS) - 1))
                    pe.wait_ge(s_work_dve, taken(last, ON_DVE, len(TURNS) - 1))
                if n >= 3:
                    pe.wait_ge(s_prob, at(STEPS, n - 2))
                out = score[:, n % 3, :]
                for m in range(pairs):
                    w = 2 * keys
                    pe.matmul(out[:, m * w:(m + 1) * w], q_sb[:, at.half, 4 * i + m0 + m, qt * P:(qt + 1) * P],
                              k_sb[:, at.half, m0 + m, :, 0:keys], start=(m == 0), stop=False, skip_group_check=True)
                g = 2 * pairs
                last = pe.matmul(out.rearrange("p (g k) -> p g k", g=g)[:, :, keys - P:keys], eye[:],
                                 hide[:].rearrange("p (a k) -> p a k", a=1).broadcast_to([P, g, P]),
                                 start=False, stop=True, skip_group_check=True)
                last.then_inc(s_score, 1)

            def turn_probs(at, n):
                pe.wait_ge(s_prob, at(STEPS, n + 1))
                if n >= 2:
                    count_copies(pe, at, n - 2)
                for m in range(4):
                    last = pe.transpose(turned[:, n % 2, m * P:(m + 1) * P], prob[:, n % 2, m * P:(m + 1) * P], ident)
                last.then_inc(s_turned, 1)

            def mix(at, n):
                qt, i, m0, pairs = UNITS[n]
                count_copies(pe, at, n)
                if n == 0:
                    pe.wait_ge(s_on, at(2, 0))
                if n == 16:
                    pe.wait_ge(s_on, at(2, 1))
                blocks = [(g, kt) for g in range(2 * pairs) for kt in range(qt + 1)]
                for m, (g, kt) in enumerate(blocks):
                    kv = 2 * m0 + g
                    head = GROUP * kv + i
                    last = pe.matmul(mixed[:, head * HD:(head + 1) * HD], probT[:, n % 2, m * P:(m + 1) * P],
                                     v_sb[:, at.half, kt, kv * HD:(kv + 1) * HD], start=(kt == 0), stop=(kt == qt))
                last.then_inc(s_pv, 1)

            pe.wait_ge(s_split, 2 * KC)
            pe.wait_ge(s_eye, 1)
            for n in range(NF):
                turn(FIRST, n)
            pe.wait_ge(s_work, NF)
            for _ in TURNS[NF:]:
                pe.nop().then_inc(s_work, 1)
            with pe.Fori(0, NB2) as it:
                for half in range(2):
                    at = At(it, half)
                    scores(at, 0)
                    scores(at, 1)
                    for n in range(STEPS + 3):
                        if n + 2 < STEPS:
                            scores(at, n + 2)
                        if n < STEPS:
                            turn_probs(at, n)
                        if 1 <= n <= STEPS:
                            mix(at, n - 1)
                        for k, (s, _) in enumerate(TURNS):
                            if s == n:
                                turn(at, k)

        @block.scalar
        def _(act):
            def turn(at, n):
                name, u = TURNS[n][1]
                if name not in ON_ACT:
                    return
                bank = work[:, n % 2, :]
                half = 1 - at.half
                act.wait_ge(s_work, at(len(TURNS), n + 1, len(TURNS)))
                if name == "x":
                    last = act.copy(x_hi[:], bank)
                elif name == "k":
                    for g in range(2):
                        last = act.activation(k_sb[:, half, :, g, u * P:(u + 1) * P],
                                              bank[0:96, :].rearrange("p (m k) -> p m k", m=4), ACT.Copy,
                                              scale=t.cst[0:96, CP + 3 + g:CP + 4 + g])
                elif name == "o":
                    last = act.copy(o_hi[:], bank)
                else:
                    g = 4 * int(name[1])
                    last = act.copy(q_sb[:, half, g:g + 4, u * P:(u + 1) * P],
                                    bank[0:96, :].rearrange("p (m k) -> p m k", m=4))
                last.then_inc(s_work_act, 1)

            def exps(at, n):
                qt, i, m0, pairs = UNITS[n]
                keys = (qt + 1) * P
                act.wait_ge(s_max, at(STEPS, n + 1))
                if n >= 2:
                    act.wait_ge(s_turned, at(STEPS, n - 1))
                if n == 0:
                    act.wait_ge(s_inv, at(2, 0))
                for g in range(2 * pairs):
                    head = GROUP * (2 * m0 + g) + i
                    last = act.activation(prob[:, n % 2, g * keys:(g + 1) * keys],
                                          score[:, n % 3, g * keys:(g + 1) * keys], ACT.Exp,
                                          bias=nmax[:, n % 3, g:g + 1], accum_out=sums[:, qt, head:head + 1])
                last.then_inc(s_prob, 1)

            for n in range(2 * KC):
                act.wait_ge(s_raw[n % 2], 16 * (n // 2 + 1))
                w = QKV if n < KC else D
                hi = wq_hi[:, n, :] if n < KC else wo_hi[:, n - KC, :]
                act.copy(hi, raw[:, n % 2, 0:w]).then_inc(s_split_hi, 1)
            for n in range(NF):
                turn(FIRST, n)
            act.wait_ge(s_work_act, sum(w in ON_ACT for _, (w, _) in TURNS[:NF]))
            for _ in range(sum(w in ON_ACT for _, (w, _) in TURNS[NF:])):
                act.nop().then_inc(s_work_act, 1)
            with act.Fori(0, NB2) as it:
                for half in range(2):
                    at = At(it, half)
                    exps(at, 0)
                    for n in range(STEPS + 3):
                        if n + 1 < STEPS:
                            exps(at, n + 1)
                        if n in PT_ON_ACT:
                            act.wait_ge(s_turned, at(STEPS, n + 1))
                            if n >= 2:
                                act.wait_ge(s_pv, at(STEPS, n - 1))
                            act.copy(probT[:, n % 2, :], turned[:, n % 2, :]).then_inc(s_pt_act, 1)
                        for k, (s, _) in enumerate(TURNS):
                            if s == n:
                                turn(at, k)

        @block.vector
        def _(dve):
            def norm(at, u, tile):
                if not (at.it is None and u == 0):
                    prev = (at, index("x", 0)) if u else (At(at.it, at.half - 1), index("x", 1))
                    dve.wait_ge(s_work, prev[0](len(TURNS), prev[1] + 1, len(TURNS)))
                h = t.h[:, tile, :] if at.it is None else t.h[:, bass.ds(tile, 1), :].rearrange("p a d -> p (a d)")
                ln = lambda k: t.ln[:, tile, k:k + 1] if at.it is None else t.ln[:, bass.ds(tile, 1), k]
                dve.tensor_scalar(xn[:], h, ln(0), ln(1), ALU.subtract, ALU.mult).then_inc(s_xn, 1)

            def rotate(bank, u, heads, at0, kind):
                x = bank[:, 0:heads * HD].rearrange("p (h c) -> p h c", c=HD)
                r1v = r1[:, at0:at0 + heads * HD].rearrange("p (h c) -> p h c", c=HD)
                r2v = r2[:, at0:at0 + heads * HD].rearrange("p (h c) -> p h c", c=HD)
                H2 = HD // 2
                tab = lambda k, a, b: rot[:, u, k, a:b].rearrange("p (o c) -> p o c", o=1).broadcast_to([P, heads, b - a])
                dve.tensor_tensor(r1v, x, tab(2 * kind, 0, HD), ALU.mult)
                dve.tensor_tensor(r2v[:, :, 0:H2], x[:, :, H2:HD], tab(2 * kind + 1, 0, H2), ALU.mult)
                return dve.tensor_tensor(r2v[:, :, H2:HD], x[:, :, 0:H2], tab(2 * kind + 1, H2, HD), ALU.mult)

            def turn(at, n):
                name, u = TURNS[n][1]
                if name not in ON_DVE:
                    return
                bank = work[:, n % 2, :]
                half = 1 - at.half
                if name == "x":
                    dve.wait_ge(s_work_act, taken(at, ON_ACT, n))
                    last = dve.tensor_tensor(x_lo[:], bank, x_hi[:].bitcast(F32), ALU.subtract)
                elif name in ("q", "kv"):
                    dve.wait_ge(s_work, at(len(TURNS), n + 1, len(TURNS)))
                    k = 2 * u + (name == "kv")
                    if not (at.it is None and u == 0):
                        prev = At(at.it, at.half - 1) if u == 0 else at
                        dve.wait_ge(s_pool, prev(16, 4 * ((k - 2) % 4 + 1), 16))
                    heads, at0 = (HEADS, 0) if name == "q" else (KV, 512)
                    if name == "kv":
                        dve.tensor_copy(v_sb[:, half, u, :], bank[:, KF:2 * KF])
                    last = rotate(bank, u, heads, at0, int(name == "kv"))
                elif name == "o":
                    dve.wait_ge(s_work_act, taken(at, ON_ACT, n))
                    last = dve.tensor_tensor(o_lo[:], bank, o_hi[:].bitcast(F32), ALU.subtract)
                elif name == "w":
                    dve.wait_ge(s_work, at(len(TURNS), n + 1, len(TURNS)))
                    tile = at.it * 4 + (2 * at.half + u)
                    h = t.h[:, bass.ds(tile, 1), :].rearrange("p a d -> p (a d)")
                    last = dve.tensor_tensor(h, h, bank, ALU.add)
                else:
                    dve.wait_ge(s_work, at(len(TURNS), n + 1, len(TURNS)))
                    g = 4 * int(name[1])
                    last = dve.tensor_copy(q_sb[:, half, g:g + 4, u * P:(u + 1) * P],
                                           bank[0:96, :].rearrange("p (m k) -> p m k", m=4))
                last.then_inc(s_work_dve, 1)

            def maxima(at, n):
                qt, i, m0, pairs = UNITS[n]
                dve.wait_ge(s_score, at(STEPS, n + 1))
                g = 2 * pairs
                dve.tensor_reduce(nmax[:, n % 3, 0:g], score[:, n % 3, :].rearrange("p (g k) -> p g k", g=g), AX.X,
                                  ALU.max, negate=True).then_inc(s_max, 1)

            def normalise(at, qt):
                last_unit = 15 if qt else 23
                dve.wait_ge(s_prob, at(STEPS, last_unit + 1))
                dve.reciprocal(inv[:, qt, :], sums[:, qt, :]).then_inc(s_inv, 1)
                dve.wait_ge(s_inv, at(2, 1 if qt else 2))
                dve.wait_ge(s_pv, at(STEPS, last_unit + 1))
                prev = At(at.it, at.half - 1) if qt else at
                dve.wait_ge(s_work, prev(len(TURNS), index("o", 0 if qt else 1) + 1, len(TURNS)))
                dve.tensor_tensor(on[:].rearrange("p (h c) -> p h c", c=HD), mixed[:].rearrange("p (h c) -> p h c", c=HD),
                                  inv[:, qt, :].rearrange("p (h o) -> p h o", o=1).broadcast_to([P, HEADS, HD]),
                                  ALU.mult).then_inc(s_on, 1)

            dve.wait_ge(s_tab, 16)
            dve.tensor_copy(eye[:], ident)
            dve.tensor_scalar(hide[:], t.cst[:, CT:CT + P], MASKED, None, ALU.mult).then_inc(s_eye, 1)
            for n in range(2 * KC):
                w = QKV if n < KC else D
                hi, lo = (wq_hi[:, n, :], wq_lo[:, n, :]) if n < KC else (wo_hi[:, n - KC, :], wo_lo[:, n - KC, :])
                dve.wait_ge(s_split_hi, n + 1)
                dve.tensor_tensor(lo, raw[:, n % 2, 0:w], hi.bitcast(F32), ALU.subtract).then_inc(s_split, 1)
            norm(FIRST, 0, 0)
            for n in range(NF):
                if TURNS[n][1] == ("x", 1):
                    norm(FIRST, 1, 1)
                turn(FIRST, n)
            dve.wait_ge(s_work_dve, sum(w in ON_DVE for _, (w, _) in TURNS[:NF]))
            for _ in range(sum(w in ON_DVE for _, (w, _) in TURNS[NF:])):
                dve.nop().then_inc(s_work_dve, 1)
            with dve.Fori(0, NB2) as it:
                for half in range(2):
                    at = At(it, half)
                    tile = it * 4 + 2 * (half + 1)
                    norm(at, 0, tile)
                    maxima(at, 0)
                    maxima(at, 1)
                    for n in range(STEPS + 3):
                        if n < STEPS and n not in PT_ON_ACT:
                            dve.wait_ge(s_turned, at(STEPS, n + 1))
                            if n >= 2:
                                dve.wait_ge(s_pv, at(STEPS, n - 1))
                            dve.tensor_copy(probT[:, n % 2, :], turned[:, n % 2, :]).then_inc(s_pt_dve, 1)
                        if n + 2 < STEPS:
                            maxima(at, n + 2)
                        if n == 9:
                            norm(at, 1, tile + 1)
                        if n == 17:
                            normalise(at, 1)
                        if n == 24:
                            normalise(at, 0)
                        for k, (s, _) in enumerate(TURNS):
                            if s == n:
                                turn(at, k)


def rope_table():
    inv = (1.0 / np.power(np.float32(10000.0), np.arange(0, HD, 2, dtype=np.float32) / np.float32(HD))).astype(np.float32)
    angle = (np.arange(SEQ, dtype=np.float32)[:, None] * inv[None, :]).astype(np.float32)
    cos, sin = np.cos(angle.astype(np.float64)), np.sin(angle.astype(np.float64))
    both = np.stack([np.concatenate([cos, cos], 1), np.concatenate([-sin, sin], 1)], 1).astype(np.float32)
    full = np.concatenate([both * np.float32(HD ** -0.5), both], 1)
    return np.ascontiguousarray(full.reshape(2, P, 4, HD).transpose(1, 0, 2, 3))


def head_order():
    half = np.concatenate([np.arange(0, HD, 2), np.arange(1, HD, 2)])
    q = [(GROUP * g + i) * HD + half for i in range(GROUP) for g in range(KV)]
    k = [g * HD + half for g in range(KV)]
    return np.concatenate(q), np.concatenate(k)


EXPERTS, TOPK, KEEP = 32, 8, 0.8
INTER = 192
XROW = D + EXPERTS
TILES = TOK * TOPK // P + EXPERTS
SLOTS = TILES + 4
NOWHERE = 32768.0


def route(nc, t, gate, xrows, out):
    with ExitStack() as ctx:
        sb = lambda n, s, d: ctx.enter_context(nc.sbuf_tensor(n, s, d))
        pb = lambda n, s, d: ctx.enter_context(nc.psum_tensor(n, s, d))
        sem = lambda n: ctx.enter_context(nc.semaphore(n))
        gate_sb = sb("gate_sb", [P, KC, EXPERTS], F32)
        stats = sb("r_stats", [P, NT, 6], F32)
        mean = sb("r_mean", [P, NT], F32)
        var = sb("r_var", [P, NT], F32)
        rstd = sb("r_rstd", [P, NT], F32)
        root = sb("r_root", [P, NT], F32)
        xn = sb("r_xn", [P, 2, D], F32)
        xT = sb("r_xT", [P, 2, D], F32)
        logit = sb("logit", [P, NT, EXPERTS], F32)
        prob = sb("r_prob", [P, NT, EXPERTS], F32)
        comb = sb("comb", [P, NT, EXPERTS], F32)
        col = sb("r_col", [P, 4, NT], F32)
        top = sb("top", [P, NT, TOPK], F32)
        top_at = sb("top_at", [P, NT, TOPK], mybir.dt.uint32)
        share = sb("share", [P, NT, TOPK], F32)
        active = sb("active", [P, NT, TOPK], F32)
        at_f = sb("at_f", [P, NT, TOPK], F32)
        picked = sb("picked", [P, NT, TOPK, EXPERTS], F32)
        product = sb("product", [P, NT, TOPK, EXPERTS], F32)
        member = sb("member", [P, NT, EXPERTS], F32)
        member_b = sb("member_b", [P, NT, EXPERTS], BF16)
        tri = sb("tri", [P, P], BF16)
        ones = sb("r_ones", [P, P], BF16)
        ones_f = sb("r_ones_f", [P, NT * EXPERTS], F32)
        tile_count = sb("tile_count", [P, EXPERTS, NT], F32)
        upto = sb("upto", [P, EXPERTS, NT], F32)
        e_col = sb("e_col", [P, 6, EXPERTS], F32)
        e_int = sb("e_int", [P, EXPERTS], I32)
        place = sb("place", [P, NT, EXPERTS], F32)
        slot = sb("slot", [P, NT * TOPK], F32)
        slot_i = sb("slot_i", [P, 3, NT * TOPK], I32)
        slot_f = sb("slot_f", [P, 2, NT * TOPK], F32)
        token = sb("r_token", [P, NT, TOPK], F32)
        counting = sb("counting", [P, 256], F32)
        row_hot = sb("r_row_hot", [P, 4, P], F32R)
        col_hot = sb("r_col_hot", [P, 4, SLOTS], F32R)
        zero = sb("r_zero", [P, SLOTS], F32R)
        zero_f = sb("r_zero_f", [P, SLOTS], F32)
        held = sb("held", [P, SLOTS], F32)
        empty = sb("empty", [P, SLOTS], F32)
        n_int = sb("n_int", [EXPERTS, 2], I32)
        n_f = sb("n_f", [EXPERTS, 4], F32)
        past = sb("past", [EXPERTS, SLOTS], F32)

        turned = pb("r_turned", [P, 2, 512], F32)
        logit_p = pb("logit_p", [P, 512], F32)
        before_p = pb("before_p", [P, 512], F32)
        total_p = pb("total_p", [P, 512], F32)
        tiny = pb("tiny", [P, 512], F32)
        slot_p = pb("slot_p", [P, 512], F32)

        s_gate = sem("s_gate")
        s_out = sem("s_out")
        s_v = sem("r_v")
        s_var = sem("r_var")
        s_root = sem("r_root")
        s_xn = sem("r_s_xn")
        s_turned = sem("r_turned")
        s_xT = sem("r_xT")
        s_logit = sem("r_logit")
        s_rows = [sem("r_rows0"), sem("r_rows1")]
        s_shift = sem("r_shift")
        s_exp = sem("r_exp")
        s_comb = sem("r_comb")
        s_comb_out = sem("r_comb_out")
        s_member = sem("r_member")
        s_before = sem("r_before")
        s_tiles = sem("r_tiles")
        s_bound = sem("r_bound")
        s_past = sem("r_past")
        s_hot = sem("r_hot")
        s_used = sem("r_used")
        s_slots = sem("r_slots")
        s_ids = sem("r_ids")
        s_pool = sem("r_pool")
        block = ctx.enter_context(nc.Block())
        ident = t.cst[:, CI:CI + P]
        flat = lambda a: a.rearrange("p a b -> p (a b)")
        over = lambda a, n: a.rearrange("p (a o) -> p a o", o=1).broadcast_to([P, a.shape[1], n])

        @block.sync
        def _(sp):
            sp.dma_start(gate_sb[:], gate).then_inc(s_gate, 16)
            sp.dma_start(out.rearrange("(j p) d -> p j d", p=P), t.h[:, 0:NT + 1, :]).then_inc(s_out, 16)
            rows = xrows.rearrange("(j p) d -> j p d", p=P)
            with sp.Fori(0, NT // 2) as i:
                for b in range(2):
                    sp.wait_ge(s_xn, i * 2 + (b + 1))
                    sp.dma_start(rows[bass.ds(i * 2 + b, 1), :, 0:D].rearrange("a p d -> p (a d)"),
                                 xn[:, b, :]).then_inc(s_rows[b], 16)
            sp.wait_ge(s_comb, 1)
            sp.dma_start(xrows.rearrange("(j p) d -> p j d", p=P)[:, :, D:XROW], comb[:]).then_inc(s_comb_out, 16)
            sp.wait_ge(s_out, 16)
            for b in range(2):
                sp.wait_ge(s_rows[b], 16 * (NT // 2))
            sp.wait_ge(s_comb_out, 16)

        @block.gpsimd
        def _(pool):
            pool.iota(counting[:], pattern=[[1, 256]], base=0, channel_multiplier=0,
                      allow_small_or_imprecise_dtypes=True).then_inc(s_pool, 1)
            pool.iota(token[:], pattern=[[P, NT], [0, TOPK]], base=1, channel_multiplier=1,
                      allow_small_or_imprecise_dtypes=True).then_inc(s_pool, 1)

        @block.tensor
        def _(pe):
            pe.wait_ge(s_gate, 16)
            with pe.Fori(0, NT // 2) as i:
                for b in range(2):
                    pe.wait_ge(s_xn, i * 2 + (b + 1))
                    for c in range(KC):
                        last = pe.transpose(turned[:, b, c * P:(c + 1) * P], xn[:, b, c * P:(c + 1) * P], ident)
                    last.then_inc(s_turned, 1)
                    pe.wait_ge(s_xT, i * 2 + (b + 1))
                    for c in range(KC):
                        last = pe.matmul(logit_p[:, bass.ds(i * (2 * EXPERTS) + b * EXPERTS, EXPERTS)],
                                         xT[:, b, c * P:(c + 1) * P], gate_sb[:, c, :], start=(c == 0), stop=(c == KC - 1))
                    last.then_inc(s_logit, 1)
            pe.wait_ge(s_member, 1)
            pe.matmul(before_p[:], tri[:], flat(member_b[:]), start=True, stop=True)
            pe.matmul(total_p[:], ones[:], flat(member_b[:]), start=True, stop=True)
            for j in range(NT):
                last = pe.matmul(tiny[0:EXPERTS, 0:1], member_b[:, j, :], ones[:, 0:1], start=(j == 0), stop=(j == NT - 1))
            last.then_inc(s_before, 1)
            pe.wait_ge(s_tiles, 1)
            pe.matmul(tiny[0:EXPERTS, 8:9], t.cst[0:EXPERTS, CT:CT + EXPERTS], n_f[:, 1:2], start=True, stop=True)
            pe.matmul(tiny[0:1, 16:16 + EXPERTS], n_f[:, 1:2], t.cst[0:EXPERTS, CI:CI + EXPERTS], start=True,
                      stop=True).then_inc(s_bound, 1)
            pe.wait_ge(s_past, 1)
            pe.matmul(tiny[0:1, 64:64 + SLOTS], ones_f[0:EXPERTS, 0:1], past[:], start=True, stop=True).then_inc(s_bound, 1)
            pe.matmul(slot_p[:, 0:SLOTS], zero[:, 0:P], zero[:], start=True, stop=False)
            with pe.Fori(0, NT * TOPK // 4) as i:
                for b in range(4):
                    pe.wait_ge(s_hot, i * 4 + (b + 1))
                    pe.matmul(slot_p[:, 0:SLOTS], row_hot[:, b, :], col_hot[:, b, :], start=False,
                              stop=False).then_inc(s_used, 1)
            pe.matmul(slot_p[:, 0:SLOTS], zero[:, 0:P], zero[:], start=False, stop=True).then_inc(s_slots, 1)

        @block.scalar
        def _(act):
            act.wait_ge(s_var, 1)
            act.activation(root[:], var[:], ACT.Sqrt).then_inc(s_root, 1)
            with act.Fori(0, NT // 2) as i:
                for b in range(2):
                    act.wait_ge(s_turned, i * 2 + (b + 1))
                    act.copy(xT[:, b, :], turned[:, b, :]).then_inc(s_xT, 1)
            act.wait_ge(s_shift, 1)
            act.activation(flat(prob[:]), flat(logit[:]), ACT.Exp).then_inc(s_exp, 1)

        @block.vector
        def _(dve):
            with dve.Fori(0, NT) as j:
                dve.bn_stats(stats[:, bass.ds(j, 1), :].rearrange("p a d -> p (a d)"),
                             t.h[:, bass.ds(j, 1), :].rearrange("p a d -> p (a d)")).then_inc(s_v, 1)
            dve.wait_ge(s_v, NT)
            moments(dve, s_v, NT, stats, mean[:], var[:], root[:])
            dve.nop().then_inc(s_var, 1)
            dve.wait_ge(s_root, 1)
            rsqrt(dve, s_v, NT + 4, rstd[:], var[:], root[:])
            with dve.Fori(0, NT // 2) as i:
                for b in range(2):
                    j = i * 2 + b
                    dve.wait_ge(s_turned, i * 2)
                    dve.wait_ge(s_rows[b], i * 16)
                    dve.tensor_scalar(xn[:, b, :], t.h[:, bass.ds(j, 1), :].rearrange("p a d -> p (a d)"),
                                      mean[:, bass.ds(j, 1)], rstd[:, bass.ds(j, 1)], ALU.subtract,
                                      ALU.mult).then_inc(s_xn, 1)
            count = [NT + 9]

            def link(ins):
                count[0] += 1
                ins.then_inc(s_v, 1)
                dve.wait_ge(s_v, count[0])

            dve.tensor_copy(tri[:], t.cst[:, CT:CT + P])
            dve.memset(ones[:], 1.0)
            dve.memset(ones_f[:], 1.0)
            link(dve.memset(zero_f[:], 0.0))
            link(dve.tensor_copy(zero[:], zero_f[:]))
            dve.wait_ge(s_logit, NT)
            link(dve.tensor_copy(flat(logit[:]), logit_p[:]))
            link(dve.tensor_reduce(col[:, 0, :], logit[:], AX.X, ALU.max))
            dve.tensor_tensor(logit[:], logit[:], over(col[:, 0, :], EXPERTS), ALU.subtract).then_inc(s_shift, 1)
            dve.wait_ge(s_exp, 1)
            link(dve.tensor_reduce(col[:, 1, :], prob[:], AX.X, ALU.add))
            link(dve.reciprocal(col[:, 1, :], col[:, 1, :]))
            link(dve.tensor_tensor(prob[:], prob[:], over(col[:, 1, :], EXPERTS), ALU.mult))
            for j in range(NT):
                last = dve.max(top[:, j, :], prob[:, j, :])
            link(last)
            for j in range(NT):
                last = dve.max_index(top_at[:, j, :], top[:, j, :], prob[:, j, :])
            link(last)
            link(dve.tensor_reduce(col[:, 2, :], top[:], AX.X, ALU.add))
            link(dve.tensor_scalar(col[:, 2, :], col[:, 2, :], 1e-12, None, ALU.max))
            link(dve.reciprocal(col[:, 2, :], col[:, 2, :]))
            link(dve.tensor_tensor(share[:], top[:], over(col[:, 2, :], TOPK), ALU.mult))
            for k in range(1, TOPK):
                link(dve.tensor_tensor(share[:, :, k], share[:, :, k], share[:, :, k - 1], ALU.add))
            dve.memset(active[:, :, 0], 1.0)
            link(dve.tensor_scalar(active[:, :, 1:TOPK], share[:, :, 0:TOPK - 1], KEEP, None, ALU.is_lt))
            link(dve.tensor_tensor(top[:], top[:], active[:], ALU.mult))
            link(dve.tensor_reduce(col[:, 3, :], top[:], AX.X, ALU.add))
            link(dve.tensor_scalar(col[:, 3, :], col[:, 3, :], 1e-12, None, ALU.max))
            link(dve.reciprocal(col[:, 3, :], col[:, 3, :]))
            dve.tensor_copy(at_f[:], top_at[:])
            link(dve.tensor_scalar(active[:], active[:], -NOWHERE, NOWHERE, ALU.mult, ALU.add))
            link(dve.tensor_tensor(at_f[:], at_f[:], active[:], ALU.add))
            dve.wait_ge(s_pool, 2)
            link(dve.tensor_tensor(picked[:].rearrange("p j k e -> p (j k) e"),
                                   counting[:, 0:EXPERTS].rearrange("p (o e) -> p o e", o=1).broadcast_to([P, NT * TOPK, EXPERTS]),
                                   over(flat(at_f[:]), EXPERTS), ALU.is_equal))
            link(dve.tensor_reduce(member[:], picked[:].rearrange("p j k e -> p j e k"), AX.X, ALU.add))
            dve.tensor_copy(member_b[:], member[:]).then_inc(s_member, 1)
            link(dve.tensor_tensor(comb[:], prob[:], member[:], ALU.mult))
            dve.tensor_tensor(comb[:], comb[:], over(col[:, 3, :], EXPERTS), ALU.mult).then_inc(s_comb, 1)
            dve.wait_ge(s_before, 1)
            link(dve.tensor_scalar(n_int[:, 0:1], tiny[0:EXPERTS, 0:1], float(P - 1), None, ALU.add))
            link(dve.tensor_scalar(n_int[:, 1:2], n_int[:, 0:1], 7, None, ALU.arith_shift_right))
            dve.tensor_copy(n_f[:, 1:2], n_int[:, 1:2]).then_inc(s_tiles, 1)
            link(dve.tensor_copy(tile_count[:], total_p[:].rearrange("p (j e) -> p e j", e=EXPERTS)))
            link(dve.tensor_tensor_scan(flat(upto[:]), ones_f[:], flat(tile_count[:]), 0.0, ALU.mult, ALU.add))
            dve.memset(e_col[:, 0, 0:1], 0.0)
            link(dve.tensor_copy(e_col[:, 0, 1:EXPERTS], upto[:, 0:EXPERTS - 1, NT - 1]))
            link(dve.tensor_tensor(e_col[:, 1, :], upto[:, :, NT - 1], e_col[:, 0, :], ALU.subtract))
            link(dve.tensor_scalar(e_int[:], e_col[:, 1, :], float(P - 1), None, ALU.add))
            link(dve.tensor_scalar(e_int[:], e_int[:], 7, None, ALU.arith_shift_right))
            link(dve.tensor_copy(e_col[:, 2, :], e_int[:]))
            link(dve.tensor_tensor_scan(e_col[:, 3, :], ones_f[:, 0:EXPERTS], e_col[:, 2, :], 0.0, ALU.mult, ALU.add))
            dve.tensor_copy(t.bound[:, 4:4 + EXPERTS], e_col[0:1, 3, :])
            dve.memset(t.bound[:, 0:4], 0)
            link(dve.tensor_tensor(e_col[:, 4, :], e_col[:, 3, :], e_col[:, 2, :], ALU.subtract))
            link(dve.scalar_tensor_tensor(e_col[:, 4, :], e_col[:, 4, :], float(P), e_col[:, 0, :], ALU.mult, ALU.subtract))
            dve.wait_ge(s_bound, 1)
            link(dve.tensor_tensor(n_f[:, 2:3], tiny[0:EXPERTS, 8:9], n_f[:, 1:2], ALU.add))
            dve.tensor_scalar(past[:], counting[0:EXPERTS, 0:SLOTS], n_f[:, 2:3], None, ALU.is_ge).then_inc(s_past, 1)
            link(dve.tensor_tensor(upto[:], upto[:], tile_count[:], ALU.subtract))
            link(dve.tensor_tensor(upto[:], upto[:], over(e_col[:, 4, :], NT), ALU.add))
            link(dve.tensor_tensor(place[:], upto[:].rearrange("p e j -> p j e"),
                                   before_p[:].rearrange("p (j e) -> p j e", e=EXPERTS), ALU.add))
            link(dve.tensor_tensor(product[:], picked[:], place[:].rearrange("p j (o e) -> p j o e", o=1).broadcast_to(
                [P, NT, TOPK, EXPERTS]), ALU.mult))
            link(dve.tensor_reduce(slot[:].rearrange("p (j k) -> p j k", k=TOPK), product[:], AX.X, ALU.add))
            link(dve.tensor_tensor(slot_i[:, 0, :], slot[:], flat(active[:]), ALU.add))
            dve.tensor_scalar(slot_i[:, 1, :], slot_i[:, 0, :], P - 1, None, ALU.bitwise_and)
            link(dve.tensor_scalar(slot_i[:, 2, :], slot_i[:, 0, :], 7, None, ALU.arith_shift_right))
            link(dve.tensor_copy(slot_f[:], slot_i[:, 1:3, :]))
            dve.wait_ge(s_bound, 2)
            link(dve.tensor_scalar(t.tile_expert[:], tiny[0:1, 64:64 + SLOTS], float(EXPERTS - 1), None, ALU.min))
            tokens = flat(token[:])
            with dve.Fori(0, NT * TOPK // 4) as i:
                for b in range(4):
                    n = i * 4 + b
                    if b == 0:
                        dve.wait_ge(s_used, i * 4)
                    dve.tensor_scalar(row_hot[:, b, :], counting[:, 0:P], slot_f[:, 0, bass.ds(n, 1)], None, ALU.is_equal)
                    dve.tensor_scalar(col_hot[:, b, :], counting[:, 0:SLOTS], slot_f[:, 1, bass.ds(n, 1)],
                                      tokens[:, bass.ds(n, 1)], ALU.is_equal, ALU.mult).then_inc(s_hot, 1)
            dve.wait_ge(s_slots, 1)
            link(dve.tensor_copy(held[:], slot_p[:, 0:SLOTS]))
            dve.tensor_scalar(t.gather[:], held[:], 1.0, 0.0, ALU.subtract, ALU.max)
            link(dve.tensor_scalar(empty[:], held[:], 0.0, None, ALU.is_equal))
            link(dve.tensor_scalar(held[:], held[:], 1.0, None, ALU.subtract))
            link(dve.tensor_scalar(zero_f[:], empty[:], float(TOK + 1), None, ALU.mult))
            link(dve.tensor_tensor(held[:], held[:], zero_f[:], ALU.add))
            link(dve.tensor_scalar(empty[:], empty[:], t.cst[:, CP:CP + 1], None, ALU.mult))
            link(dve.tensor_tensor(t.scatter[:], held[:], empty[:], ALU.add))


def experts(nc, t, gate_up, down_a, down_b, xrows, out):
    NW = 4
    GU = 2 * INTER
    I2 = INTER - P
    with ExitStack() as ctx:
        sb = lambda n, s, d: ctx.enter_context(nc.sbuf_tensor(n, s, d))
        pb = lambda n, s, d: ctx.enter_context(nc.psum_tensor(n, s, d))
        sem = lambda n: ctx.enter_context(nc.semaphore(n))
        w_gu = sb("w_gu", [P, NW * KC * GU], F32)
        w_da = sb("w_da", [P, NW * D], F32)
        w_db = sb("w_db", [I2, NW * D], F32)
        x = sb("e_x", [P, 2, XROW], F32)
        read_at = sb("read_at", [P, 2], I32)
        add_at = sb("add_at", [P, 2], I32)
        weight = sb("e_weight", [P, 2], F32)
        xT = sb("e_xT", [P, 2, D], F32)
        gated = sb("gated", [P, INTER], F32)
        h = sb("e_h", [P, INTER], F32)
        hT = sb("e_hT", [P, 2, P], F32)
        y = sb("e_y", [P, 2, D], F32)
        xT_p = pb("xT_p", [P, 512], F32)
        gu_p = pb("gu_p", [P, 512], F32)
        hT_p = pb("hT_p", [P, 512], F32)
        y_p = pb("y_p", [P, 512], F32)

        s_w = [sem(f"s_w{b}") for b in range(NW)]
        s_expert = sem("s_expert")
        s_read_at = sem("s_read_at")
        s_add_at = sem("s_add_at")
        s_x = [sem("s_x0"), sem("s_x1")]
        s_pool_step = sem("s_pool_step")
        s_end = sem("s_end")
        s_xT = sem("e_s_xT")
        s_xT_sb = sem("e_xT_sb")
        s_weight = sem("e_weight_s")
        s_gu = sem("s_gu")
        s_silu = sem("s_silu")
        s_h = sem("e_s_h")
        s_hT = sem("e_s_hT")
        s_hT_sb = sem("e_hT_sb")
        s_y = sem("e_s_y")
        s_y_sb = sem("e_y_sb")
        s_added = [sem("s_added0"), sem("s_added1")]
        block = ctx.enter_context(nc.Block())
        ident = t.cst[:, CI:CI + P]

        def tiles_in_use(eng):
            return eng.value_load(t.bound[0:1, 3 + EXPERTS:4 + EXPERTS], min_val=1, max_val=TILES)

        def steps(eng, body):
            tiles = tiles_in_use(eng)
            with eng.Fori(0, TILES // 2) as m:
                with eng.If(m * 2 < tiles):
                    for b in (1, 0):
                        body(m, b, m * 2 + (2 - b))

        @block.sync
        def _(sp):
            with sp.Fori(0, EXPERTS // NW) as m:
                for b in range(NW):
                    e = m * NW + b
                    sp.wait_ge(s_y, sp.value_load(t.bound[0:1, bass.ds(e, 1)], min_val=0, max_val=TILES))
                    for w, src, n in ((w_gu, gate_up, KC * GU), (w_da, down_a, D), (w_db, down_b, D)):
                        sp.dma_start(w[:, b * n:(b + 1) * n], src[bass.ds(e, 1)].rearrange("a p c -> (a p) c")).then_inc(s_w[b], 16)
                    sp.wait_ge(s_w[(b + 2) % NW], (m + (b >= 2)) * 48)
                    sp.nop().then_inc(s_expert, 1)
            for b in range(2, NW):
                sp.wait_ge(s_w[b], 48 * (EXPERTS // NW))
                sp.nop().then_inc(s_expert, 1)
            rounds = (tiles_in_use(sp) + 1) >> 1
            for b in range(2):
                sp.wait_ge(s_added[b], rounds * 16)
                sp.wait_ge(s_x[b], (rounds + (2 - b)) * 16)
            sp.nop().then_inc(s_end, 1)

        @block.gpsimd
        def _(pool):
            def read(b):
                pool.indirect_dma_start(x[:, b, :], None, xrows, bass.IndirectOffsetOnAxis(ap=read_at[:, b:b + 1], axis=0),
                                        bounds_check=TOK - 1, oob_is_err=False).then_inc(s_x[b], 16)

            def add(b):
                pool.indirect_dma_start(out, bass.IndirectOffsetOnAxis(ap=add_at[:, b:b + 1], axis=0), y[:, b, :], None,
                                        bounds_check=TOK + P - 1, oob_is_err=True,
                                        compute_op=ALU.add).then_inc(s_added[b], 16)

            for n in range(3):
                pool.wait_ge(s_read_at, n + 1)
                if n == 2:
                    pool.wait_ge(s_xT, 1)
                    pool.wait_ge(s_weight, 1)
                read(n % 2)

            def body(m, b, i):
                pool.wait_ge(s_read_at, i + 3)
                pool.wait_ge(s_xT, i + 1)
                pool.wait_ge(s_weight, i + 1)
                pool.nop().then_inc(s_pool_step, 1)
                read(b)
                pool.wait_ge(s_add_at, i)
                pool.wait_ge(s_y_sb, i)
                pool.wait_ge(s_added[b], (m + (1 - b)) * 16)
                pool.nop().then_inc(s_pool_step, 1)
                add(1 - b)

            steps(pool, body)

        @block.tensor
        def _(pe):
            def turn_x(b):
                for c in range(KC):
                    last = pe.transpose(xT_p[:, c * P:(c + 1) * P], x[:, b, c * P:(c + 1) * P], ident)
                last.then_inc(s_xT, 1)

            def expert_of(i):
                return pe.value_load(t.tile_expert[0:1, bass.ds(i, 1)], min_val=0, max_val=EXPERTS - 1)

            def multiply(b, e):
                pe.wait_ge(s_expert, e + 3)
                at = (e & (NW - 1)) * (KC * GU)
                for c in range(KC):
                    last = pe.matmul(gu_p[:, 0:GU], xT[:, b, c * P:(c + 1) * P], w_gu[:, bass.ds(at + c * GU, GU)],
                                     start=(c == 0), stop=(c == KC - 1))
                last.then_inc(s_gu, 1)

            for b in range(2):
                pe.wait_ge(s_x[b], 16)
                if b:
                    pe.wait_ge(s_xT_sb, 1)
                turn_x(b)
            multiply(0, expert_of(0))

            def body(m, b, i):
                pe.wait_ge(s_h, i)
                pe.transpose(hT_p[:, 0:P], h[:, 0:P], ident)
                pe.transpose(hT_p[0:I2, P:2 * P], h[:, P:INTER], ident).then_inc(s_hT, 1)
                pe.wait_ge(s_x[1 - b], m * 16 + 32)
                pe.wait_ge(s_xT_sb, i + 1)
                turn_x(1 - b)
                at = (expert_of(i - 1) & (NW - 1)) * D
                pe.wait_ge(s_hT_sb, i)
                pe.wait_ge(s_y_sb, i - 1)
                pe.matmul(y_p[:], hT[:, 0, :], w_da[:, bass.ds(at, D)], start=True, stop=False)
                pe.matmul(y_p[:], hT[0:I2, 1, :], w_db[:, bass.ds(at, D)], start=False, stop=True).then_inc(s_y, 1)
                multiply(b, expert_of(i))

            steps(pe, body)

        @block.scalar
        def _(act):
            def copy_xT(b):
                act.copy(xT[:, b, :], xT_p[:]).then_inc(s_xT_sb, 1)

            def take_weight(b, i):
                e = act.value_load(t.tile_expert[0:1, bass.ds(i, 1)], min_val=0, max_val=EXPERTS - 1)
                act.copy(weight[:, b:b + 1], x[:, b, bass.ds(e + D, 1)]).then_inc(s_weight, 1)

            for b in range(2):
                act.wait_ge(s_xT, b + 1)
                copy_xT(b)
                take_weight(b, b)
            act.wait_ge(s_gu, 1)
            act.activation(gated[:], gu_p[:, 0:INTER], ACT.Silu).then_inc(s_silu, 1)

            def body(m, b, i):
                act.wait_ge(s_xT, i + 2)
                act.wait_ge(s_gu, i)
                copy_xT(1 - b)
                act.wait_ge(s_y, i)
                act.wait_ge(s_added[1 - b], m * 16)
                act.activation(y[:, 1 - b, :], y_p[:], ACT.Copy, scale=weight[:, 1 - b:2 - b]).then_inc(s_y_sb, 1)
                act.wait_ge(s_y_sb, i)
                take_weight(1 - b, i + 1)
                act.wait_ge(s_gu, i + 1)
                act.wait_ge(s_h, i)
                act.activation(gated[:], gu_p[:, 0:INTER], ACT.Silu).then_inc(s_silu, 1)

            steps(act, body)

        @block.vector
        def _(dve):
            def next_read(b, i):
                dve.tensor_copy(read_at[:, b:b + 1], t.gather[:, bass.ds(i, 1)]).then_inc(s_read_at, 1)

            for b in range(2):
                next_read(b, b)
            dve.wait_ge(s_x[0], 16)
            next_read(0, 2)
            dve.wait_ge(s_silu, 1)
            dve.tensor_tensor(h[:], gated[:], gu_p[:, INTER:GU], ALU.mult).then_inc(s_h, 1)

            def body(m, b, i):
                dve.wait_ge(s_hT, i)
                dve.wait_ge(s_y, i - 1)
                dve.tensor_copy(hT[0:I2, 1, :], hT_p[0:I2, P:2 * P])
                dve.tensor_copy(hT[:, 0, :], hT_p[:, 0:P]).then_inc(s_hT_sb, 1)
                dve.wait_ge(s_added[1 - b], m * 16)
                dve.tensor_copy(add_at[:, 1 - b:2 - b], t.scatter[:, bass.ds(i - 1, 1)]).then_inc(s_add_at, 1)
                dve.wait_ge(s_x[b], (m + (2 - b)) * 16)
                next_read(b, i + 2)
                dve.wait_ge(s_silu, i + 1)
                dve.tensor_tensor(h[:], gated[:], gu_p[:, INTER:GU], ALU.mult).then_inc(s_h, 1)

            steps(dve, body)


def program(nc, ids, hot_ids, hot_w, cold_w, proj, wqkv, wo, gate, gate_up, down_a, down_b, cst, rope, out):
    t = Chip()
    table = nc.dram_tensor("token_table", (VOCAB, 4), I32).ap()
    xrows = nc.dram_tensor("expert_rows", (TOK, XROW), F32).ap()
    with ExitStack() as ctx:
        sb = lambda n, s, d: ctx.enter_context(nc.sbuf_tensor(n, s, d))
        t.h = sb("h", [P, NT + 2, D], F32)
        t.cst = sb("cst", [P, CST_COLS], F32)
        with nc.sbuf_tensor("ln", [P, NT + 2, 2], F32) as t.ln:
            embed(nc, t, ids, hot_ids, hot_w, cold_w, proj, cst, table)
            attend(nc, t, wqkv, wo, rope)
        t.bound = sb("bound", [1, EXPERTS + 4], I32)
        t.tile_expert = sb("tile_expert", [1, SLOTS], I32)
        t.gather = sb("gather", [P, SLOTS], I32)
        t.scatter = sb("scatter", [P, SLOTS], I32)
        route(nc, t, gate, xrows, out)
        experts(nc, t, gate_up, down_a, down_b, xrows, out)


def by_partition(w):
    return w.reshape(-1, P, w.shape[-1]).transpose(1, 0, 2)


def kernel(**inputs):
    import concourse.bacc as bacc
    from concourse.bass_utils import run_bass_kernel_spmd

    given = {name: np.asarray(a) for name, a in inputs.items()}
    q_order, k_order = head_order()
    w_gu = given["L0_ffn_gate_up_proj"].transpose(0, 2, 1).reshape(EXPERTS, KC, P, 2 * INTER)
    w_down = given["L0_ffn_down_proj"].transpose(0, 2, 1)
    laid = dict(
        ids=given["x"].reshape(NT, P).T,
        hot_ids=given["L0_tok_hot_token_ids"],
        hot_w=given["L0_tok_hot_emb_w"],
        cold_w=given["L0_tok_cold_emb_w"],
        proj=given["L0_tok_proj_w"].T,
        wqkv=by_partition(np.concatenate([given["L0_attn_wq"][q_order], given["L0_attn_wk"][k_order],
                                          given["L0_attn_wv"]], 0).T),
        wo=by_partition(given["L0_attn_wo"].T),
        gate=by_partition(given["L0_ffn_gate_weight"].T),
        gate_up=w_gu.transpose(0, 2, 1, 3).reshape(EXPERTS, P, KC * 2 * INTER),
        down_a=w_down[:, :P],
        down_b=w_down[:, P:],
        constants=constants(),
        rope=rope_table(),
    )
    nc = bacc.Bacc("TRN2", target_bir_lowering=False, num_devices=1)
    arrays, args = {}, []
    for name, a in laid.items():
        arrays["in_" + name] = np.ascontiguousarray(a)
        args.append(nc.dram_tensor("in_" + name, a.shape, mybir.dt.from_np(a.dtype), kind="ExternalInput").ap())
    args.append(nc.dram_tensor("out_rows", (TOK + P, D), F32, kind="ExternalOutput").ap())
    program(nc, *args)
    r = run_bass_kernel_spmd(nc, [arrays], core_ids=[0])
    return r.results[0]["out_rows"][:TOK].reshape(BATCH, SEQ, D)
```

```python
from contextlib import ExitStack

import numpy as np
import concourse.bass as bass
from concourse import mybir

F32 = mybir.dt.float32
F32R = mybir.dt.float32r
BF16 = mybir.dt.bfloat16
F16 = mybir.dt.float16
I32 = mybir.dt.int32
ALU = mybir.AluOpType
ACT = mybir.ActivationFunctionType
AX = mybir.AxisListType

P = 128
BATCH, SEQ = 8, 256
TOK = BATCH * SEQ
NT = TOK // P
D = 512
KC = D // P
VOCAB, HOT, LATENT = 32000, 8000, 128
COLD = VOCAB - HOT
VR, VC = 125, 256
HR, HC = 125, 64
HOT_UNIT = 8192.0
EPS = 1e-5

CI, CT, CN, CP = 0, 128, 256, 512
CST_COLS = CP + 5


def constants():
    c = np.zeros((P, CST_COLS), np.float32)
    p = np.arange(P)
    c[:, CI:CI + P] = np.eye(P)
    c[:, CT:CT + P] = p[:, None] < p[None, :]
    c[:, CN:CN + VC] = np.arange(VC)
    c[:, CP] = p
    c[:, CP + 1] = HC * (HOT_UNIT / HC + p)
    c[:, CP + 2] = VC * p
    c[:, CP + 3] = p % 32 < 16
    c[:, CP + 4] = p % 32 >= 16
    return c


class Chip:
    pass


def linker(eng, sem):
    count = [0]

    def link(ins, base=0):
        count[0] += 1
        ins.then_inc(sem, 1)
        eng.wait_ge(sem, base + count[0])

    return link


def rsqrt(dve, sem, at, out, var, root):
    y = out
    dve.reciprocal(y, root).then_inc(sem, 1)
    dve.wait_ge(sem, at + 1)
    dve.tensor_tensor(root, y, y, ALU.mult).then_inc(sem, 1)
    dve.wait_ge(sem, at + 2)
    dve.tensor_tensor(root, root, var, ALU.mult).then_inc(sem, 1)
    dve.wait_ge(sem, at + 3)
    dve.tensor_scalar(root, root, -0.5, 1.5, ALU.mult, ALU.add).then_inc(sem, 1)
    dve.wait_ge(sem, at + 4)
    dve.tensor_tensor(out, y, root, ALU.mult).then_inc(sem, 1)
    dve.wait_ge(sem, at + 5)


def moments(dve, sem, at, stats, mean, var, calc):
    dve.tensor_tensor(mean, stats[:, :, 1], stats[:, :, 4], ALU.add)
    dve.tensor_tensor(calc, stats[:, :, 1], stats[:, :, 4], ALU.subtract).then_inc(sem, 1)
    dve.wait_ge(sem, at + 1)
    dve.tensor_scalar(mean, mean, 0.5, None, ALU.mult)
    dve.scalar_tensor_tensor(calc, calc, 0.25, calc, ALU.mult, ALU.mult)
    dve.tensor_tensor(var, stats[:, :, 2], stats[:, :, 5], ALU.add).then_inc(sem, 1)
    dve.wait_ge(sem, at + 2)
    dve.scalar_tensor_tensor(calc, var, 1.0 / D, calc, ALU.mult, ALU.add).then_inc(sem, 1)
    dve.wait_ge(sem, at + 3)
    dve.tensor_scalar(var, calc, EPS, None, ALU.add).then_inc(sem, 1)
    dve.wait_ge(sem, at + 4)


def embed(nc, t, ids, hot_ids, hot_w, cold_w, proj, wqkv, wo, cst, table):
    NB = 4
    NH = 8
    with ExitStack() as ctx:
        sb = lambda n, s, d: ctx.enter_context(nc.sbuf_tensor(n, s, d))
        pb = lambda n, s, d: ctx.enter_context(nc.psum_tensor(n, s, d))
        sem = lambda n: ctx.enter_context(nc.semaphore(n))
        tok = sb("tok", [P, NT], I32)
        tok_neg = sb("tok_neg", [P, NT], I32)
        tokf = sb("tokf", [P, NT], F32)
        hid = sb("hid", [HR, HC], I32)
        hneg = sb("hneg", [HR, HC], I32)
        hi = sb("hi", [HR, 2, HC], I32)
        hf = sb("hf", [HR, 2, HC], F32)
        count_row = sb("count_row", [P, VC], BF16)
        row_hot = sb("row_hot", [HR, NH, 2, VR], BF16)
        col_hot = sb("col_hot", [HR, NH, VC], BF16)
        zero = sb("zero", [HR, VC], BF16)
        ones = sb("ones", [P, VC], F32)
        hits = sb("hits", [VR, VC], F32)
        is_hot = sb("is_hot", [VR, VC], F32)
        run = sb("run", [VR, VC], F32)
        calc = sb("calc", [VR, VC], F32)
        side = sb("side", [VR, 4], F32)
        flag = sb("flag", [1, 1], I32)
        rows = sb("rows", [VR, VC, 4], I32)
        look = sb("look", [P, NT, 4], I32)
        hot_at = sb("hot_at", [P, NT], I32)
        cold = sb("cold", [P, NT], I32)
        lat = sb("lat", [P, NB, LATENT], F32)
        row = sb("row", [P, NB, D], F32)
        stats = sb("stats", [P, NT, 6], F32)
        take = sb("take", [P, NB], I32)
        ln_calc = sb("ln_calc", [P, 2, NT], F32)
        latT = sb("latT", [P, 2, P], F32)
        pj = sb("proj_sb", [P, D], F32)
        all_i = sb("all_i", [P, HOT], I32)
        all_f = sb("all_f", [P, HOT], F32)
        order = t.h[:, 0:NT, :].rearrange("p a d -> p (a d)")[:, 0:HOT]
        raw = sb("w_raw", [P, 2, QKV], F32)
        best = sb("best", [P, 2], F32)

        count = pb("count", [P, 512], F32)
        small = pb("small", [P, 512], F32)
        turned = pb("turned", [P, 2, 512], F32)
        projected = pb("projected", [P, 2, 512], F32)

        s_ids = sem("s_ids")
        s_hid = sem("s_hid")
        s_cst = sem("s_cst")
        s_pj = sem("s_pj")
        s_v = sem("s_v")
        s_onehot = sem("s_onehot")
        s_counted = sem("s_counted")
        s_total = sem("s_total")
        s_scan = sem("s_scan")
        s_inputs = sem("s_inputs")
        s_prefix = sem("s_prefix")
        s_rows = sem("s_rows")
        s_flag = sem("s_flag")
        s_tok = sem("s_tok")
        s_table = sem("s_table")
        s_raw = [sem("s_raw0"), sem("s_raw1")]
        s_split_hi = sem("s_split_hi")
        s_split = sem("s_split")
        s_look = sem("s_look")
        s_index = sem("s_index")
        s_hot = [sem(f"s_hot{b}") for b in range(NB)]
        s_lat = [sem(f"s_lat{b}") for b in range(NB)]
        s_turned = sem("s_turned")
        s_latT = sem("s_latT")
        s_proj = sem("s_proj")
        s_token = sem("s_token")
        s_all = sem("s_all")
        s_done = sem("s_done")
        s_kept = sem("s_kept")
        s_take = sem("s_take")
        s_stat = sem("s_stat")
        s_var = sem("s_var")
        s_sqrt = sem("s_sqrt")
        block = ctx.enter_context(nc.Block())

        iota = t.cst[:, CN:CN + VC]

        @block.sync
        def _(sp):
            sp.dma_start(hid[:], hot_ids.rearrange("(p c) -> p c", c=HC)).then_inc(s_hid, 16)
            sp.dma_start(t.cst[:], cst).then_inc(s_cst, 16)
            sp.dma_start(tok[:], ids).then_inc(s_ids, 16)
            sp.dma_start(pj[:], proj).then_inc(s_pj, 16)
            sp.wait_ge(s_rows, 1)
            sp.dma_start(table.rearrange("(p c) k -> p c k", c=VC), rows[:]).then_inc(s_table, 16)
            sp.wait_ge(s_flag, 1)
            twice = sp.value_load(flag[0:1, 0:1], min_val=0, max_val=1)
            with sp.If(twice > 0):
                sp.dma_start(all_i[:], hot_ids.rearrange("(a c) -> a c", a=1).broadcast_to([P, HOT])).then_inc(s_all, 16)
            sp.wait_ge(s_table, 16)

        def is_first(j):
            return isinstance(j, int) and j < 2

        chunks = ([(wqkv[:, c, :], t.wq_hi[:, c, :], t.wq_lo[:, c, :], QKV) for c in range(KC)]
                  + [(wo[:, c, :], t.wo_hi[:, c, :], t.wo_lo[:, c, :], D) for c in range(KC)])

        @block.gpsimd
        def _(pool):
            for n, (_, hi, lo, w) in enumerate(chunks):
                pool.wait_ge(s_split_hi, n + 1)
                pool.tensor_tensor(lo, raw[:, n % 2, 0:w], hi.bitcast(F32), ALU.subtract).then_inc(s_split, 1)
            pool.wait_ge(s_table, 16)
            pool.wait_ge(s_tok, 1)
            for j in range(NT):
                pool.indirect_dma_start(look[:, j, :], None, table, bass.IndirectOffsetOnAxis(ap=tok[:, j:j + 1], axis=0),
                                        bounds_check=VOCAB - 1, oob_is_err=False).then_inc(s_look, 16)
            pool.wait_ge(s_index, 1)
            for j in range(NT):
                b, k = j % NB, j // NB
                if k:
                    pool.wait_ge(s_hot[b], 16 * k)
                    pool.wait_ge(s_turned, NB * (k - 1) + b + 1)
                    pool.wait_ge(s_kept, NB * (k - 1) + b + 1)
                    pool.wait_ge(s_stat, NB * (k - 1) + b + 1)
                pool.indirect_dma_start(lat[:, b, :], None, cold_w, bass.IndirectOffsetOnAxis(ap=cold[:, j:j + 1], axis=0),
                                        bounds_check=COLD - 1, oob_is_err=False).then_inc(s_lat[b], 16)
                pool.indirect_dma_start(row[:, b, :], None, hot_w, bass.IndirectOffsetOnAxis(ap=hot_at[:, j:j + 1], axis=0),
                                        bounds_check=HOT - 1, oob_is_err=False).then_inc(s_hot[b], 16)

        @block.tensor
        def _(pe):
            pe.wait_ge(s_v, 1)
            pe.matmul(count[0:VR, 0:VC], zero[:, 0:VR], zero[:], start=True, stop=False)
            with pe.Fori(0, HC // NH) as i:
                for b in range(NH):
                    pe.wait_ge(s_onehot, i * NH + (b + 1))
                    pe.matmul(count[0:VR, 0:VC], row_hot[:, b, 0, :], col_hot[:, b, :], start=False, stop=False)
                    pe.matmul(count[0:VR, 0:VC], row_hot[:, b, 1, :], col_hot[:, b, :], start=False,
                              stop=False).then_inc(s_counted, 1)
            pe.matmul(count[0:VR, 0:VC], zero[:, 0:VR], zero[:], start=False, stop=True).then_inc(s_total, 1)
            pe.wait_ge(s_scan, 1)
            pe.matmul(small[0:VR, 0:1], t.cst[0:VR, CT:CT + VR], run[:, VC - 1:VC], start=True, stop=True)
            pe.matmul(small[0:1, 1:2], ones[0:VR, 0:1], side[:, 1:2], start=True, stop=True).then_inc(s_prefix, 1)
            pe.wait_ge(s_pj, 16)

            def turn(b, j, landed):
                pe.wait_ge(s_lat[b], landed)
                if not is_first(j):
                    pe.wait_ge(s_latT, j - 1)
                pe.transpose(turned[:, b % 2, 0:P], lat[:, b, :], t.cst[:, CI:CI + P]).then_inc(s_turned, 1)

            def project(b, j):
                pe.wait_ge(s_latT, j + 1)
                if not is_first(j):
                    pe.wait_ge(s_token, j - 1)
                pe.matmul(projected[:, b % 2, :], latT[:, b % 2, :], pj[:], start=True, stop=True).then_inc(s_proj, 1)

            turn(0, 0, 16)
            for b in range(NB):
                if b + 1 < NB:
                    turn(b + 1, b + 1, 16)
                    project(b, b)
            with pe.Fori(1, NT // NB) as i:
                for b in range(NB):
                    turn(b, i * NB + b, i * 16 + 16)
                    project((b - 1) % NB, i * NB + (b - 1))
            project(NB - 1, NT - 1)

        @block.scalar
        def _(act):
            def load(n):
                act.dma_start(raw[:, n % 2, 0:chunks[n][3]], chunks[n][0]).then_inc(s_raw[n % 2], 16)

            load(0)
            load(1)
            for n, (_, hi, _, w) in enumerate(chunks):
                act.wait_ge(s_raw[n % 2], 16 * (n // 2 + 1))
                act.copy(hi, raw[:, n % 2, 0:w]).then_inc(s_split_hi, 1)
                if n + 2 < len(chunks):
                    act.wait_ge(s_split, n + 1)
                    load(n + 2)

            def copy_latT(b, j):
                act.wait_ge(s_turned, j + 1)
                if not is_first(j):
                    act.wait_ge(s_proj, j - 1)
                act.copy(latT[:, b % 2, :], turned[:, b % 2, 0:P]).then_inc(s_latT, 1)

            def keep(b, j):
                act.wait_ge(s_token, j + 1)
                act.copy(t.h[:, bass.ds(j, 1), :].rearrange("p a d -> p (a d)"), row[:, b, :]).then_inc(s_kept, 1)

            for b in range(NB):
                copy_latT(b, b)
                if b:
                    keep(b - 1, b - 1)
            with act.Fori(1, NT // NB) as i:
                for b in range(NB):
                    copy_latT(b, i * NB + b)
                    keep((b - 1) % NB, i * NB + (b - 1))
            keep(NB - 1, NT - 1)
            act.wait_ge(s_var, 1)
            act.activation(ln_calc[:, 0, :], ln_calc[:, 1, :], ACT.Sqrt).then_inc(s_sqrt, 1)

        @block.vector
        def _(dve):
            link = linker(dve, s_v)
            link(dve.memset(zero[:], 0.0))
            dve.memset(ones[:], 1.0).then_inc(s_done, 1)
            dve.wait_ge(s_hid, 16)
            link(dve.tensor_scalar(hneg[:], hid[:], 0, VOCAB, ALU.is_lt, ALU.mult))
            link(dve.tensor_tensor(hid[:], hid[:], hneg[:], ALU.add))
            dve.tensor_scalar(hi[:, 0, :], hid[:], 8, None, ALU.arith_shift_right).then_inc(s_done, 1)
            link(dve.tensor_scalar(hi[:, 1, :], hid[:], VC - 1, None, ALU.bitwise_and))
            dve.wait_ge(s_done, 2)
            link(dve.tensor_copy(hf[:], hi[:]))
            dve.wait_ge(s_cst, 16)
            link(dve.tensor_copy(count_row[:], iota))
            def one_hots(b, c):
                row_id, col_id = hf[:, 0, bass.ds(c, 1)], hf[:, 1, bass.ds(c, 1)]
                dve.tensor_scalar(row_hot[:, b, 0, :], count_row[0:HR, 0:VR], row_id, t.cst[0:HR, CP + 1:CP + 2],
                                  ALU.is_equal, ALU.mult)
                dve.tensor_scalar(row_hot[:, b, 1, :], count_row[0:HR, 0:VR], row_id, t.cst[0:HR, bass.ds(c + CN, 1)],
                                  ALU.is_equal, ALU.mult)
                dve.tensor_scalar(col_hot[:, b, :], count_row[0:HR, :], col_id, None, ALU.is_equal).then_inc(s_onehot, 1)

            for b in range(NH):
                one_hots(b, b)
            with dve.Fori(1, HC // NH) as i:
                for b in range(NH):
                    dve.wait_ge(s_counted, (i - 1) * NH + (b + 1))
                    one_hots(b, i * NH + b)
            dve.wait_ge(s_ids, 16)
            link(dve.tensor_scalar(tok_neg[:], tok[:], 0, VOCAB, ALU.is_lt, ALU.mult))
            link(dve.tensor_tensor(tok[:], tok[:], tok_neg[:], ALU.add))
            link(dve.tensor_scalar(tok[:], tok[:], 0, VOCAB - 1, ALU.max, ALU.min))
            dve.tensor_copy(tokf[:], tok[:]).then_inc(s_tok, 1)
            dve.wait_ge(s_total, 1)
            link(dve.tensor_copy(hits[:], count[0:VR, 0:VC]))
            dve.memset(rows[:], 0).then_inc(s_done, 1)
            dve.tensor_reduce(side[:, 0:1], hits[:], AX.X, ALU.max).then_inc(s_done, 1)
            link(dve.tensor_scalar(is_hot[:], hits[:], HOT_UNIT, None, ALU.is_ge))
            dve.wait_ge(s_done, 4)
            dve.tensor_scalar(side[:, 1:2], side[:, 0:1], 2 * HOT_UNIT, None, ALU.is_ge).then_inc(s_done, 1)
            link(dve.tensor_tensor_scan(run[:], ones[0:VR, :], is_hot[:], 0.0, ALU.mult, ALU.add))
            dve.wait_ge(s_done, 5)
            dve.nop().then_inc(s_scan, 1)
            link(dve.scalar_tensor_tensor(calc[:], is_hot[:], -HOT_UNIT, hits[:], ALU.mult, ALU.add))
            link(dve.tensor_scalar(rows[:, :, 0], calc[:], float(HOT - 1), None, ALU.min))
            link(dve.scalar_tensor_tensor(calc[:], iota[0:VR, :], t.cst[0:VR, CP + 2:CP + 3], run[:], ALU.add, ALU.subtract))
            dve.wait_ge(s_prefix, 1)
            dve.tensor_scalar(flag[:], small[0:1, 1:2], 0.0, None, ALU.is_gt).then_inc(s_flag, 1)
            link(dve.tensor_copy(side[:, 2:3], small[0:VR, 0:1]))
            link(dve.tensor_scalar(calc[:], calc[:], side[:, 2:3], 0.0, ALU.subtract, ALU.max))
            link(dve.tensor_scalar(rows[:, :, 1], calc[:], float(COLD - 1), None, ALU.min))
            dve.tensor_scalar(rows[:, :, 2], is_hot[:], -1.0, 1.0, ALU.mult, ALU.add).then_inc(s_rows, 1)
            dve.wait_ge(s_look, 16 * NT)
            link(dve.tensor_copy(hot_at[:], look[:, :, 0]))
            dve.wait_ge(s_flag, 1)
            twice = dve.value_load(flag[0:1, 0:1], min_val=0, max_val=1)
            with dve.If(twice > 0):
                dve.wait_ge(s_all, 16)
                dve.memset(all_f[:], 1.0).then_inc(s_done, 1)
                dve.wait_ge(s_done, 6)
                dve.tensor_tensor_scan(order, all_f[:], all_f[:], 0.0, ALU.mult, ALU.add).then_inc(s_done, 1)
                dve.wait_ge(s_done, 7)
                dve.tensor_scalar(all_f[:], all_i[:], 0, float(VOCAB), ALU.is_lt, ALU.mult).then_inc(s_done, 1)
                dve.wait_ge(s_done, 8)
                dve.tensor_tensor(all_f[:], all_f[:], all_i[:], ALU.add).then_inc(s_done, 1)
                dve.wait_ge(s_done, 9)
                scratch = all_i[:].bitcast(F32)
                with dve.Fori(0, NT) as j:
                    dve.scalar_tensor_tensor(scratch, all_f[:], tokf[:, bass.ds(j, 1)], order, ALU.is_equal,
                                             ALU.mult).then_inc(s_done, 1)
                    dve.wait_ge(s_done, j * 3 + 10)
                    dve.tensor_reduce(best[:, 0:1], scratch, AX.X, ALU.max).then_inc(s_done, 1)
                    dve.wait_ge(s_done, j * 3 + 11)
                    dve.tensor_scalar(hot_at[:, bass.ds(j, 1)], best[:, 0:1], 1.0, 0.0, ALU.subtract,
                                      ALU.max).then_inc(s_done, 1)
                    dve.wait_ge(s_done, j * 3 + 12)
            dve.tensor_copy(cold[:], look[:, :, 1]).then_inc(s_index, 1)
            with dve.Fori(0, NT // NB) as i:
                for b in range(NB):
                    j = i * NB + b
                    dve.tensor_copy(take[:, b:b + 1], look[:, bass.ds(j, 1), 2]).then_inc(s_take, 1)
                    dve.wait_ge(s_proj, j + 1)
                    dve.wait_ge(s_hot[b], i * 16 + 16)
                    dve.wait_ge(s_take, j + 1)
                    dve.nop().then_inc(s_inputs, 1)
                    dve.copy_predicated(row[:, b, :], take[:, b:b + 1].broadcast_to([P, D]),
                                        projected[:, b % 2, :]).then_inc(s_token, 1)
                    dve.wait_ge(s_token, j + 1)
                    dve.bn_stats(stats[:, bass.ds(j, 1), :].rearrange("p a d -> p (a d)"), row[:, b, :]).then_inc(s_stat, 1)
            dve.memset(t.h[:, NT:, :], 0.0).then_inc(s_stat, 1)
            dve.memset(t.ln[:, NT:, :], 0.0).then_inc(s_stat, 1)
            dve.wait_ge(s_stat, NT + 2)
            moments(dve, s_stat, NT + 2, stats, t.ln[:, 0:NT, 0], ln_calc[:, 1, :], ln_calc[:, 0, :])
            dve.nop().then_inc(s_var, 1)
            dve.wait_ge(s_sqrt, 1)
            rsqrt(dve, s_stat, NT + 6, t.ln[:, 0:NT, 1], ln_calc[:, 1, :], ln_calc[:, 0, :])


HEADS, KV, HD = 32, 8, 16
GROUP = HEADS // KV
QKV = (HEADS + 2 * KV) * HD
KF = KV * HD
NG = 20
MASKED = -1e30
STEPS = 24


def attention_units():
    return ([(1, i, m, 1) for i in range(GROUP) for m in range(KV // 2)]
            + [(0, i, m, 2) for i in range(GROUP) for m in (0, 2)])


UNITS = attention_units()
FRONT = [("x", 0), ("q", 1), ("kv", 2), ("g0", 4), ("g1", 5), ("g2", 6), ("g3", 7), ("k", 8)]
TURNS = ([(s + 3, (w, 0)) for w, s in FRONT] + [(s + 12, (w, 1)) for w, s in FRONT]
         + [(21, ("o", 1)), (22, ("w", 1)), (25, ("o", 0)), (26, ("w", 0))])
AHEAD = 3
NF = len(FRONT) * 2
ON_ACT = {"x", "g0", "g1", "k", "o"}
ON_DVE = {"x", "q", "kv", "g2", "g3", "o", "w"}
PT_ON_ACT = [n for n in range(STEPS) if n % 5 in (1, 3)]


def attend(nc, t, rope):
    NB2 = BATCH // 2
    with ExitStack() as ctx:
        sb = lambda n, s, d: ctx.enter_context(nc.sbuf_tensor(n, s, d))
        pb = lambda n, s, d: ctx.enter_context(nc.psum_tensor(n, s, d))
        sem = lambda n: ctx.enter_context(nc.semaphore(n))
        wq_hi, wq_lo, wo_hi, wo_lo = t.wq_hi, t.wq_lo, t.wo_hi, t.wo_lo
        rot = sb("rot", [P, 2, 4, HD], F32)
        hide = sb("hide", [P, P], BF16)
        eye = sb("eye", [P, P], BF16)
        xn = sb("xn", [P, D], F32)
        x_hi = sb("x_hi", [P, D], F32R)
        x_lo = sb("x_lo", [P, D], F32R)
        r1 = sb("r1", [P, NG * 32], F32)
        r2 = sb("r2", [P, NG * 32], F32)
        parts = sb("parts", [P, NG, 96], F32R)
        q_sb = sb("q_sb", [96, 2, 16, SEQ], F32R)
        k_sb = sb("k_sb", [96, 2, 4, 2, SEQ], F32R)
        v_sb = sb("v_sb", [P, 2, 2, KF], F32)
        nmax = sb("nmax", [P, 3, 4], F32)
        sums = sb("sums", [P, 2, HEADS], F32)
        inv = sb("inv", [P, 2, HEADS], F32)
        prob = sb("prob", [P, 2, 512], F32)
        probT = sb("probT", [P, 2, 512], F32)
        on = sb("on", [P, D], F32)
        o_hi = sb("o_hi", [P, D], F32R)
        o_lo = sb("o_lo", [P, D], F32R)

        score = pb("score", [P, 3, 512], F32)
        turned = pb("p_turned", [P, 2, 512], F32)
        mixed = pb("mixed", [P, 512], F32)
        work = pb("work", [P, 2, 512], F32)

        s_tab = sem("s_tab")
        s_eye = sem("s_eye")
        s_xn = sem("s_xn")
        s_work = sem("s_work")
        s_work_act = sem("s_work_act")
        s_work_dve = sem("s_work_dve")
        s_pool = sem("s_pool")
        s_score = sem("s_score")
        s_max = sem("s_max")
        s_prob = sem("s_prob")
        s_turned = sem("s_pturned")
        s_pt_act = sem("s_pt_act")
        s_pt_dve = sem("s_pt_dve")
        s_pv = sem("s_pv")
        s_inv = sem("s_inv")
        s_on = sem("s_on")
        block = ctx.enter_context(nc.Block())

        ident = t.cst[:, CI:CI + P]

        class At:

            def __init__(self, it, half):
                self.it, self.half = it, half
                self.first = it is None or (isinstance(it, int) and half == 0)
                self.buf = half % 2

            def __call__(self, per_batch, k, before=0):
                if self.it is None:
                    return k
                return self.it * (2 * per_batch) + (before + self.half * per_batch + k)

        FIRST = At(None, 1)

        def unit(at, n):
            return At(at.it, at.half + n // STEPS), n % STEPS

        def taken(at, names, n):
            per = sum(w in names for _, (w, _) in TURNS)
            return at(per, sum(w in names for _, (w, _) in TURNS[:n + 1]), per)

        def index(name, u):
            return [w for _, w in TURNS].index((name, u))

        def count_copies(eng, at, n):
            at, n = unit(at, n)
            if n in PT_ON_ACT:
                eng.wait_ge(s_pt_act, at(len(PT_ON_ACT), sum(m <= n for m in PT_ON_ACT)))
            else:
                eng.wait_ge(s_pt_dve, at(STEPS - len(PT_ON_ACT), sum(m <= n for m in range(STEPS) if m not in PT_ON_ACT)))

        @block.sync
        def _(sp):
            sp.dma_start(rot[:], rope).then_inc(s_tab, 16)

        @block.gpsimd
        def _(pool):
            def halves(at, u):
                for w, (g0, g1) in enumerate(((0, 16), (16, NG))):
                    pool.wait_ge(s_work_dve, taken(at, ON_DVE, index(("q", "kv")[w], u)))
                    if w == 0 and not (at.it is None and u == 0):
                        prev = (at, index("k", 0)) if u else (At(at.it, at.half - 1), index("k", 1))
                        pool.wait_ge(s_work, prev[0](len(TURNS), prev[1] + 1, len(TURNS)))
                    base = 4 * (2 * u + w)
                    a = r1[:, g0 * 32:g1 * 32].rearrange("p (g c) -> p g c", c=32)
                    b = r2[:, g0 * 32:g1 * 32].rearrange("p (g c) -> p g c", c=32)
                    hi, lo, other = (0, 32, 64) if w == 0 else (0, 64, 32)
                    pool.tensor_tensor(parts[:, g0:g1, hi:hi + 32], a, b, ALU.add).then_inc(s_pool, 1)
                    pool.tensor_tensor(parts[:, g0:g1, other:other + 32], a, b, ALU.add).then_inc(s_pool, 1)
                    pool.tensor_tensor(a, a, b, ALU.add).then_inc(s_pool, 1)
                    pool.wait_ge(s_pool, at(16, base + 3, 16))
                    pool.tensor_tensor(parts[:, g0:g1, lo:lo + 32], a, parts[:, g0:g1, hi:hi + 32].bitcast(F32),
                                       ALU.subtract).then_inc(s_pool, 1)

            for u in range(2):
                halves(FIRST, u)
            with pool.Fori(0, NB2) as it:
                for half in range(2):
                    for u in range(2):
                        halves(At(it, half), u)

        @block.tensor
        def _(pe):
            def three(out, hi, lo, w_hi, w_lo):
                for c in range(KC):
                    cut = slice(c * P, (c + 1) * P)
                    pe.matmul(out, hi[:, cut], w_hi(c), start=(c == 0), stop=False)
                    pe.matmul(out, hi[:, cut], w_lo(c), start=False, stop=False)
                    last = pe.matmul(out, lo[:, cut], w_hi(c), start=False, stop=(c == KC - 1))
                return last

            def turn(at, n):
                name, u = TURNS[n][1]
                bank = work[:, n % 2, :]
                if not (at.it is None and n < 2):
                    prev, m = (at, n - 2) if n >= 2 else (At(at.it, at.half - 1), n - 2 + len(TURNS))
                    pe.wait_ge(s_work_act, taken(prev, ON_ACT, m))
                    pe.wait_ge(s_work_dve, taken(prev, ON_DVE, m))
                if name == "x":
                    pe.wait_ge(s_xn, at(2, u + 1, 2))
                    for c in range(KC):
                        last = pe.transpose(bank[:, c * P:(c + 1) * P], xn[:, c * P:(c + 1) * P], ident)
                elif name in ("q", "kv"):
                    if name == "q":
                        pe.wait_ge(s_work_act, taken(at, ON_ACT, index("x", u)))
                        pe.wait_ge(s_work_dve, taken(at, ON_DVE, index("x", u)))
                    a, b = (0, 512) if name == "q" else (512, QKV)
                    last = three(bank[:, 0:b - a], x_hi, x_lo, lambda c: wq_hi[:, c, a:b], lambda c: wq_lo[:, c, a:b])
                elif name in ("g0", "g1", "g2", "g3", "k"):
                    g = 4 * int(name[1]) if name != "k" else 16
                    pe.wait_ge(s_pool, at(16, 8 * u + (8 if name == "k" else 4), 16))
                    for m in range(4):
                        last = pe.transpose(bank[0:96, m * P:(m + 1) * P], parts[:, g + m, :].bitcast(F32), ident)
                elif name == "o":
                    pe.wait_ge(s_on, at(2, 1 if u else 2))
                    for c in range(KC):
                        last = pe.transpose(bank[:, c * P:(c + 1) * P], on[:, c * P:(c + 1) * P], ident)
                else:
                    pe.wait_ge(s_work_act, taken(at, ON_ACT, index("o", u)))
                    pe.wait_ge(s_work_dve, taken(at, ON_DVE, index("o", u)))
                    last = three(bank, o_hi, o_lo, lambda c: wo_hi[:, c, :], lambda c: wo_lo[:, c, :])
                last.then_inc(s_work, 1)

            def scores(at, n):
                at, n = unit(at, n)
                qt, i, m0, pairs = UNITS[n]
                keys = (qt + 1) * P
                if n == 0:
                    last = At(at.it, at.half - 1)
                    pe.wait_ge(s_work_act, taken(last, ON_ACT, NF - 1))
                    pe.wait_ge(s_work_dve, taken(last, ON_DVE, NF - 1))
                if n >= 3 or not at.first:
                    pe.wait_ge(s_prob, at(STEPS, n - 2))
                out = score[:, n % 3, :]
                for m in range(pairs):
                    w = 2 * keys
                    pe.matmul(out[:, m * w:(m + 1) * w], q_sb[:, at.buf, 4 * i + m0 + m, qt * P:(qt + 1) * P],
                              k_sb[:, at.buf, m0 + m, :, 0:keys], start=(m == 0), stop=False, skip_group_check=True)
                g = 2 * pairs
                last = pe.matmul(out.rearrange("p (g k) -> p g k", g=g)[:, :, keys - P:keys], eye[:],
                                 hide[:].rearrange("p (a k) -> p a k", a=1).broadcast_to([P, g, P]),
                                 start=False, stop=True, skip_group_check=True)
                last.then_inc(s_score, 1)

            def turn_probs(at, n):
                pe.wait_ge(s_prob, at(STEPS, n + 1))
                if n >= 2 or not at.first:
                    count_copies(pe, at, n - 2)
                for m in range(4):
                    last = pe.transpose(turned[:, n % 2, m * P:(m + 1) * P], prob[:, n % 2, m * P:(m + 1) * P], ident)
                last.then_inc(s_turned, 1)

            def mix(at, n):
                count_copies(pe, at, n)
                at, n = unit(at, n)
                qt, i, m0, pairs = UNITS[n]
                if n == 0 and not at.first:
                    pe.wait_ge(s_on, at(2, 0))
                if n == 16:
                    pe.wait_ge(s_on, at(2, 1))
                blocks = [(g, kt) for g in range(2 * pairs) for kt in range(qt + 1)]
                for m, (g, kt) in enumerate(blocks):
                    kv = 2 * m0 + g
                    head = GROUP * kv + i
                    last = pe.matmul(mixed[:, head * HD:(head + 1) * HD], probT[:, n % 2, m * P:(m + 1) * P],
                                     v_sb[:, at.buf, kt, kv * HD:(kv + 1) * HD], start=(kt == 0), stop=(kt == qt))
                last.then_inc(s_pv, 1)

            pe.wait_ge(s_eye, 1)
            for n in range(NF):
                turn(FIRST, n)
            pe.wait_ge(s_work, NF)
            for _ in TURNS[NF:]:
                pe.nop().then_inc(s_work, 1)
            def step(at, n):
                scores(at, n + 2)
                turn_probs(at, n)
                if n >= 1:
                    mix(at, n - 1)

            start = At(0, 0)
            scores(start, 0)
            scores(start, 1)
            for n in range(AHEAD):
                step(start, n)
            with pe.Fori(0, NB2) as it:
                for half in range(2):
                    at = At(it, half)
                    for n in range(AHEAD, AHEAD + STEPS):
                        step(at, n)
                        for k, (s, _) in enumerate(TURNS):
                            if s == n:
                                turn(at, k)

        @block.scalar
        def _(act):
            def turn(at, n):
                name, u = TURNS[n][1]
                if name not in ON_ACT:
                    return
                bank = work[:, n % 2, :]
                half = 1 - at.buf
                act.wait_ge(s_work, at(len(TURNS), n + 1, len(TURNS)))
                if name == "x":
                    last = act.copy(x_hi[:], bank)
                elif name == "k":
                    for g in range(2):
                        last = act.activation(k_sb[:, half, :, g, u * P:(u + 1) * P],
                                              bank[0:96, :].rearrange("p (m k) -> p m k", m=4), ACT.Copy,
                                              scale=t.cst[0:96, CP + 3 + g:CP + 4 + g])
                elif name == "o":
                    last = act.copy(o_hi[:], bank)
                else:
                    g = 4 * int(name[1])
                    last = act.copy(q_sb[:, half, g:g + 4, u * P:(u + 1) * P],
                                    bank[0:96, :].rearrange("p (m k) -> p m k", m=4))
                last.then_inc(s_work_act, 1)

            def exps(at, n):
                at, n = unit(at, n)
                qt, i, m0, pairs = UNITS[n]
                keys = (qt + 1) * P
                act.wait_ge(s_max, at(STEPS, n + 1))
                if n >= 2 or not at.first:
                    act.wait_ge(s_turned, at(STEPS, n - 1))
                if n in (0, 2) and not at.first:
                    act.wait_ge(s_inv, at(2, 0 if n else -1))
                for g in range(2 * pairs):
                    head = GROUP * (2 * m0 + g) + i
                    last = act.activation(prob[:, n % 2, g * keys:(g + 1) * keys],
                                          score[:, n % 3, g * keys:(g + 1) * keys], ACT.Exp,
                                          bias=nmax[:, n % 3, g:g + 1], accum_out=sums[:, qt, head:head + 1])
                last.then_inc(s_prob, 1)

            for n in range(NF):
                turn(FIRST, n)
            act.wait_ge(s_work_act, sum(w in ON_ACT for _, (w, _) in TURNS[:NF]))
            for _ in range(sum(w in ON_ACT for _, (w, _) in TURNS[NF:])):
                act.nop().then_inc(s_work_act, 1)
            def step(at, n):
                exps(at, n + 1)
                if n % STEPS in PT_ON_ACT:
                    act.wait_ge(s_turned, at(STEPS, n + 1))
                    if n >= 2:
                        act.wait_ge(s_pv, at(STEPS, n - 1))
                    act.copy(probT[:, n % 2, :], turned[:, n % 2, :]).then_inc(s_pt_act, 1)

            start = At(0, 0)
            exps(start, 0)
            for n in range(AHEAD):
                step(start, n)
            with act.Fori(0, NB2) as it:
                for half in range(2):
                    at = At(it, half)
                    for n in range(AHEAD, AHEAD + STEPS):
                        step(at, n)
                        for k, (s, _) in enumerate(TURNS):
                            if s == n:
                                turn(at, k)

        @block.vector
        def _(dve):
            def norm(at, u, tile):
                if not (at.it is None and u == 0):
                    prev = (at, index("x", 0)) if u else (At(at.it, at.half - 1), index("x", 1))
                    dve.wait_ge(s_work, prev[0](len(TURNS), prev[1] + 1, len(TURNS)))
                h = t.h[:, tile, :] if at.it is None else t.h[:, bass.ds(tile, 1), :].rearrange("p a d -> p (a d)")
                ln = lambda k: t.ln[:, tile, k:k + 1] if at.it is None else t.ln[:, bass.ds(tile, 1), k]
                dve.tensor_scalar(xn[:], h, ln(0), ln(1), ALU.subtract, ALU.mult).then_inc(s_xn, 1)

            def rotate(bank, u, heads, at0, kind):
                x = bank[:, 0:heads * HD].rearrange("p (h c) -> p h c", c=HD)
                r1v = r1[:, at0:at0 + heads * HD].rearrange("p (h c) -> p h c", c=HD)
                r2v = r2[:, at0:at0 + heads * HD].rearrange("p (h c) -> p h c", c=HD)
                H2 = HD // 2
                tab = lambda k, a, b: rot[:, u, k, a:b].rearrange("p (o c) -> p o c", o=1).broadcast_to([P, heads, b - a])
                dve.tensor_tensor(r1v, x, tab(2 * kind, 0, HD), ALU.mult)
                dve.tensor_tensor(r2v[:, :, 0:H2], x[:, :, H2:HD], tab(2 * kind + 1, 0, H2), ALU.mult)
                return dve.tensor_tensor(r2v[:, :, H2:HD], x[:, :, 0:H2], tab(2 * kind + 1, H2, HD), ALU.mult)

            def turn(at, n):
                name, u = TURNS[n][1]
                if name not in ON_DVE:
                    return
                bank = work[:, n % 2, :]
                half = 1 - at.buf
                if name == "x":
                    dve.wait_ge(s_work_act, taken(at, ON_ACT, n))
                    last = dve.tensor_tensor(x_lo[:], bank, x_hi[:].bitcast(F32), ALU.subtract)
                elif name in ("q", "kv"):
                    dve.wait_ge(s_work, at(len(TURNS), n + 1, len(TURNS)))
                    k = 2 * u + (name == "kv")
                    if not (at.it is None and u == 0):
                        prev = At(at.it, at.half - 1) if u == 0 else at
                        dve.wait_ge(s_pool, prev(16, 4 * ((k - 2) % 4 + 1), 16))
                    heads, at0 = (HEADS, 0) if name == "q" else (KV, 512)
                    if name == "kv":
                        dve.tensor_copy(v_sb[:, half, u, :], bank[:, KF:2 * KF])
                    last = rotate(bank, u, heads, at0, int(name == "kv"))
                elif name == "o":
                    dve.wait_ge(s_work_act, taken(at, ON_ACT, n))
                    last = dve.tensor_tensor(o_lo[:], bank, o_hi[:].bitcast(F32), ALU.subtract)
                elif name == "w":
                    dve.wait_ge(s_work, at(len(TURNS), n + 1, len(TURNS)))
                    tile = at.it * 4 + (2 * at.half + u)
                    h = t.h[:, bass.ds(tile, 1), :].rearrange("p a d -> p (a d)")
                    last = dve.tensor_tensor(h, h, bank, ALU.add)
                else:
                    dve.wait_ge(s_work, at(len(TURNS), n + 1, len(TURNS)))
                    g = 4 * int(name[1])
                    last = dve.tensor_copy(q_sb[:, half, g:g + 4, u * P:(u + 1) * P],
                                           bank[0:96, :].rearrange("p (m k) -> p m k", m=4))
                last.then_inc(s_work_dve, 1)

            def maxima(at, n):
                at, n = unit(at, n)
                qt, i, m0, pairs = UNITS[n]
                dve.wait_ge(s_score, at(STEPS, n + 1))
                g = 2 * pairs
                dve.tensor_reduce(nmax[:, n % 3, 0:g], score[:, n % 3, :].rearrange("p (g k) -> p g k", g=g), AX.X,
                                  ALU.max, negate=True).then_inc(s_max, 1)

            def normalise(at, qt):
                last_unit = 15 if qt else 23
                dve.wait_ge(s_prob, at(STEPS, last_unit + 1))
                dve.reciprocal(inv[:, qt, :], sums[:, qt, :]).then_inc(s_inv, 1)
                dve.wait_ge(s_inv, at(2, 1 if qt else 2))
                dve.wait_ge(s_pv, at(STEPS, last_unit + 1))
                prev = At(at.it, at.half - 1) if qt else at
                dve.wait_ge(s_work, prev(len(TURNS), index("o", 0 if qt else 1) + 1, len(TURNS)))
                dve.tensor_tensor(on[:].rearrange("p (h c) -> p h c", c=HD), mixed[:].rearrange("p (h c) -> p h c", c=HD),
                                  inv[:, qt, :].rearrange("p (h o) -> p h o", o=1).broadcast_to([P, HEADS, HD]),
                                  ALU.mult).then_inc(s_on, 1)

            dve.wait_ge(s_tab, 16)
            dve.tensor_copy(eye[:], ident)
            dve.tensor_scalar(hide[:], t.cst[:, CT:CT + P], MASKED, None, ALU.mult).then_inc(s_eye, 1)
            norm(FIRST, 0, 0)
            for n in range(NF):
                if TURNS[n][1] == ("x", 1):
                    norm(FIRST, 1, 1)
                turn(FIRST, n)
            dve.wait_ge(s_work_dve, sum(w in ON_DVE for _, (w, _) in TURNS[:NF]))
            for _ in range(sum(w in ON_DVE for _, (w, _) in TURNS[NF:])):
                dve.nop().then_inc(s_work_dve, 1)
            def step(at, n):
                if n % STEPS not in PT_ON_ACT:
                    dve.wait_ge(s_turned, at(STEPS, n + 1))
                    if n >= 2:
                        dve.wait_ge(s_pv, at(STEPS, n - 1))
                    dve.tensor_copy(probT[:, n % 2, :], turned[:, n % 2, :]).then_inc(s_pt_dve, 1)
                maxima(at, n + 2)

            start = At(0, 0)
            maxima(start, 0)
            maxima(start, 1)
            for n in range(AHEAD):
                step(start, n)
            with dve.Fori(0, NB2) as it:
                for half in range(2):
                    at = At(it, half)
                    tile = it * 4 + 2 * (half + 1)
                    for n in range(AHEAD, AHEAD + STEPS):
                        if n == 3:
                            norm(at, 0, tile)
                        step(at, n)
                        if n == 11:
                            norm(at, 1, tile + 1)
                        if n == 17:
                            normalise(at, 1)
                        if n == 24:
                            normalise(at, 0)
                        for k, (s, _) in enumerate(TURNS):
                            if s == n:
                                turn(at, k)


def rope_table():
    inv = (1.0 / np.power(np.float32(10000.0), np.arange(0, HD, 2, dtype=np.float32) / np.float32(HD))).astype(np.float32)
    angle = (np.arange(SEQ, dtype=np.float32)[:, None] * inv[None, :]).astype(np.float32)
    cos, sin = np.cos(angle.astype(np.float64)), np.sin(angle.astype(np.float64))
    both = np.stack([np.concatenate([cos, cos], 1), np.concatenate([-sin, sin], 1)], 1).astype(np.float32)
    full = np.concatenate([both * np.float32(HD ** -0.5), both], 1)
    return np.ascontiguousarray(full.reshape(2, P, 4, HD).transpose(1, 0, 2, 3))


def head_order():
    half = np.concatenate([np.arange(0, HD, 2), np.arange(1, HD, 2)])
    q = [(GROUP * g + i) * HD + half for i in range(GROUP) for g in range(KV)]
    k = [g * HD + half for g in range(KV)]
    return np.concatenate(q), np.concatenate(k)


EXPERTS, TOPK, KEEP = 32, 8, 0.8
INTER = 192
XROW = D + EXPERTS
TILES = TOK * TOPK // P + EXPERTS
SLOTS = TILES + 8
NOWHERE = 32768.0


def route(nc, t, gate, xrows, out):
    NH = 16
    with ExitStack() as ctx:
        sb = lambda n, s, d: ctx.enter_context(nc.sbuf_tensor(n, s, d))
        pb = lambda n, s, d: ctx.enter_context(nc.psum_tensor(n, s, d))
        sem = lambda n: ctx.enter_context(nc.semaphore(n))
        gate_sb = sb("gate_sb", [P, KC, EXPERTS], F32)
        stats = sb("r_stats", [P, NT, 6], F32)
        mean = sb("r_mean", [P, NT], F32)
        var = sb("r_var", [P, NT], F32)
        rstd = sb("r_rstd", [P, NT], F32)
        root = sb("r_root", [P, NT], F32)
        xn = sb("r_xn", [P, 2, D], F32)
        xT = sb("r_xT", [P, 2, D], F32)
        logit = sb("logit", [P, NT, EXPERTS], F32)
        prob = sb("r_prob", [P, NT, EXPERTS], F32)
        comb = sb("comb", [P, NT, EXPERTS], F32)
        col = sb("r_col", [P, 4, NT], F32)
        top = sb("top", [P, NT, TOPK], F32)
        top_at = sb("top_at", [P, NT, TOPK], mybir.dt.uint32)
        share = sb("share", [P, NT, TOPK], F32)
        active = sb("active", [P, NT, TOPK], F32)
        at_f = sb("at_f", [P, NT, TOPK], F32)
        picked = sb("picked", [P, NT, TOPK, EXPERTS], F32)
        product = sb("product", [P, NT, TOPK, EXPERTS], F32)
        member = sb("member", [P, NT, EXPERTS], F32)
        member_b = sb("member_b", [P, NT, EXPERTS], BF16)
        tri = sb("tri", [P, P], BF16)
        ones = sb("r_ones", [P, P], BF16)
        ones_f = sb("r_ones_f", [P, NT * EXPERTS], F32)
        tile_count = sb("tile_count", [P, EXPERTS, NT], F32)
        upto = sb("upto", [P, EXPERTS, NT], F32)
        e_col = sb("e_col", [P, 6, EXPERTS], F32)
        e_int = sb("e_int", [P, EXPERTS], I32)
        place = sb("place", [P, NT, EXPERTS], F32)
        slot = sb("slot", [P, NT * TOPK], F32)
        slot_i = sb("slot_i", [P, 3, NT * TOPK], I32)
        slot_f = sb("slot_f", [P, 2, NT * TOPK], F32)
        token = sb("r_token", [P, NT, TOPK], F32)
        counting = sb("counting", [P, 256], F32)
        counting_h = sb("counting_h", [P, 256], F16)
        row_hot = sb("r_row_hot", [P, NH, P], F16)
        col_hot = sb("r_col_hot", [P, NH, SLOTS], F16)
        zero = sb("r_zero", [P, SLOTS], F16)
        zero_f = sb("r_zero_f", [P, SLOTS], F32)
        held = sb("held", [P, SLOTS], F32)
        empty = sb("empty", [P, SLOTS], F32)
        n_int = sb("n_int", [EXPERTS, 2], I32)
        n_f = sb("n_f", [EXPERTS, 4], F32)
        past = sb("past", [EXPERTS, SLOTS], F32)
        served = sb("served", [EXPERTS, EXPERTS + 1], F32)

        turned = pb("r_turned", [P, 2, 512], F32)
        logit_p = pb("logit_p", [P, 512], F32)
        before_p = pb("before_p", [P, 512], F32)
        total_p = pb("total_p", [P, 512], F32)
        tiny = pb("tiny", [P, 512], F32)
        slot_p = pb("slot_p", [P, 512], F32)

        s_gate = sem("s_gate")
        s_out = sem("s_out")
        s_v = sem("r_v")
        s_var = sem("r_var")
        s_root = sem("r_root")
        s_xn = sem("r_s_xn")
        s_turned = sem("r_turned")
        s_xT = sem("r_xT")
        s_logit = sem("r_logit")
        s_rows = [sem("r_rows0"), sem("r_rows1")]
        s_shift = sem("r_shift")
        s_exp = sem("r_exp")
        s_comb = sem("r_comb")
        s_comb_out = sem("r_comb_out")
        s_member = sem("r_member")
        s_before = sem("r_before")
        s_tiles = sem("r_tiles")
        s_bound = sem("r_bound")
        s_past = sem("r_past")
        s_hot = sem("r_hot")
        s_used = sem("r_used")
        s_slots = sem("r_slots")
        s_ids = sem("r_ids")
        s_pool = sem("r_pool")
        block = ctx.enter_context(nc.Block())
        ident = t.cst[:, CI:CI + P]
        flat = lambda a: a.rearrange("p a b -> p (a b)")
        over = lambda a, n: a.rearrange("p (a o) -> p a o", o=1).broadcast_to([P, a.shape[1], n])

        @block.sync
        def _(sp):
            sp.dma_start(gate_sb[:], gate).then_inc(s_gate, 16)
            sp.dma_start(out.rearrange("(j p) d -> p j d", p=P), t.h[:, 0:NT + 1, :]).then_inc(s_out, 16)
            rows = xrows.rearrange("(j p) d -> j p d", p=P)
            with sp.Fori(0, NT // 2) as i:
                for b in range(2):
                    sp.wait_ge(s_xn, i * 2 + (b + 1))
                    sp.dma_start(rows[bass.ds(i * 2 + b, 1), :, 0:D].rearrange("a p d -> p (a d)"),
                                 xn[:, b, :]).then_inc(s_rows[b], 16)
            sp.wait_ge(s_comb, 1)
            sp.dma_start(xrows.rearrange("(j p) d -> p j d", p=P)[:, :, D:XROW], comb[:]).then_inc(s_comb_out, 16)
            sp.wait_ge(s_out, 16)
            for b in range(2):
                sp.wait_ge(s_rows[b], 16 * (NT // 2))
            sp.wait_ge(s_comb_out, 16)

        @block.gpsimd
        def _(pool):
            pool.iota(counting[:], pattern=[[1, 256]], base=0, channel_multiplier=0,
                      allow_small_or_imprecise_dtypes=True).then_inc(s_pool, 1)
            pool.iota(token[:], pattern=[[P, NT], [0, TOPK]], base=1, channel_multiplier=1,
                      allow_small_or_imprecise_dtypes=True).then_inc(s_pool, 1)

        @block.tensor
        def _(pe):
            pe.wait_ge(s_gate, 16)
            def turn(b, j):
                pe.wait_ge(s_xn, j + 1)
                for c in range(KC):
                    last = pe.transpose(turned[:, b, c * P:(c + 1) * P], xn[:, b, c * P:(c + 1) * P], ident)
                last.then_inc(s_turned, 1)

            def gates(b, j):
                pe.wait_ge(s_xT, j + 1)
                for c in range(KC):
                    last = pe.matmul(logit_p[:, bass.ds(j * EXPERTS, EXPERTS)], xT[:, b, c * P:(c + 1) * P],
                                     gate_sb[:, c, :], start=(c == 0), stop=(c == KC - 1))
                last.then_inc(s_logit, 1)

            turn(0, 0)
            with pe.Fori(0, NT // 2 - 1) as i:
                for b in range(2):
                    turn(1 - b, i * 2 + (b + 1))
                    gates(b, i * 2 + b)
            turn(1, NT - 1)
            gates(0, NT - 2)
            gates(1, NT - 1)
            pe.wait_ge(s_member, 1)
            pe.matmul(before_p[:], tri[:], flat(member_b[:]), start=True, stop=True)
            pe.matmul(total_p[:], ones[:], flat(member_b[:]), start=True, stop=True)
            for j in range(NT):
                last = pe.matmul(tiny[0:EXPERTS, 0:1], member_b[:, j, :], ones[:, 0:1], start=(j == 0), stop=(j == NT - 1))
            last.then_inc(s_before, 1)
            pe.wait_ge(s_tiles, 1)
            pe.matmul(tiny[0:EXPERTS, 8:10], t.cst[0:EXPERTS, CT:CT + EXPERTS], n_f[:, 0:2], start=True,
                      stop=True).then_inc(s_bound, 1)
            pe.wait_ge(s_past, 1)
            one = ones_f[0:EXPERTS, 0:1]
            pe.matmul(tiny[0:1, 16:16 + SLOTS], one, past[:], start=True, stop=True)
            pe.matmul(tiny[0:1, 192:192 + SLOTS], n_f[:, 0:1], past[:], start=True, stop=True)
            pe.matmul(tiny[0:1, 384:384 + EXPERTS + 1], one, served[:], start=True, stop=True)
            pe.matmul(tiny[0:1, 448:448 + EXPERTS + 1], n_f[:, 1:2], served[:], start=True, stop=True).then_inc(s_bound, 1)
            pe.matmul(slot_p[:, 0:SLOTS], zero[:, 0:P], zero[:], start=True, stop=False)
            with pe.Fori(0, NT * TOPK // NH) as i:
                for b in range(NH):
                    pe.wait_ge(s_hot, i * NH + (b + 1))
                    pe.matmul(slot_p[:, 0:SLOTS], row_hot[:, b, :], col_hot[:, b, :], start=False,
                              stop=False).then_inc(s_used, 1)
            pe.matmul(slot_p[:, 0:SLOTS], zero[:, 0:P], zero[:], start=False, stop=True).then_inc(s_slots, 1)

        @block.scalar
        def _(act):
            act.wait_ge(s_var, 1)
            act.activation(root[:], var[:], ACT.Sqrt).then_inc(s_root, 1)
            def copy_xT(b, j):
                act.wait_ge(s_turned, j + 1)
                if not isinstance(j, int):
                    act.wait_ge(s_logit, j - 1)
                act.copy(xT[:, b, :], turned[:, b, :]).then_inc(s_xT, 1)

            for b in range(2):
                copy_xT(b, b)
            with act.Fori(1, NT // 2) as i:
                for b in range(2):
                    copy_xT(b, i * 2 + b)
            act.wait_ge(s_shift, 1)
            act.activation(flat(prob[:]), flat(logit[:]), ACT.Exp).then_inc(s_exp, 1)

        @block.vector
        def _(dve):
            with dve.Fori(0, NT) as j:
                dve.bn_stats(stats[:, bass.ds(j, 1), :].rearrange("p a d -> p (a d)"),
                             t.h[:, bass.ds(j, 1), :].rearrange("p a d -> p (a d)")).then_inc(s_v, 1)
            dve.wait_ge(s_v, NT)
            moments(dve, s_v, NT, stats, mean[:], var[:], root[:])
            dve.nop().then_inc(s_var, 1)
            dve.wait_ge(s_root, 1)
            rsqrt(dve, s_v, NT + 4, rstd[:], var[:], root[:])

            def norm(b, j):
                dve.tensor_scalar(xn[:, b, :], t.h[:, bass.ds(j, 1), :].rearrange("p a d -> p (a d)"),
                                  mean[:, bass.ds(j, 1)], rstd[:, bass.ds(j, 1)], ALU.subtract,
                                  ALU.mult).then_inc(s_xn, 1)

            for b in range(2):
                norm(b, b)
            with dve.Fori(1, NT // 2) as i:
                for b in range(2):
                    dve.wait_ge(s_turned, i * 2 + (b - 1))
                    dve.wait_ge(s_rows[b], i * 16)
                    norm(b, i * 2 + b)
            count = [NT + 9]

            def link(ins):
                count[0] += 1
                ins.then_inc(s_v, 1)
                dve.wait_ge(s_v, count[0])

            dve.tensor_copy(tri[:], t.cst[:, CT:CT + P])
            dve.memset(ones[:], 1.0)
            dve.memset(ones_f[:], 1.0)
            link(dve.memset(zero_f[:], 0.0))
            dve.tensor_copy(zero[:], zero_f[:])
            dve.wait_ge(s_pool, 1)
            link(dve.tensor_copy(counting_h[:], counting[:]))
            dve.wait_ge(s_logit, NT)
            link(dve.tensor_copy(flat(logit[:]), logit_p[:]))
            link(dve.tensor_reduce(col[:, 0, :], logit[:], AX.X, ALU.max))
            dve.tensor_tensor(logit[:], logit[:], over(col[:, 0, :], EXPERTS), ALU.subtract).then_inc(s_shift, 1)
            dve.wait_ge(s_exp, 1)
            link(dve.tensor_reduce(col[:, 1, :], prob[:], AX.X, ALU.add))
            link(dve.reciprocal(col[:, 1, :], col[:, 1, :]))
            link(dve.tensor_tensor(prob[:], prob[:], over(col[:, 1, :], EXPERTS), ALU.mult))
            for j in range(NT):
                last = dve.max(top[:, j, :], prob[:, j, :])
            link(last)
            for j in range(NT):
                last = dve.max_index(top_at[:, j, :], top[:, j, :], prob[:, j, :])
            link(last)
            link(dve.tensor_reduce(col[:, 2, :], top[:], AX.X, ALU.add))
            link(dve.tensor_scalar(col[:, 2, :], col[:, 2, :], 1e-12, None, ALU.max))
            link(dve.reciprocal(col[:, 2, :], col[:, 2, :]))
            link(dve.tensor_tensor(share[:], top[:], over(col[:, 2, :], TOPK), ALU.mult))
            for k in range(1, TOPK):
                link(dve.tensor_tensor(share[:, :, k], share[:, :, k], share[:, :, k - 1], ALU.add))
            dve.memset(active[:, :, 0], 1.0)
            link(dve.tensor_scalar(active[:, :, 1:TOPK], share[:, :, 0:TOPK - 1], KEEP, None, ALU.is_lt))
            link(dve.tensor_tensor(top[:], top[:], active[:], ALU.mult))
            link(dve.tensor_reduce(col[:, 3, :], top[:], AX.X, ALU.add))
            link(dve.tensor_scalar(col[:, 3, :], col[:, 3, :], 1e-12, None, ALU.max))
            link(dve.reciprocal(col[:, 3, :], col[:, 3, :]))
            dve.tensor_copy(at_f[:], top_at[:])
            link(dve.tensor_scalar(active[:], active[:], -NOWHERE, NOWHERE, ALU.mult, ALU.add))
            link(dve.tensor_tensor(at_f[:], at_f[:], active[:], ALU.add))
            dve.wait_ge(s_pool, 2)
            link(dve.tensor_tensor(picked[:].rearrange("p j k e -> p (j k) e"),
                                   counting[:, 0:EXPERTS].rearrange("p (o e) -> p o e", o=1).broadcast_to([P, NT * TOPK, EXPERTS]),
                                   over(flat(at_f[:]), EXPERTS), ALU.is_equal))
            link(dve.tensor_reduce(member[:], picked[:].rearrange("p j k e -> p j e k"), AX.X, ALU.add))
            dve.tensor_copy(member_b[:], member[:]).then_inc(s_member, 1)
            link(dve.tensor_tensor(comb[:], prob[:], member[:], ALU.mult))
            dve.tensor_tensor(comb[:], comb[:], over(col[:, 3, :], EXPERTS), ALU.mult).then_inc(s_comb, 1)
            dve.wait_ge(s_before, 1)
            link(dve.tensor_scalar(n_int[:, 0:1], tiny[0:EXPERTS, 0:1], float(P - 1), None, ALU.add))
            link(dve.tensor_scalar(n_int[:, 1:2], n_int[:, 0:1], 7, None, ALU.arith_shift_right))
            dve.tensor_scalar(n_f[:, 0:1], n_int[:, 1:2], 0, None, ALU.is_gt)
            dve.tensor_copy(n_f[:, 1:2], n_int[:, 1:2]).then_inc(s_tiles, 1)
            link(dve.tensor_copy(tile_count[:], total_p[:].rearrange("p (j e) -> p e j", e=EXPERTS)))
            link(dve.tensor_tensor_scan(flat(upto[:]), ones_f[:], flat(tile_count[:]), 0.0, ALU.mult, ALU.add))
            dve.memset(e_col[:, 0, 0:1], 0.0)
            link(dve.tensor_copy(e_col[:, 0, 1:EXPERTS], upto[:, 0:EXPERTS - 1, NT - 1]))
            link(dve.tensor_tensor(e_col[:, 1, :], upto[:, :, NT - 1], e_col[:, 0, :], ALU.subtract))
            link(dve.tensor_scalar(e_int[:], e_col[:, 1, :], float(P - 1), None, ALU.add))
            link(dve.tensor_scalar(e_int[:], e_int[:], 7, None, ALU.arith_shift_right))
            link(dve.tensor_copy(e_col[:, 2, :], e_int[:]))
            link(dve.tensor_tensor_scan(e_col[:, 3, :], ones_f[:, 0:EXPERTS], e_col[:, 2, :], 0.0, ALU.mult, ALU.add))
            dve.memset(t.bound[:, 0:3], 0)
            link(dve.tensor_tensor(e_col[:, 4, :], e_col[:, 3, :], e_col[:, 2, :], ALU.subtract))
            link(dve.scalar_tensor_tensor(e_col[:, 4, :], e_col[:, 4, :], float(P), e_col[:, 0, :], ALU.mult, ALU.subtract))
            dve.wait_ge(s_bound, 1)
            link(dve.tensor_tensor(n_f[:, 2:4], tiny[0:EXPERTS, 8:10], n_f[:, 0:2], ALU.add))
            dve.tensor_scalar(served[:], counting[0:EXPERTS, 0:EXPERTS + 1], n_f[:, 2:3], None, ALU.is_ge)
            dve.tensor_scalar(past[:], counting[0:EXPERTS, 0:SLOTS], n_f[:, 3:4], None, ALU.is_ge).then_inc(s_past, 1)
            link(dve.tensor_tensor(upto[:], upto[:], tile_count[:], ALU.subtract))
            link(dve.tensor_tensor(upto[:], upto[:], over(e_col[:, 4, :], NT), ALU.add))
            link(dve.tensor_tensor(place[:], upto[:].rearrange("p e j -> p j e"),
                                   before_p[:].rearrange("p (j e) -> p j e", e=EXPERTS), ALU.add))
            link(dve.tensor_tensor(product[:], picked[:], place[:].rearrange("p j (o e) -> p j o e", o=1).broadcast_to(
                [P, NT, TOPK, EXPERTS]), ALU.mult))
            link(dve.tensor_reduce(slot[:].rearrange("p (j k) -> p j k", k=TOPK), product[:], AX.X, ALU.add))
            link(dve.tensor_tensor(slot_i[:, 0, :], slot[:], flat(active[:]), ALU.add))
            dve.tensor_scalar(slot_i[:, 1, :], slot_i[:, 0, :], P - 1, None, ALU.bitwise_and)
            link(dve.tensor_scalar(slot_i[:, 2, :], slot_i[:, 0, :], 7, None, ALU.arith_shift_right))
            link(dve.tensor_copy(slot_f[:], slot_i[:, 1:3, :]))
            dve.wait_ge(s_bound, 2)
            link(dve.tensor_scalar(t.tile_expert[:], tiny[0:1, 16:16 + SLOTS], float(EXPERTS - 1), None, ALU.min))
            link(dve.tensor_scalar(t.tile_turn[:], tiny[0:1, 192:192 + SLOTS], float(EXPERTS - 1), None, ALU.min))
            link(dve.tensor_scalar(t.turn_expert[:], tiny[0:1, 384:384 + EXPERTS], float(EXPERTS - 1), None, ALU.min))
            link(dve.tensor_copy(t.bound[:, 3:4 + EXPERTS], tiny[0:1, 448:449 + EXPERTS]))
            tokens = flat(token[:])
            def one_hots(b, n):
                dve.tensor_scalar(row_hot[:, b, :], counting_h[:, 0:P], slot_f[:, 0, bass.ds(n, 1)], None, ALU.is_equal)
                dve.tensor_scalar(col_hot[:, b, :], counting_h[:, 0:SLOTS], slot_f[:, 1, bass.ds(n, 1)],
                                  tokens[:, bass.ds(n, 1)], ALU.is_equal, ALU.mult).then_inc(s_hot, 1)

            for b in range(NH):
                one_hots(b, b)
            with dve.Fori(1, NT * TOPK // NH) as i:
                for b in range(NH):
                    dve.wait_ge(s_used, (i - 1) * NH + (b + 1))
                    one_hots(b, i * NH + b)
            dve.wait_ge(s_slots, 1)
            link(dve.tensor_copy(held[:], slot_p[:, 0:SLOTS]))
            dve.tensor_scalar(t.gather[:], held[:], 1.0, 0.0, ALU.subtract, ALU.max)
            link(dve.tensor_scalar(empty[:], held[:], 0.0, None, ALU.is_equal))
            link(dve.tensor_scalar(held[:], held[:], 1.0, None, ALU.subtract))
            link(dve.tensor_scalar(zero_f[:], empty[:], float(TOK + 1), None, ALU.mult))
            link(dve.tensor_tensor(held[:], held[:], zero_f[:], ALU.add))
            link(dve.tensor_scalar(empty[:], empty[:], t.cst[:, CP:CP + 1], None, ALU.mult))
            link(dve.tensor_tensor(t.scatter[:], held[:], empty[:], ALU.add))


def experts(nc, t, gate_up, down_a, down_b, xrows, out):
    NW = 4
    INNER = 4
    GU = 2 * INTER
    I2 = INTER - P
    with ExitStack() as ctx:
        sb = lambda n, s, d: ctx.enter_context(nc.sbuf_tensor(n, s, d))
        pb = lambda n, s, d: ctx.enter_context(nc.psum_tensor(n, s, d))
        sem = lambda n: ctx.enter_context(nc.semaphore(n))
        w_gu = sb("w_gu", [P, NW * KC * GU], F32)
        w_da = sb("w_da", [P, NW * D], F32)
        w_db = sb("w_db", [I2, NW * D], F32)
        x = sb("e_x", [P, 2, XROW], F32)
        read_at = sb("read_at", [P, 2], I32)
        add_at = sb("add_at", [P, 2], I32)
        weight = sb("e_weight", [P, 2], F32)
        xT = sb("e_xT", [P, 2, D], F32)
        gated = sb("gated", [P, INTER], F32)
        h = sb("e_h", [P, INTER], F32)
        hT = sb("e_hT", [P, 2, P], F32)
        y = sb("e_y", [P, 2, D], F32)
        xT_p = pb("xT_p", [P, 512], F32)
        gu_p = pb("gu_p", [P, 512], F32)
        hT_p = pb("hT_p", [P, 512], F32)
        y_p = pb("y_p", [P, 512], F32)

        s_w = [sem(f"s_w{b}") for b in range(NW)]
        s_expert = sem("s_expert")
        s_read_at = sem("s_read_at")
        s_add_at = sem("s_add_at")
        s_x = [sem("s_x0"), sem("s_x1")]
        s_pool_step = sem("s_pool_step")
        s_end = sem("s_end")
        s_xT = sem("e_s_xT")
        s_xT_sb = sem("e_xT_sb")
        s_weight = sem("e_weight_s")
        s_gu = sem("s_gu")
        s_silu = sem("s_silu")
        s_h = sem("e_s_h")
        s_hT = sem("e_s_hT")
        s_hT_sb = sem("e_hT_sb")
        s_y = sem("e_s_y")
        s_y_sb = sem("e_y_sb")
        s_added = [sem("s_added0"), sem("s_added1")]
        block = ctx.enter_context(nc.Block())
        ident = t.cst[:, CI:CI + P]

        def tiles_in_use(eng):
            return eng.value_load(t.bound[0:1, 3 + EXPERTS:4 + EXPERTS], min_val=1, max_val=TILES)

        def is_first(m):
            return isinstance(m, int)

        def steps(eng, body):
            tiles = tiles_in_use(eng)
            for b in (1, 0):
                body(0, b, 2 - b)
            with eng.Fori(0, TILES // (2 * INNER)) as outer:
                with eng.If(outer * (2 * INNER) + 2 < tiles):
                    with eng.Fori(0, INNER) as inner:
                        m = outer * INNER + inner + 1
                        with eng.If(m * 2 < tiles):
                            for b in (1, 0):
                                body(m, b, m * 2 + (2 - b))

        @block.sync
        def _(sp):
            def load(b, turn, e):
                for w, src, n in ((w_gu, gate_up, KC * GU), (w_da, down_a, D), (w_db, down_b, D)):
                    sp.dma_start(w[:, b * n:(b + 1) * n],
                                 src[bass.ds(e, 1)].rearrange("a p c -> (a p) c")).then_inc(s_w[b], 16)

            def expert(turn):
                return sp.value_load(t.turn_expert[0:1, bass.ds(turn, 1)], min_val=0, max_val=EXPERTS - 1)

            for b in range(NW):
                if b >= 2:
                    sp.wait_ge(s_w[b - 2], 48)
                    sp.nop().then_inc(s_expert, 1)
                load(b, b, expert(b))
            with sp.Fori(1, EXPERTS // NW) as m:
                for b in range(NW):
                    turn = m * NW + b
                    sp.wait_ge(s_w[(b + 2) % NW], (m + (b >= 2)) * 48)
                    sp.nop().then_inc(s_expert, 1)
                    e = expert(turn)
                    sp.wait_ge(s_y, sp.value_load(t.bound[0:1, bass.ds(turn, 1)], min_val=1, max_val=TILES))
                    load(b, turn, e)
            for b in range(2, NW):
                sp.wait_ge(s_w[b], 48 * (EXPERTS // NW))
                sp.nop().then_inc(s_expert, 1)
            rounds = (tiles_in_use(sp) + 1) >> 1
            for b in range(2):
                sp.wait_ge(s_added[b], rounds * 16)
                sp.wait_ge(s_x[b], (rounds + (2 - b)) * 16)
            sp.nop().then_inc(s_end, 1)

        @block.gpsimd
        def _(pool):
            def read(b):
                pool.indirect_dma_start(x[:, b, :], None, xrows, bass.IndirectOffsetOnAxis(ap=read_at[:, b:b + 1], axis=0),
                                        bounds_check=TOK - 1, oob_is_err=False).then_inc(s_x[b], 16)

            def add(b):
                pool.indirect_dma_start(out, bass.IndirectOffsetOnAxis(ap=add_at[:, b:b + 1], axis=0), y[:, b, :], None,
                                        bounds_check=TOK + P - 1, oob_is_err=True,
                                        compute_op=ALU.add).then_inc(s_added[b], 16)

            for n in range(3):
                pool.wait_ge(s_read_at, n + 1)
                if n == 2:
                    pool.wait_ge(s_xT, 1)
                    pool.wait_ge(s_weight, 1)
                read(n % 2)

            def body(m, b, i):
                pool.wait_ge(s_read_at, i + 3)
                pool.wait_ge(s_xT, i + 1)
                pool.wait_ge(s_weight, i + 1)
                pool.nop().then_inc(s_pool_step, 1)
                read(b)
                pool.wait_ge(s_add_at, i)
                pool.wait_ge(s_y_sb, i)
                if not (is_first(m) and b):
                    pool.wait_ge(s_added[b], (m + (1 - b)) * 16)
                pool.nop().then_inc(s_pool_step, 1)
                add(1 - b)

            steps(pool, body)

        @block.tensor
        def _(pe):
            def turn_x(b):
                for c in range(KC):
                    last = pe.transpose(xT_p[:, c * P:(c + 1) * P], x[:, b, c * P:(c + 1) * P], ident)
                last.then_inc(s_xT, 1)

            def turn_of(i):
                return pe.value_load(t.tile_turn[0:1, bass.ds(i, 1)], min_val=0, max_val=EXPERTS - 1)

            def multiply(b, turn):
                pe.wait_ge(s_expert, turn + 1)
                at = (turn & (NW - 1)) * (KC * GU)
                for c in range(KC):
                    last = pe.matmul(gu_p[:, 0:GU], xT[:, b, c * P:(c + 1) * P], w_gu[:, bass.ds(at + c * GU, GU)],
                                     start=(c == 0), stop=(c == KC - 1))
                last.then_inc(s_gu, 1)

            def turn_h():
                pe.transpose(hT_p[:, 0:P], h[:, 0:P], ident)
                pe.transpose(hT_p[0:I2, P:2 * P], h[:, P:INTER], ident).then_inc(s_hT, 1)

            pe.wait_ge(s_x[0], 16)
            turn_x(0)
            pe.wait_ge(s_xT_sb, 1)
            multiply(0, turn_of(0))
            pe.wait_ge(s_x[1], 16)
            turn_x(1)
            pe.wait_ge(s_h, 1)
            turn_h()

            def body(m, b, i):
                turn = turn_of(i)
                at = (turn_of(i - 1) & (NW - 1)) * D
                pe.wait_ge(s_xT_sb, i + 1)
                multiply(b, turn)
                pe.wait_ge(s_x[1 - b], m * 16 + 32)
                turn_x(1 - b)
                pe.wait_ge(s_hT_sb, i)
                if not (is_first(m) and b):
                    pe.wait_ge(s_y_sb, i - 1)
                pe.matmul(y_p[:], hT[:, 0, :], w_da[:, bass.ds(at, D)], start=True, stop=False)
                pe.matmul(y_p[:], hT[0:I2, 1, :], w_db[:, bass.ds(at, D)], start=False, stop=True).then_inc(s_y, 1)
                pe.wait_ge(s_h, i + 1)
                turn_h()

            steps(pe, body)

        @block.scalar
        def _(act):
            def copy_xT(b):
                act.copy(xT[:, b, :], xT_p[:]).then_inc(s_xT_sb, 1)

            def take_weight(b, i):
                e = act.value_load(t.tile_expert[0:1, bass.ds(i, 1)], min_val=0, max_val=EXPERTS - 1)
                act.copy(weight[:, b:b + 1], x[:, b, bass.ds(e + D, 1)]).then_inc(s_weight, 1)

            def gate_tile():
                act.activation(gated[:], gu_p[:, 0:INTER], ACT.Silu).then_inc(s_silu, 1)

            act.wait_ge(s_xT, 1)
            copy_xT(0)
            take_weight(0, 0)
            act.wait_ge(s_gu, 1)
            gate_tile()
            act.wait_ge(s_xT, 2)
            copy_xT(1)
            take_weight(1, 1)

            def body(m, b, i):
                act.wait_ge(s_gu, i + 1)
                act.wait_ge(s_h, i)
                gate_tile()
                act.wait_ge(s_xT, i + 2)
                copy_xT(1 - b)
                act.wait_ge(s_y, i)
                if not is_first(m):
                    act.wait_ge(s_added[1 - b], m * 16)
                act.activation(y[:, 1 - b, :], y_p[:], ACT.Copy, scale=weight[:, 1 - b:2 - b]).then_inc(s_y_sb, 1)
                act.wait_ge(s_y_sb, i)
                take_weight(1 - b, i + 1)

            steps(act, body)

        @block.vector
        def _(dve):
            def next_read(b, i):
                dve.tensor_copy(read_at[:, b:b + 1], t.gather[:, bass.ds(i, 1)]).then_inc(s_read_at, 1)

            for b in range(2):
                next_read(b, b)
            dve.wait_ge(s_x[0], 16)
            next_read(0, 2)

            def product():
                dve.tensor_tensor(h[:], gated[:], gu_p[:, INTER:GU], ALU.mult).then_inc(s_h, 1)

            def copy_hT():
                dve.tensor_copy(hT[0:I2, 1, :], hT_p[0:I2, P:2 * P])
                dve.tensor_copy(hT[:, 0, :], hT_p[:, 0:P]).then_inc(s_hT_sb, 1)

            dve.wait_ge(s_silu, 1)
            product()
            dve.wait_ge(s_hT, 1)
            copy_hT()

            def body(m, b, i):
                dve.wait_ge(s_silu, i + 1)
                dve.wait_ge(s_hT, i)
                product()
                if not is_first(m):
                    dve.wait_ge(s_added[1 - b], m * 16)
                dve.tensor_copy(add_at[:, 1 - b:2 - b], t.scatter[:, bass.ds(i - 1, 1)]).then_inc(s_add_at, 1)
                dve.wait_ge(s_x[b], (m + (2 - b)) * 16)
                next_read(b, i + 2)
                dve.wait_ge(s_hT, i + 1)
                dve.wait_ge(s_y, i)
                copy_hT()

            steps(dve, body)


def program(nc, ids, hot_ids, hot_w, cold_w, proj, wqkv, wo, gate, gate_up, down_a, down_b, cst, rope, out):
    t = Chip()
    table = nc.dram_tensor("token_table", (VOCAB, 4), I32).ap()
    xrows = nc.dram_tensor("expert_rows", (TOK, XROW), F32).ap()
    with ExitStack() as ctx:
        sb = lambda n, s, d: ctx.enter_context(nc.sbuf_tensor(n, s, d))
        t.h = sb("h", [P, NT + 2, D], F32)
        t.cst = sb("cst", [P, CST_COLS], F32)
        with ExitStack() as until_routed:
            early = lambda n, s, d: until_routed.enter_context(nc.sbuf_tensor(n, s, d))
            t.ln = early("ln", [P, NT + 2, 2], F32)
            t.wq_hi, t.wq_lo = early("wq_hi", [P, KC, QKV], F32R), early("wq_lo", [P, KC, QKV], F32R)
            t.wo_hi, t.wo_lo = early("wo_hi", [P, KC, D], F32R), early("wo_lo", [P, KC, D], F32R)
            embed(nc, t, ids, hot_ids, hot_w, cold_w, proj, wqkv, wo, cst, table)
            attend(nc, t, rope)
        t.bound = sb("bound", [1, EXPERTS + 4], I32)
        t.tile_expert = sb("tile_expert", [1, SLOTS], I32)
        t.tile_turn = sb("tile_turn", [1, SLOTS], I32)
        t.turn_expert = sb("turn_expert", [1, EXPERTS], I32)
        t.gather = sb("gather", [P, SLOTS], I32)
        t.scatter = sb("scatter", [P, SLOTS], I32)
        route(nc, t, gate, xrows, out)
        experts(nc, t, gate_up, down_a, down_b, xrows, out)


def by_partition(w):
    return w.reshape(-1, P, w.shape[-1]).transpose(1, 0, 2)


def kernel(**inputs):
    import concourse.bacc as bacc
    from concourse.bass_utils import run_bass_kernel_spmd

    given = {name: np.asarray(a) for name, a in inputs.items()}
    q_order, k_order = head_order()
    w_gu = given["L0_ffn_gate_up_proj"].transpose(0, 2, 1).reshape(EXPERTS, KC, P, 2 * INTER)
    w_down = given["L0_ffn_down_proj"].transpose(0, 2, 1)
    laid = dict(
        ids=given["x"].reshape(NT, P).T,
        hot_ids=given["L0_tok_hot_token_ids"],
        hot_w=given["L0_tok_hot_emb_w"],
        cold_w=given["L0_tok_cold_emb_w"],
        proj=given["L0_tok_proj_w"].T,
        wqkv=by_partition(np.concatenate([given["L0_attn_wq"][q_order], given["L0_attn_wk"][k_order],
                                          given["L0_attn_wv"]], 0).T),
        wo=by_partition(given["L0_attn_wo"].T),
        gate=by_partition(given["L0_ffn_gate_weight"].T),
        gate_up=w_gu.transpose(0, 2, 1, 3).reshape(EXPERTS, P, KC * 2 * INTER),
        down_a=w_down[:, :P],
        down_b=w_down[:, P:],
        constants=constants(),
        rope=rope_table(),
    )
    nc = bacc.Bacc("TRN2", target_bir_lowering=False, num_devices=1)
    arrays, args = {}, []
    for name, a in laid.items():
        arrays["in_" + name] = np.ascontiguousarray(a)
        args.append(nc.dram_tensor("in_" + name, a.shape, mybir.dt.from_np(a.dtype), kind="ExternalInput").ap())
    args.append(nc.dram_tensor("out_rows", (TOK + P, D), F32, kind="ExternalOutput").ap())
    program(nc, *args)
    r = run_bass_kernel_spmd(nc, [arrays], core_ids=[0])
    return r.results[0]["out_rows"][:TOK].reshape(BATCH, SEQ, D)
```

```python
from contextlib import ExitStack

import numpy as np
import concourse.bass as bass
from concourse import mybir

F32 = mybir.dt.float32
F32R = mybir.dt.float32r
BF16 = mybir.dt.bfloat16
F16 = mybir.dt.float16
I32 = mybir.dt.int32
ALU = mybir.AluOpType
ACT = mybir.ActivationFunctionType
AX = mybir.AxisListType

P = 128
BATCH, SEQ = 8, 256
TOK = BATCH * SEQ
NT = TOK // P
D = 512
KC = D // P
VOCAB, HOT, LATENT = 32000, 8000, 128
COLD = VOCAB - HOT
VR, VC = 125, 256
HR, HC = 125, 64
HOT_UNIT = 8192.0
EPS = 1e-5

CI, CT, CN, CP = 0, 128, 256, 512
CST_COLS = CP + 5


def constants():
    c = np.zeros((P, CST_COLS), np.float32)
    p = np.arange(P)
    c[:, CI:CI + P] = np.eye(P)
    c[:, CT:CT + P] = p[:, None] < p[None, :]
    c[:, CN:CN + VC] = np.arange(VC)
    c[:, CP] = p
    c[:, CP + 1] = HC * (HOT_UNIT / HC + p)
    c[:, CP + 2] = VC * p
    c[:, CP + 3] = p % 32 < 16
    c[:, CP + 4] = p % 32 >= 16
    return c


class Chip:
    pass


def linker(eng, sem):
    count = [0]

    def link(ins, base=0):
        count[0] += 1
        ins.then_inc(sem, 1)
        eng.wait_ge(sem, base + count[0])

    return link


def rsqrt(dve, sem, at, out, var, root):
    y = out
    dve.reciprocal(y, root).then_inc(sem, 1)
    dve.wait_ge(sem, at + 1)
    dve.tensor_tensor(root, y, y, ALU.mult).then_inc(sem, 1)
    dve.wait_ge(sem, at + 2)
    dve.tensor_tensor(root, root, var, ALU.mult).then_inc(sem, 1)
    dve.wait_ge(sem, at + 3)
    dve.tensor_scalar(root, root, -0.5, 1.5, ALU.mult, ALU.add).then_inc(sem, 1)
    dve.wait_ge(sem, at + 4)
    dve.tensor_tensor(out, y, root, ALU.mult).then_inc(sem, 1)
    dve.wait_ge(sem, at + 5)


def moments(dve, sem, at, stats, mean, var, calc):
    dve.tensor_tensor(mean, stats[:, :, 1], stats[:, :, 4], ALU.add)
    dve.tensor_tensor(calc, stats[:, :, 1], stats[:, :, 4], ALU.subtract).then_inc(sem, 1)
    dve.wait_ge(sem, at + 1)
    dve.tensor_scalar(mean, mean, 0.5, None, ALU.mult)
    dve.scalar_tensor_tensor(calc, calc, 0.25, calc, ALU.mult, ALU.mult)
    dve.tensor_tensor(var, stats[:, :, 2], stats[:, :, 5], ALU.add).then_inc(sem, 1)
    dve.wait_ge(sem, at + 2)
    dve.scalar_tensor_tensor(calc, var, 1.0 / D, calc, ALU.mult, ALU.add).then_inc(sem, 1)
    dve.wait_ge(sem, at + 3)
    dve.tensor_scalar(var, calc, EPS, None, ALU.add).then_inc(sem, 1)
    dve.wait_ge(sem, at + 4)


def embed(nc, t, ids, hot_ids, hot_w, cold_w, proj, wqkv, wo, cst, table):
    NB = 4
    NH = 16
    with ExitStack() as ctx:
        sb = lambda n, s, d: ctx.enter_context(nc.sbuf_tensor(n, s, d))
        pb = lambda n, s, d: ctx.enter_context(nc.psum_tensor(n, s, d))
        sem = lambda n: ctx.enter_context(nc.semaphore(n))
        tok = sb("tok", [P, NT], I32)
        tok_neg = sb("tok_neg", [P, NT], I32)
        tokf = sb("tokf", [P, NT], F32)
        hid = sb("hid", [HR, HC], I32)
        hneg = sb("hneg", [HR, HC], I32)
        hi = sb("hi", [HR, 2, HC], I32)
        hf = sb("hf", [HR, 2, HC], F32)
        count_row = sb("count_row", [P, VC], BF16)
        row_hot = sb("row_hot", [HR, HC, VR], BF16)
        col_hot = sb("col_hot", [HR, NH, 2, VC], BF16)
        zero = sb("zero", [HR, VC], BF16)
        ones = sb("ones", [P, VC], F32)
        hits = sb("hits", [VR, VC], F32)
        is_hot = sb("is_hot", [VR, VC], F32)
        run = sb("run", [VR, VC], F32)
        calc = sb("calc", [VR, VC], F32)
        side = sb("side", [VR, 4], F32)
        flag = sb("flag", [1, 1], I32)
        rows = sb("rows", [VR, VC, 4], I32)
        look = sb("look", [P, NT, 4], I32)
        hot_at = sb("hot_at", [P, NT], I32)
        cold = sb("cold", [P, NT], I32)
        lat = sb("lat", [P, NB, LATENT], F32)
        row = sb("row", [P, NB, D], F32)
        stats = sb("stats", [P, NT, 6], F32)
        take = sb("take", [P, NB], I32)
        ln_calc = sb("ln_calc", [P, 2, NT], F32)
        latT = sb("latT", [P, 2, P], F32)
        pj = sb("proj_sb", [P, D], F32)
        all_i = sb("all_i", [P, HOT], I32)
        all_f = sb("all_f", [P, HOT], F32)
        order = t.h[:, 0:NT, :].rearrange("p a d -> p (a d)")[:, 0:HOT]
        raw = sb("w_raw", [P, 2, QKV], F32)
        best = sb("best", [P, 2], F32)

        count = pb("count", [P, 512], F32)
        small = pb("small", [P, 512], F32)
        turned = pb("turned", [P, 2, 512], F32)
        projected = pb("projected", [P, 2, 512], F32)

        s_ids = sem("s_ids")
        s_hid = sem("s_hid")
        s_cst = sem("s_cst")
        s_pj = sem("s_pj")
        s_v = sem("s_v")
        s_onehot = sem("s_onehot")
        s_hf = sem("s_hf")
        s_far = sem("s_far")
        s_abs = sem("s_abs")
        s_row_hot = sem("s_row_hot")
        s_counted = sem("s_counted")
        s_total = sem("s_total")
        s_scan = sem("s_scan")
        s_inputs = sem("s_inputs")
        s_prefix = sem("s_prefix")
        s_rows = sem("s_rows")
        s_flag = sem("s_flag")
        s_tok = sem("s_tok")
        s_table = sem("s_table")
        s_raw = [sem("s_raw0"), sem("s_raw1")]
        s_split_hi = sem("s_split_hi")
        s_split = sem("s_split")
        s_look = sem("s_look")
        s_index = sem("s_index")
        s_hot = [sem(f"s_hot{b}") for b in range(NB)]
        s_lat = [sem(f"s_lat{b}") for b in range(NB)]
        s_turned = sem("s_turned")
        s_latT = sem("s_latT")
        s_proj = sem("s_proj")
        s_token = sem("s_token")
        s_all = sem("s_all")
        s_done = sem("s_done")
        s_kept = sem("s_kept")
        s_take = sem("s_take")
        s_stat = sem("s_stat")
        s_var = sem("s_var")
        s_sqrt = sem("s_sqrt")
        block = ctx.enter_context(nc.Block())

        iota = t.cst[:, CN:CN + VC]

        @block.sync
        def _(sp):
            sp.dma_start(hid[:], hot_ids.rearrange("(p c) -> p c", c=HC)).then_inc(s_hid, 16)
            sp.dma_start(t.cst[:], cst).then_inc(s_cst, 16)
            sp.dma_start(tok[:], ids).then_inc(s_ids, 16)
            sp.dma_start(pj[:], proj).then_inc(s_pj, 16)
            sp.wait_ge(s_rows, 1)
            sp.dma_start(table.rearrange("(p c) k -> p c k", c=VC), rows[:]).then_inc(s_table, 16)
            sp.wait_ge(s_flag, 1)
            twice = sp.value_load(flag[0:1, 0:1], min_val=0, max_val=1)
            with sp.If(twice > 0):
                sp.dma_start(all_i[:], hot_ids.rearrange("(a c) -> a c", a=1).broadcast_to([P, HOT])).then_inc(s_all, 16)
            sp.wait_ge(s_table, 16)

        def is_first(j):
            return isinstance(j, int) and j < 2

        chunks = ([(wqkv[:, c, :], t.wq_hi[:, c, :], t.wq_lo[:, c, :], QKV) for c in range(KC)]
                  + [(wo[:, c, :], t.wo_hi[:, c, :], t.wo_lo[:, c, :], D) for c in range(KC)])

        @block.gpsimd
        def _(pool):
            pool.wait_ge(s_hf, 1)
            for g in range(HC // NH):
                cut = slice(g * NH, (g + 1) * NH)
                pool.tensor_tensor(row_hot[:, cut, :],
                                   count_row[0:HR, 0:VR].rearrange("p (o c) -> p o c", o=1).broadcast_to([HR, NH, VR]),
                                   hf[:, 0, cut].rearrange("p (c o) -> p c o", o=1).broadcast_to([HR, NH, VR]),
                                   ALU.subtract).then_inc(s_far, 1)
            for n, (_, hi, lo, w) in enumerate(chunks):
                pool.wait_ge(s_split_hi, n + 1)
                pool.tensor_tensor(lo, raw[:, n % 2, 0:w], hi.bitcast(F32), ALU.subtract).then_inc(s_split, 1)
            pool.wait_ge(s_table, 16)
            pool.wait_ge(s_tok, 1)
            for j in range(NT):
                pool.indirect_dma_start(look[:, j, :], None, table, bass.IndirectOffsetOnAxis(ap=tok[:, j:j + 1], axis=0),
                                        bounds_check=VOCAB - 1, oob_is_err=False).then_inc(s_look, 16)
            pool.wait_ge(s_index, 1)
            for j in range(NT):
                b, k = j % NB, j // NB
                if k:
                    pool.wait_ge(s_hot[b], 16 * k)
                    pool.wait_ge(s_turned, NB * (k - 1) + b + 1)
                    pool.wait_ge(s_kept, NB * (k - 1) + b + 1)
                    pool.wait_ge(s_stat, NB * (k - 1) + b + 1)
                pool.indirect_dma_start(lat[:, b, :], None, cold_w, bass.IndirectOffsetOnAxis(ap=cold[:, j:j + 1], axis=0),
                                        bounds_check=COLD - 1, oob_is_err=False).then_inc(s_lat[b], 16)
                pool.indirect_dma_start(row[:, b, :], None, hot_w, bass.IndirectOffsetOnAxis(ap=hot_at[:, j:j + 1], axis=0),
                                        bounds_check=HOT - 1, oob_is_err=False).then_inc(s_hot[b], 16)

        @block.tensor
        def _(pe):
            pe.wait_ge(s_v, 1)
            pe.matmul(count[0:VR, 0:VC], zero[:, 0:VR], zero[:], start=True, stop=False)
            with pe.Fori(0, HC // NH) as i:
                pe.wait_ge(s_row_hot, i + 1)
                for b in range(NH):
                    pe.wait_ge(s_onehot, i * NH + (b + 1))
                    rows_of = row_hot[:, bass.ds(i * NH + b, 1), :].rearrange("p a c -> p (a c)")
                    pe.matmul(count[0:VR, 0:VC], rows_of, col_hot[:, b, 0, :], start=False, stop=False)
                    pe.matmul(count[0:VR, 0:VC], rows_of, col_hot[:, b, 1, :], start=False,
                              stop=False).then_inc(s_counted, 1)
            pe.matmul(count[0:VR, 0:VC], zero[:, 0:VR], zero[:], start=False, stop=True).then_inc(s_total, 1)
            pe.wait_ge(s_scan, 1)
            pe.matmul(small[0:VR, 0:1], t.cst[0:VR, CT:CT + VR], run[:, VC - 1:VC], start=True, stop=True)
            pe.matmul(small[0:1, 1:2], ones[0:VR, 0:1], side[:, 1:2], start=True, stop=True).then_inc(s_prefix, 1)
            pe.wait_ge(s_pj, 16)

            def turn(b, j, landed):
                pe.wait_ge(s_lat[b], landed)
                if not is_first(j):
                    pe.wait_ge(s_latT, j - 1)
                pe.transpose(turned[:, b % 2, 0:P], lat[:, b, :], t.cst[:, CI:CI + P]).then_inc(s_turned, 1)

            def project(b, j):
                pe.wait_ge(s_latT, j + 1)
                if not is_first(j):
                    pe.wait_ge(s_token, j - 1)
                pe.matmul(projected[:, b % 2, :], latT[:, b % 2, :], pj[:], start=True, stop=True).then_inc(s_proj, 1)

            turn(0, 0, 16)
            for b in range(NB):
                if b + 1 < NB:
                    turn(b + 1, b + 1, 16)
                    project(b, b)
            with pe.Fori(1, NT // NB) as i:
                for b in range(NB):
                    turn(b, i * NB + b, i * 16 + 16)
                    project((b - 1) % NB, i * NB + (b - 1))
            project(NB - 1, NT - 1)

        @block.scalar
        def _(act):
            def load(n):
                act.dma_start(raw[:, n % 2, 0:chunks[n][3]], chunks[n][0]).then_inc(s_raw[n % 2], 16)

            load(0)
            load(1)
            for g in range(HC // NH):
                part = row_hot[:, g * NH:(g + 1) * NH, :].rearrange("p a b -> p (a b)")
                act.wait_ge(s_far, g + 1)
                act.activation(part, part, ACT.Abs).then_inc(s_abs, 1)
                act.wait_ge(s_abs, g + 1)
                act.activation(part, part, ACT.Relu, bias=ones[0:HR, 0:1], scale=-1.0).then_inc(s_row_hot, 1)
            for n, (_, hi, _, w) in enumerate(chunks):
                act.wait_ge(s_raw[n % 2], 16 * (n // 2 + 1))
                act.copy(hi, raw[:, n % 2, 0:w]).then_inc(s_split_hi, 1)
                if n + 2 < len(chunks):
                    act.wait_ge(s_split, n + 1)
                    load(n + 2)

            def copy_latT(b, j):
                act.wait_ge(s_turned, j + 1)
                if not is_first(j):
                    act.wait_ge(s_proj, j - 1)
                act.copy(latT[:, b % 2, :], turned[:, b % 2, 0:P]).then_inc(s_latT, 1)

            def keep(b, j):
                act.wait_ge(s_token, j + 1)
                act.copy(t.h[:, bass.ds(j, 1), :].rearrange("p a d -> p (a d)"), row[:, b, :]).then_inc(s_kept, 1)

            for b in range(NB):
                copy_latT(b, b)
                if b:
                    keep(b - 1, b - 1)
            with act.Fori(1, NT // NB) as i:
                for b in range(NB):
                    copy_latT(b, i * NB + b)
                    keep((b - 1) % NB, i * NB + (b - 1))
            keep(NB - 1, NT - 1)
            act.wait_ge(s_var, 1)
            act.activation(ln_calc[:, 0, :], ln_calc[:, 1, :], ACT.Sqrt).then_inc(s_sqrt, 1)

        @block.vector
        def _(dve):
            link = linker(dve, s_v)
            link(dve.memset(zero[:], 0.0))
            dve.memset(ones[:], 1.0).then_inc(s_done, 1)
            dve.wait_ge(s_hid, 16)
            link(dve.tensor_scalar(hneg[:], hid[:], 0, VOCAB, ALU.is_lt, ALU.mult))
            link(dve.tensor_tensor(hid[:], hid[:], hneg[:], ALU.add))
            dve.tensor_scalar(hi[:, 0, :], hid[:], 8, None, ALU.arith_shift_right).then_inc(s_done, 1)
            link(dve.tensor_scalar(hi[:, 1, :], hid[:], VC - 1, None, ALU.bitwise_and))
            dve.wait_ge(s_done, 2)
            link(dve.tensor_copy(hf[:], hi[:]))
            dve.wait_ge(s_cst, 16)
            link(dve.tensor_copy(count_row[:], iota))
            dve.nop().then_inc(s_hf, 1)
            def one_hots(b, c):
                col_id = hf[:, 1, bass.ds(c, 1)]
                dve.tensor_scalar(col_hot[:, b, 0, :], count_row[0:HR, :], col_id, t.cst[0:HR, CP + 1:CP + 2],
                                  ALU.is_equal, ALU.mult)
                dve.tensor_scalar(col_hot[:, b, 1, :], count_row[0:HR, :], col_id, t.cst[0:HR, bass.ds(c + CN, 1)],
                                  ALU.is_equal, ALU.mult).then_inc(s_onehot, 1)

            for b in range(NH):
                one_hots(b, b)
            with dve.Fori(1, HC // NH) as i:
                for b in range(NH):
                    dve.wait_ge(s_counted, (i - 1) * NH + (b + 1))
                    one_hots(b, i * NH + b)
            dve.wait_ge(s_ids, 16)
            link(dve.tensor_scalar(tok_neg[:], tok[:], 0, VOCAB, ALU.is_lt, ALU.mult))
            link(dve.tensor_tensor(tok[:], tok[:], tok_neg[:], ALU.add))
            link(dve.tensor_scalar(tok[:], tok[:], 0, VOCAB - 1, ALU.max, ALU.min))
            dve.tensor_copy(tokf[:], tok[:]).then_inc(s_tok, 1)
            dve.wait_ge(s_total, 1)
            link(dve.tensor_copy(hits[:], count[0:VR, 0:VC]))
            dve.memset(rows[:], 0).then_inc(s_done, 1)
            dve.tensor_reduce(side[:, 0:1], hits[:], AX.X, ALU.max).then_inc(s_done, 1)
            link(dve.tensor_scalar(is_hot[:], hits[:], HOT_UNIT, None, ALU.is_ge))
            dve.wait_ge(s_done, 4)
            dve.tensor_scalar(side[:, 1:2], side[:, 0:1], 2 * HOT_UNIT, None, ALU.is_ge).then_inc(s_done, 1)
            link(dve.tensor_tensor_scan(run[:], ones[0:VR, :], is_hot[:], 0.0, ALU.mult, ALU.add))
            dve.wait_ge(s_done, 5)
            dve.nop().then_inc(s_scan, 1)
            link(dve.scalar_tensor_tensor(calc[:], is_hot[:], -HOT_UNIT, hits[:], ALU.mult, ALU.add))
            link(dve.tensor_scalar(rows[:, :, 0], calc[:], float(HOT - 1), None, ALU.min))
            link(dve.scalar_tensor_tensor(calc[:], iota[0:VR, :], t.cst[0:VR, CP + 2:CP + 3], run[:], ALU.add, ALU.subtract))
            dve.wait_ge(s_prefix, 1)
            dve.tensor_scalar(flag[:], small[0:1, 1:2], 0.0, None, ALU.is_gt).then_inc(s_flag, 1)
            link(dve.tensor_copy(side[:, 2:3], small[0:VR, 0:1]))
            link(dve.tensor_scalar(calc[:], calc[:], side[:, 2:3], 0.0, ALU.subtract, ALU.max))
            link(dve.tensor_scalar(rows[:, :, 1], calc[:], float(COLD - 1), None, ALU.min))
            dve.tensor_scalar(rows[:, :, 2], is_hot[:], -1.0, 1.0, ALU.mult, ALU.add).then_inc(s_rows, 1)
            dve.wait_ge(s_look, 16 * NT)
            link(dve.tensor_copy(hot_at[:], look[:, :, 0]))
            dve.wait_ge(s_flag, 1)
            twice = dve.value_load(flag[0:1, 0:1], min_val=0, max_val=1)
            with dve.If(twice > 0):
                dve.wait_ge(s_all, 16)
                dve.memset(all_f[:], 1.0).then_inc(s_done, 1)
                dve.wait_ge(s_done, 6)
                dve.tensor_tensor_scan(order, all_f[:], all_f[:], 0.0, ALU.mult, ALU.add).then_inc(s_done, 1)
                dve.wait_ge(s_done, 7)
                dve.tensor_scalar(all_f[:], all_i[:], 0, float(VOCAB), ALU.is_lt, ALU.mult).then_inc(s_done, 1)
                dve.wait_ge(s_done, 8)
                dve.tensor_tensor(all_f[:], all_f[:], all_i[:], ALU.add).then_inc(s_done, 1)
                dve.wait_ge(s_done, 9)
                scratch = all_i[:].bitcast(F32)
                with dve.Fori(0, NT) as j:
                    dve.scalar_tensor_tensor(scratch, all_f[:], tokf[:, bass.ds(j, 1)], order, ALU.is_equal,
                                             ALU.mult).then_inc(s_done, 1)
                    dve.wait_ge(s_done, j * 3 + 10)
                    dve.tensor_reduce(best[:, 0:1], scratch, AX.X, ALU.max).then_inc(s_done, 1)
                    dve.wait_ge(s_done, j * 3 + 11)
                    dve.tensor_scalar(hot_at[:, bass.ds(j, 1)], best[:, 0:1], 1.0, 0.0, ALU.subtract,
                                      ALU.max).then_inc(s_done, 1)
                    dve.wait_ge(s_done, j * 3 + 12)
            dve.tensor_copy(cold[:], look[:, :, 1]).then_inc(s_index, 1)
            with dve.Fori(0, NT // NB) as i:
                for b in range(NB):
                    j = i * NB + b
                    dve.tensor_copy(take[:, b:b + 1], look[:, bass.ds(j, 1), 2]).then_inc(s_take, 1)
                    dve.wait_ge(s_proj, j + 1)
                    dve.wait_ge(s_hot[b], i * 16 + 16)
                    dve.wait_ge(s_take, j + 1)
                    dve.nop().then_inc(s_inputs, 1)
                    dve.copy_predicated(row[:, b, :], take[:, b:b + 1].broadcast_to([P, D]),
                                        projected[:, b % 2, :]).then_inc(s_token, 1)
                    dve.wait_ge(s_token, j + 1)
                    dve.bn_stats(stats[:, bass.ds(j, 1), :].rearrange("p a d -> p (a d)"), row[:, b, :]).then_inc(s_stat, 1)
            dve.memset(t.h[:, NT:, :], 0.0).then_inc(s_stat, 1)
            dve.wait_ge(s_stat, NT + 1)
            moments(dve, s_stat, NT + 1, stats, t.ln[:, 0:NT, 0], ln_calc[:, 1, :], ln_calc[:, 0, :])
            dve.nop().then_inc(s_var, 1)
            dve.wait_ge(s_sqrt, 1)
            rsqrt(dve, s_stat, NT + 5, t.ln[:, 0:NT, 1], ln_calc[:, 1, :], ln_calc[:, 0, :])


HEADS, KV, HD = 32, 8, 16
GROUP = HEADS // KV
QKV = (HEADS + 2 * KV) * HD
KF = KV * HD
NG = 20
MASKED = -1e30
STEPS = 24


def attention_units():
    return ([(1, i, m, 1) for i in range(GROUP) for m in range(KV // 2)]
            + [(0, i, m, 2) for i in range(GROUP) for m in (0, 2)])


UNITS = attention_units()
FRONT = [(3, "x", 0), (4, "q", 0), (5, "kv", 0), (7, "x", 1), (8, "q", 1), (9, "g0", 0), (10, "g1", 0), (11, "g2", 0),
         (11, "g3", 0), (12, "k", 0), (13, "kv", 1), (15, "g0", 1), (16, "g1", 1), (17, "g2", 1), (18, "g3", 1), (19, "k", 1)]
TURNS = [(s, (w, u)) for s, w, u in FRONT + [(21, "o", 1), (22, "w", 1), (25, "o", 0), (26, "w", 0)]]
AHEAD = 3
NF = len(FRONT)
ON_ACT = {"x", "g0", "g1", "k", "o"}
ON_DVE = {"x", "q", "kv", "g2", "g3", "o", "w"}
PT_ON_ACT = [n for n in range(STEPS) if n % 5 in (0, 3)]


def attend(nc, t, rope):
    NB2 = BATCH // 2
    with ExitStack() as ctx:
        sb = lambda n, s, d: ctx.enter_context(nc.sbuf_tensor(n, s, d))
        pb = lambda n, s, d: ctx.enter_context(nc.psum_tensor(n, s, d))
        sem = lambda n: ctx.enter_context(nc.semaphore(n))
        wq_hi, wq_lo, wo_hi, wo_lo = t.wq_hi, t.wq_lo, t.wo_hi, t.wo_lo
        rot = sb("rot", [P, 2, 4, HD], F32)
        hide = sb("hide", [P, P], BF16)
        eye = sb("eye", [P, P], BF16)
        xn = sb("xn", [P, D], F32)
        x_hi = sb("x_hi", [P, D], F32R)
        x_lo = sb("x_lo", [P, D], F32R)
        r1 = sb("r1", [P, NG * 32], F32)
        r2 = sb("r2", [P, NG * 32], F32)
        parts = sb("parts", [P, NG, 96], F32R)
        q_sb = sb("q_sb", [96, 2, 16, SEQ], F32R)
        k_sb = sb("k_sb", [96, 2, 4, 2, SEQ], F32R)
        v_sb = sb("v_sb", [P, 2, 2, KF], F32)
        nmax = sb("nmax", [P, 3, 4], F32)
        sums = sb("sums", [P, 2, HEADS], F32)
        inv = sb("inv", [P, 2, HEADS], F32)
        prob = sb("prob", [P, 2, 512], F32)
        probT = sb("probT", [P, 2, 512], F32)
        on = sb("on", [P, D], F32)
        o_hi = sb("o_hi", [P, D], F32R)
        o_lo = sb("o_lo", [P, D], F32R)

        score = pb("score", [P, 3, 512], F32)
        turned = pb("p_turned", [P, 2, 512], F32)
        mixed = pb("mixed", [P, 512], F32)
        work = pb("work", [P, 2, 512], F32)

        s_tab = sem("s_tab")
        s_eye = sem("s_eye")
        s_xn = sem("s_xn")
        s_work = sem("s_work")
        s_work_act = sem("s_work_act")
        s_work_dve = sem("s_work_dve")
        s_pool = sem("s_pool")
        s_score = sem("s_score")
        s_max = sem("s_max")
        s_prob = sem("s_prob")
        s_turned = sem("s_pturned")
        s_pt_act = sem("s_pt_act")
        s_pt_dve = sem("s_pt_dve")
        s_pv = sem("s_pv")
        s_inv = sem("s_inv")
        s_stat = sem("s_ln_stat")
        s_on = sem("s_on")
        block = ctx.enter_context(nc.Block())

        ident = t.cst[:, CI:CI + P]

        class At:

            def __init__(self, it, half):
                self.it, self.half = it, half
                self.first = it is None or (isinstance(it, int) and it + half == 0)
                self.buf = half % 2

            def __call__(self, per_batch, k, before=0):
                if self.it is None:
                    return k
                return self.it * (2 * per_batch) + (before + self.half * per_batch + k)

        FIRST = At(None, 1)
        LOOPS = NB2 - 1
        LAST = [At(NB2 - 1, 0), At(NB2 - 1, 1)]

        def unit(at, n):
            return At(at.it, at.half + n // STEPS), n % STEPS

        def taken(at, names, n):
            per = sum(w in names for _, (w, _) in TURNS)
            return at(per, sum(w in names for _, (w, _) in TURNS[:n + 1]), per)

        def index(name, u):
            return [w for _, w in TURNS].index((name, u))

        def count_copies(eng, at, n):
            at, n = unit(at, n)
            if n in PT_ON_ACT:
                eng.wait_ge(s_pt_act, at(len(PT_ON_ACT), sum(m <= n for m in PT_ON_ACT)))
            else:
                eng.wait_ge(s_pt_dve, at(STEPS - len(PT_ON_ACT), sum(m <= n for m in range(STEPS) if m not in PT_ON_ACT)))

        @block.sync
        def _(sp):
            sp.dma_start(rot[:], rope).then_inc(s_tab, 16)

        @block.gpsimd
        def _(pool):
            def halves(at, u):
                for w, (g0, g1) in enumerate(((0, 16), (16, NG))):
                    pool.wait_ge(s_work_dve, taken(at, ON_DVE, index(("q", "kv")[w], u)))
                    if w == 0 and not (at.it is None and u == 0):
                        prev = (at, index("k", 0)) if u else (At(at.it, at.half - 1), index("k", 1))
                        pool.wait_ge(s_work, prev[0](len(TURNS), prev[1] + 1, len(TURNS)))
                    base = 4 * (2 * u + w)
                    a = r1[:, g0 * 32:g1 * 32].rearrange("p (g c) -> p g c", c=32)
                    b = r2[:, g0 * 32:g1 * 32].rearrange("p (g c) -> p g c", c=32)
                    hi, lo, other = (0, 32, 64) if w == 0 else (0, 64, 32)
                    pool.tensor_tensor(parts[:, g0:g1, hi:hi + 32], a, b, ALU.add).then_inc(s_pool, 1)
                    pool.tensor_tensor(parts[:, g0:g1, other:other + 32], a, b, ALU.add).then_inc(s_pool, 1)
                    pool.tensor_tensor(a, a, b, ALU.add).then_inc(s_pool, 1)
                    pool.wait_ge(s_pool, at(16, base + 3, 16))
                    pool.tensor_tensor(parts[:, g0:g1, lo:lo + 32], a, parts[:, g0:g1, hi:hi + 32].bitcast(F32),
                                       ALU.subtract).then_inc(s_pool, 1)

            for u in range(2):
                halves(FIRST, u)
            with pool.Fori(0, LOOPS) as it:
                for half in range(2):
                    for u in range(2):
                        halves(At(it, half), u)
            for u in range(2):
                halves(LAST[0], u)

        @block.tensor
        def _(pe):
            def three(out, hi, lo, w_hi, w_lo):
                for c in range(KC):
                    cut = slice(c * P, (c + 1) * P)
                    pe.matmul(out, hi[:, cut], w_hi(c), start=(c == 0), stop=False)
                    pe.matmul(out, hi[:, cut], w_lo(c), start=False, stop=False)
                    last = pe.matmul(out, lo[:, cut], w_hi(c), start=False, stop=(c == KC - 1))
                return last

            def turn(at, n):
                name, u = TURNS[n][1]
                bank = work[:, n % 2, :]
                if not (at.it is None and n < 2):
                    prev, m = (at, n - 2) if n >= 2 else (At(at.it, at.half - 1), n - 2 + len(TURNS))
                    pe.wait_ge(s_work_act, taken(prev, ON_ACT, m))
                    pe.wait_ge(s_work_dve, taken(prev, ON_DVE, m))
                if name == "x":
                    pe.wait_ge(s_xn, at(2, u + 1, 2))
                    for c in range(KC):
                        last = pe.transpose(bank[:, c * P:(c + 1) * P], xn[:, c * P:(c + 1) * P], ident)
                elif name in ("q", "kv"):
                    if name == "q":
                        pe.wait_ge(s_work_act, taken(at, ON_ACT, index("x", u)))
                        pe.wait_ge(s_work_dve, taken(at, ON_DVE, index("x", u)))
                    a, b = (0, 512) if name == "q" else (512, QKV)
                    last = three(bank[:, 0:b - a], x_hi, x_lo, lambda c: wq_hi[:, c, a:b], lambda c: wq_lo[:, c, a:b])
                elif name in ("g0", "g1", "g2", "g3", "k"):
                    g = 4 * int(name[1]) if name != "k" else 16
                    pe.wait_ge(s_pool, at(16, 8 * u + (8 if name == "k" else 4), 16))
                    for m in range(4):
                        last = pe.transpose(bank[0:96, m * P:(m + 1) * P], parts[:, g + m, :].bitcast(F32), ident)
                elif name == "o":
                    pe.wait_ge(s_on, at(2, 1 if u else 2))
                    for c in range(KC):
                        last = pe.transpose(bank[:, c * P:(c + 1) * P], on[:, c * P:(c + 1) * P], ident)
                else:
                    pe.wait_ge(s_work_act, taken(at, ON_ACT, index("o", u)))
                    pe.wait_ge(s_work_dve, taken(at, ON_DVE, index("o", u)))
                    last = three(bank, o_hi, o_lo, lambda c: wo_hi[:, c, :], lambda c: wo_lo[:, c, :])
                last.then_inc(s_work, 1)

            def scores(at, n):
                at, n = unit(at, n)
                qt, i, m0, pairs = UNITS[n]
                keys = (qt + 1) * P
                if n == 0:
                    last = At(at.it, at.half - 1)
                    pe.wait_ge(s_work_act, taken(last, ON_ACT, NF - 1))
                    pe.wait_ge(s_work_dve, taken(last, ON_DVE, NF - 1))
                if n >= 3 or not at.first:
                    pe.wait_ge(s_prob, at(STEPS, n - 2))
                out = score[:, n % 3, :]
                for m in range(pairs):
                    w = 2 * keys
                    pe.matmul(out[:, m * w:(m + 1) * w], q_sb[:, at.buf, 4 * i + m0 + m, qt * P:(qt + 1) * P],
                              k_sb[:, at.buf, m0 + m, :, 0:keys], start=(m == 0), stop=False, skip_group_check=True)
                g = 2 * pairs
                last = pe.matmul(out.rearrange("p (g k) -> p g k", g=g)[:, :, keys - P:keys], eye[:],
                                 hide[:].rearrange("p (a k) -> p a k", a=1).broadcast_to([P, g, P]),
                                 start=False, stop=True, skip_group_check=True)
                last.then_inc(s_score, 1)

            def turn_probs(at, n):
                pe.wait_ge(s_prob, at(STEPS, n + 1))
                if n >= 2 or not at.first:
                    count_copies(pe, at, n - 2)
                for m in range(4):
                    last = pe.transpose(turned[:, n % 2, m * P:(m + 1) * P], prob[:, n % 2, m * P:(m + 1) * P], ident)
                last.then_inc(s_turned, 1)

            def mix(at, n):
                count_copies(pe, at, n)
                at, n = unit(at, n)
                qt, i, m0, pairs = UNITS[n]
                if n == 0 and not at.first:
                    pe.wait_ge(s_on, at(2, 0))
                if n == 16:
                    pe.wait_ge(s_on, at(2, 1))
                blocks = [(g, kt) for g in range(2 * pairs) for kt in range(qt + 1)]
                for m, (g, kt) in enumerate(blocks):
                    kv = 2 * m0 + g
                    head = GROUP * kv + i
                    last = pe.matmul(mixed[:, head * HD:(head + 1) * HD], probT[:, n % 2, m * P:(m + 1) * P],
                                     v_sb[:, at.buf, kt, kv * HD:(kv + 1) * HD], start=(kt == 0), stop=(kt == qt))
                last.then_inc(s_pv, 1)

            pe.wait_ge(s_eye, 1)
            for n in range(NF):
                turn(FIRST, n)
            pe.wait_ge(s_work, NF)
            pe.nop().then_inc(s_work, len(TURNS) - NF)
            def step(at, n):
                scores(at, n + 2)
                turn_probs(at, n)
                if n >= 1:
                    mix(at, n - 1)

            start = At(0, 0)
            scores(start, 0)
            scores(start, 1)
            for n in range(AHEAD):
                step(start, n)

            def batch(at):
                for n in range(AHEAD, AHEAD + STEPS):
                    step(at, n)
                    for k, (s, _) in enumerate(TURNS):
                        if s == n:
                            turn(at, k)

            with pe.Fori(0, LOOPS) as it:
                for half in range(2):
                    batch(At(it, half))
            batch(LAST[0])
            at = LAST[1]
            pe.wait_ge(s_work, at(len(TURNS), 0, len(TURNS)))
            pe.nop().then_inc(s_work, NF)
            for n in range(AHEAD, STEPS + 1):
                if n + 2 < STEPS:
                    scores(at, n + 2)
                if n < STEPS:
                    turn_probs(at, n)
                mix(at, n - 1)
                for k in range(NF, NF + 2):
                    if TURNS[k][0] == n:
                        turn(at, k)
            for k in range(NF + 2, len(TURNS)):
                turn(at, k)

        @block.scalar
        def _(act):
            def turn(at, n):
                name, u = TURNS[n][1]
                if name not in ON_ACT:
                    return
                bank = work[:, n % 2, :]
                half = 1 - at.buf
                act.wait_ge(s_work, at(len(TURNS), n + 1, len(TURNS)))
                if name == "x":
                    last = act.copy(x_hi[:], bank)
                elif name == "k":
                    for g in range(2):
                        last = act.activation(k_sb[:, half, :, g, u * P:(u + 1) * P],
                                              bank[0:96, :].rearrange("p (m k) -> p m k", m=4), ACT.Copy,
                                              scale=t.cst[0:96, CP + 3 + g:CP + 4 + g])
                elif name == "o":
                    last = act.copy(o_hi[:], bank)
                else:
                    g = 4 * int(name[1])
                    last = act.copy(q_sb[:, half, g:g + 4, u * P:(u + 1) * P],
                                    bank[0:96, :].rearrange("p (m k) -> p m k", m=4))
                last.then_inc(s_work_act, 1)

            def exps(at, n):
                at, n = unit(at, n)
                qt, i, m0, pairs = UNITS[n]
                keys = (qt + 1) * P
                act.wait_ge(s_max, at(STEPS, n + 1))
                if n >= 2 or not at.first:
                    act.wait_ge(s_turned, at(STEPS, n - 1))
                if n in (0, 2) and not at.first:
                    act.wait_ge(s_inv, at(2, 0 if n else -1))
                for g in range(2 * pairs):
                    head = GROUP * (2 * m0 + g) + i
                    last = act.activation(prob[:, n % 2, g * keys:(g + 1) * keys],
                                          score[:, n % 3, g * keys:(g + 1) * keys], ACT.Exp,
                                          bias=nmax[:, n % 3, g:g + 1], accum_out=sums[:, qt, head:head + 1])
                last.then_inc(s_prob, 1)

            for n in range(NF):
                turn(FIRST, n)
            act.wait_ge(s_work_act, sum(w in ON_ACT for _, (w, _) in TURNS[:NF]))
            act.nop().then_inc(s_work_act, sum(w in ON_ACT for _, (w, _) in TURNS[NF:]))
            def copy_probs(at, n):
                act.wait_ge(s_turned, at(STEPS, n + 1))
                if n >= 2:
                    act.wait_ge(s_pv, at(STEPS, n - 1))
                act.copy(probT[:, n % 2, :], turned[:, n % 2, :]).then_inc(s_pt_act, 1)

            def step(at, n):
                exps(at, n + 1)
                if n % STEPS in PT_ON_ACT:
                    copy_probs(at, n)

            start = At(0, 0)
            exps(start, 0)
            for n in range(AHEAD):
                step(start, n)

            def batch(at):
                for n in range(AHEAD, AHEAD + STEPS):
                    step(at, n)
                    for k, (s, _) in enumerate(TURNS):
                        if s == n:
                            turn(at, k)

            with act.Fori(0, LOOPS) as it:
                for half in range(2):
                    batch(At(it, half))
            batch(LAST[0])
            at = LAST[1]
            per = sum(w in ON_ACT for _, (w, _) in TURNS)
            act.wait_ge(s_work_act, at(per, 0, per))
            act.nop().then_inc(s_work_act, sum(w in ON_ACT for _, (w, _) in TURNS[:NF]))
            for n in range(AHEAD, STEPS):
                if n + 1 < STEPS:
                    exps(at, n + 1)
                if n in PT_ON_ACT:
                    copy_probs(at, n)
                for k in range(NF, NF + 2):
                    if TURNS[k][0] == n:
                        turn(at, k)
            for k in range(NF + 2, len(TURNS)):
                turn(at, k)

        @block.vector
        def _(dve):
            def norm(at, u, tile):
                if not (at.it is None and u == 0):
                    prev = (at, index("x", 0)) if u else (At(at.it, at.half - 1), index("x", 1))
                    dve.wait_ge(s_work, prev[0](len(TURNS), prev[1] + 1, len(TURNS)))
                h = t.h[:, tile, :] if isinstance(tile, int) else t.h[:, bass.ds(tile, 1), :].rearrange("p a d -> p (a d)")
                ln = lambda k: t.ln[:, tile, k:k + 1] if isinstance(tile, int) else t.ln[:, bass.ds(tile, 1), k]
                dve.tensor_scalar(xn[:], h, ln(0), ln(1), ALU.subtract, ALU.mult).then_inc(s_xn, 1)

            def rotate(bank, u, heads, at0, kind):
                x = bank[:, 0:heads * HD].rearrange("p (h c) -> p h c", c=HD)
                r1v = r1[:, at0:at0 + heads * HD].rearrange("p (h c) -> p h c", c=HD)
                r2v = r2[:, at0:at0 + heads * HD].rearrange("p (h c) -> p h c", c=HD)
                H2 = HD // 2
                tab = lambda k, a, b: rot[:, u, k, a:b].rearrange("p (o c) -> p o c", o=1).broadcast_to([P, heads, b - a])
                dve.tensor_tensor(r1v, x, tab(2 * kind, 0, HD), ALU.mult)
                dve.tensor_tensor(r2v[:, :, 0:H2], x[:, :, H2:HD], tab(2 * kind + 1, 0, H2), ALU.mult)
                return dve.tensor_tensor(r2v[:, :, H2:HD], x[:, :, 0:H2], tab(2 * kind + 1, H2, HD), ALU.mult)

            def turn(at, n):
                name, u = TURNS[n][1]
                if name not in ON_DVE:
                    return
                bank = work[:, n % 2, :]
                half = 1 - at.buf
                if name == "x":
                    dve.wait_ge(s_work_act, taken(at, ON_ACT, n))
                    last = dve.tensor_tensor(x_lo[:], bank, x_hi[:].bitcast(F32), ALU.subtract)
                elif name in ("q", "kv"):
                    dve.wait_ge(s_work, at(len(TURNS), n + 1, len(TURNS)))
                    k = 2 * u + (name == "kv")
                    if not (at.it is None and u == 0):
                        prev = At(at.it, at.half - 1) if u == 0 else at
                        dve.wait_ge(s_pool, prev(16, 4 * ((k - 2) % 4 + 1), 16))
                    heads, at0 = (HEADS, 0) if name == "q" else (KV, 512)
                    if name == "kv":
                        dve.tensor_copy(v_sb[:, half, u, :], bank[:, KF:2 * KF])
                    last = rotate(bank, u, heads, at0, int(name == "kv"))
                elif name == "o":
                    dve.wait_ge(s_work_act, taken(at, ON_ACT, n))
                    last = dve.tensor_tensor(o_lo[:], bank, o_hi[:].bitcast(F32), ALU.subtract)
                elif name == "w":
                    dve.wait_ge(s_work, at(len(TURNS), n + 1, len(TURNS)))
                    tile = at.it * 4 + (2 * at.half + u)
                    h = t.h[:, bass.ds(tile, 1), :].rearrange("p a d -> p (a d)")
                    dve.tensor_tensor(h, h, bank, ALU.add).then_inc(s_work_dve, 1)
                    dve.wait_ge(s_work_dve, taken(at, ON_DVE, n))
                    dve.bn_stats(t.stats[:, bass.ds(tile, 1), :].rearrange("p a d -> p (a d)"), h).then_inc(s_stat, 1)
                    return
                else:
                    dve.wait_ge(s_work, at(len(TURNS), n + 1, len(TURNS)))
                    g = 4 * int(name[1])
                    last = dve.tensor_copy(q_sb[:, half, g:g + 4, u * P:(u + 1) * P],
                                           bank[0:96, :].rearrange("p (m k) -> p m k", m=4))
                last.then_inc(s_work_dve, 1)

            def maxima(at, n):
                at, n = unit(at, n)
                qt, i, m0, pairs = UNITS[n]
                dve.wait_ge(s_score, at(STEPS, n + 1))
                g = 2 * pairs
                dve.tensor_reduce(nmax[:, n % 3, 0:g], score[:, n % 3, :].rearrange("p (g k) -> p g k", g=g), AX.X,
                                  ALU.max, negate=True).then_inc(s_max, 1)

            def invert(at, qt):
                dve.wait_ge(s_prob, at(STEPS, 16 if qt else 24))
                dve.reciprocal(inv[:, qt, :], sums[:, qt, :]).then_inc(s_inv, 1)

            def normalise(at, qt):
                last_unit = 15 if qt else 23
                dve.wait_ge(s_inv, at(2, 1 if qt else 2))
                dve.wait_ge(s_pv, at(STEPS, last_unit + 1))
                prev = At(at.it, at.half - 1) if qt else at
                dve.wait_ge(s_work, prev(len(TURNS), index("o", 0 if qt else 1) + 1, len(TURNS)))
                dve.tensor_tensor(on[:].rearrange("p (h c) -> p h c", c=HD), mixed[:].rearrange("p (h c) -> p h c", c=HD),
                                  inv[:, qt, :].rearrange("p (h o) -> p h o", o=1).broadcast_to([P, HEADS, HD]),
                                  ALU.mult).then_inc(s_on, 1)

            dve.wait_ge(s_tab, 16)
            dve.tensor_copy(eye[:], ident)
            dve.tensor_scalar(hide[:], t.cst[:, CT:CT + P], MASKED, None, ALU.mult).then_inc(s_eye, 1)
            norm(FIRST, 0, 0)
            for n in range(NF):
                if TURNS[n][1] == ("x", 1):
                    norm(FIRST, 1, 1)
                turn(FIRST, n)
            dve.wait_ge(s_work_dve, sum(w in ON_DVE for _, (w, _) in TURNS[:NF]))
            dve.nop().then_inc(s_work_dve, sum(w in ON_DVE for _, (w, _) in TURNS[NF:]))
            def copy_probs(at, n):
                dve.wait_ge(s_turned, at(STEPS, n + 1))
                if n >= 2:
                    dve.wait_ge(s_pv, at(STEPS, n - 1))
                dve.tensor_copy(probT[:, n % 2, :], turned[:, n % 2, :]).then_inc(s_pt_dve, 1)

            def step(at, n):
                if n % STEPS not in PT_ON_ACT:
                    copy_probs(at, n)
                maxima(at, n + 2)

            start = At(0, 0)
            maxima(start, 0)
            maxima(start, 1)
            for n in range(AHEAD):
                step(start, n)

            def batch(at):
                tile = at.it * 4 + 2 * (at.half + 1)
                for n in range(AHEAD, AHEAD + STEPS):
                    if n == 3:
                        norm(at, 0, tile)
                    if n in (16, 24):
                        invert(at, int(n == 16))
                    step(at, n)
                    if n == 6:
                        norm(at, 1, tile + 1)
                    if n in (16, 24):
                        normalise(at, int(n == 16))
                    for k, (s, _) in enumerate(TURNS):
                        if s == n:
                            turn(at, k)

            with dve.Fori(0, LOOPS) as it:
                for half in range(2):
                    batch(At(it, half))
            batch(LAST[0])
            at = LAST[1]
            per = sum(w in ON_DVE for _, (w, _) in TURNS)
            dve.wait_ge(s_work_dve, at(per, 0, per))
            dve.nop().then_inc(s_work_dve, sum(w in ON_DVE for _, (w, _) in TURNS[:NF]))
            for n in range(AHEAD, STEPS + 1):
                if n in (16, 24):
                    invert(at, int(n == 16))
                if n < STEPS and n not in PT_ON_ACT:
                    copy_probs(at, n)
                if n + 2 < STEPS:
                    maxima(at, n + 2)
                if n in (16, 24):
                    normalise(at, int(n == 16))
                for k in range(NF, NF + 2):
                    if TURNS[k][0] == n:
                        turn(at, k)
            for k in range(NF + 2, len(TURNS)):
                turn(at, k)


def rope_table():
    inv = (1.0 / np.power(np.float32(10000.0), np.arange(0, HD, 2, dtype=np.float32) / np.float32(HD))).astype(np.float32)
    angle = (np.arange(SEQ, dtype=np.float32)[:, None] * inv[None, :]).astype(np.float32)
    cos, sin = np.cos(angle.astype(np.float64)), np.sin(angle.astype(np.float64))
    both = np.stack([np.concatenate([cos, cos], 1), np.concatenate([-sin, sin], 1)], 1).astype(np.float32)
    full = np.concatenate([both * np.float32(HD ** -0.5), both], 1)
    return np.ascontiguousarray(full.reshape(2, P, 4, HD).transpose(1, 0, 2, 3))


def head_order():
    half = np.concatenate([np.arange(0, HD, 2), np.arange(1, HD, 2)])
    q = [(GROUP * g + i) * HD + half for i in range(GROUP) for g in range(KV)]
    k = [g * HD + half for g in range(KV)]
    return np.concatenate(q), np.concatenate(k)


EXPERTS, TOPK, KEEP = 32, 8, 0.8
INTER = 192
XROW = D + EXPERTS
TILES = TOK * TOPK // P + EXPERTS
SLOTS = TILES + 8
NOWHERE = 32768.0


NW = 4
GU = 2 * INTER


def turn_expert(sp, t, turn):
    return sp.value_load(t.turn_expert[0:1, bass.ds(turn, 1)], min_val=0, max_val=EXPERTS - 1)


def load_expert(sp, t, b, e, gate_up, down_a, down_b):
    for w, src, n in ((t.w_gu, gate_up, KC * GU), (t.w_da, down_a, D), (t.w_db, down_b, D)):
        sp.dma_start(w[:, b * n:(b + 1) * n], src[bass.ds(e, 1)].rearrange("a p c -> (a p) c")).then_inc(t.s_w[b], 16)


def route(nc, t, gate, gate_up, down_a, down_b, xrows, out):
    NH = 16
    GT = 4
    with ExitStack() as ctx:
        sb = lambda n, s, d: ctx.enter_context(nc.sbuf_tensor(n, s, d))
        pb = lambda n, s, d: ctx.enter_context(nc.psum_tensor(n, s, d))
        sem = lambda n: ctx.enter_context(nc.semaphore(n))
        gate_sb = sb("gate_sb", [P, KC, EXPERTS], F32)
        mean = sb("r_mean", [P, NT], F32)
        var = sb("r_var", [P, NT], F32)
        rstd = sb("r_rstd", [P, NT], F32)
        root = sb("r_root", [P, NT], F32)
        xn = sb("r_xn", [P, GT, D], F32)
        xT = sb("r_xT", [P, KC, TOK], F32)
        logitT = sb("logitT", [EXPERTS, TOK], F32)
        logit = sb("logit", [P, NT, EXPERTS], F32)
        prob = sb("r_prob", [P, NT, EXPERTS], F32)
        comb = sb("comb", [P, NT, EXPERTS], F32)
        col = sb("r_col", [P, 4, NT], F32)
        top = sb("top", [P, NT, TOPK], F32)
        top_at = sb("top_at", [P, NT, TOPK], mybir.dt.uint32)
        share = sb("share", [P, NT, TOPK], F32)
        active = sb("active", [P, NT, TOPK], F32)
        at_f = sb("at_f", [P, NT, TOPK], F32)
        after = xT[:].rearrange("p c k -> p (c k)").rearrange("p (n j k e) -> p n j k e", n=2, j=NT, k=TOPK)
        picked, product = after[:, 0], after[:, 1]
        member = sb("member", [P, NT, EXPERTS], F32)
        member_b = sb("member_b", [P, NT, EXPERTS], BF16)
        tri = sb("tri", [P, P], BF16)
        ones = sb("r_ones", [P, P], BF16)
        ones_f = sb("r_ones_f", [P, NT * EXPERTS], F32)
        tile_count = sb("tile_count", [P, EXPERTS, NT], F32)
        upto = sb("upto", [P, EXPERTS, NT], F32)
        e_col = sb("e_col", [P, 6, EXPERTS], F32)
        e_int = sb("e_int", [P, EXPERTS], I32)
        place = sb("place", [P, NT, EXPERTS], F32)
        slot = sb("slot", [P, NT * TOPK], F32)
        slot_i = sb("slot_i", [P, 3, NT * TOPK], I32)
        slot_f = sb("slot_f", [P, 2, NT * TOPK], F32)
        token = sb("r_token", [P, NT, TOPK], F32)
        counting = sb("counting", [P, 256], F32)
        counting_h = sb("counting_h", [P, 256], F16)
        row_hot = sb("r_row_hot", [P, NT * TOPK, P], F16)
        col_hot = sb("r_col_hot", [P, NH, SLOTS], F16)
        zero = sb("r_zero", [P, SLOTS], F16)
        zero_f = sb("r_zero_f", [P, SLOTS], F32)
        held = sb("held", [P, SLOTS], F32)
        empty = sb("empty", [P, SLOTS], F32)
        n_int = sb("n_int", [EXPERTS, 2], I32)
        n_f = sb("n_f", [EXPERTS, 4], F32)
        past = sb("past", [EXPERTS, SLOTS], F32)
        served = sb("served", [EXPERTS, EXPERTS + 1], F32)

        turned = pb("r_turned", [P, 2, 512], F32)
        logitT_p = pb("logitT_p", [P, 512], F32)
        logit_p = pb("logit_p", [P, 512], F32)
        before_p = pb("before_p", [P, 512], F32)
        total_p = pb("total_p", [P, 512], F32)
        tiny = pb("tiny", [P, 512], F32)
        slot_p = pb("slot_p", [P, 512], F32)

        s_gate = sem("s_gate")
        s_out = sem("s_out")
        s_v = sem("r_v")
        s_var = sem("r_var")
        s_root = sem("r_root")
        s_xn = sem("r_s_xn")
        s_turned = sem("r_turned")
        s_xT = sem("r_xT")
        s_gates = sem("r_gates")
        s_logitT = sem("r_logitT")
        s_logit = sem("r_logit")
        s_rows = [sem(f"r_rows{b}") for b in range(GT)]
        s_shift = sem("r_shift")
        s_exp = sem("r_exp")
        s_comb = sem("r_comb")
        s_comb_out = sem("r_comb_out")
        s_member = sem("r_member")
        s_before = sem("r_before")
        s_tiles = sem("r_tiles")
        s_bound = sem("r_bound")
        s_past = sem("r_past")
        s_hot = sem("r_hot")
        s_slot = sem("r_slot")
        s_turns = sem("r_turns")
        s_far = sem("r_far")
        s_abs = sem("r_abs")
        s_row_hot = sem("r_s_row_hot")
        s_used = sem("r_used")
        s_slots = sem("r_slots")
        s_pool = sem("r_pool")
        block = ctx.enter_context(nc.Block())
        ident = t.cst[:, CI:CI + P]
        flat = lambda a: a.rearrange("p a b -> p (a b)")
        over = lambda a, n: a.rearrange("p (a o) -> p a o", o=1).broadcast_to([P, a.shape[1], n])

        @block.sync
        def _(sp):
            sp.dma_start(gate_sb[:], gate).then_inc(s_gate, 16)
            rows = xrows.rearrange("(j p) d -> j p d", p=P)
            with sp.Fori(0, NT // GT) as g:
                for b in range(GT):
                    sp.wait_ge(s_xn, g * GT + (b + 1))
                    sp.dma_start(rows[bass.ds(g * GT + b, 1), :, 0:D].rearrange("a p d -> p (a d)"),
                                 xn[:, b, :]).then_inc(s_rows[b], 16)
            sp.dma_start(out.rearrange("(j p) d -> p j d", p=P), t.h[:, 0:NT + 1, :]).then_inc(s_out, 16)
            sp.wait_ge(s_comb, 1)
            sp.dma_start(xrows.rearrange("(j p) d -> p j d", p=P)[:, :, D:XROW], comb[:]).then_inc(s_comb_out, 16)
            sp.wait_ge(s_turns, 1)
            for b in range(NW):
                load_expert(sp, t, b, turn_expert(sp, t, b), gate_up, down_a, down_b)
            sp.wait_ge(s_out, 16)
            for b in range(GT):
                sp.wait_ge(s_rows[b], 16 * (NT // GT))
            sp.wait_ge(s_comb_out, 16)

        @block.gpsimd
        def _(pool):
            pool.iota(counting[:], pattern=[[1, 256]], base=0, channel_multiplier=0,
                      allow_small_or_imprecise_dtypes=True).then_inc(s_pool, 1)
            pool.iota(token[:], pattern=[[P, NT], [0, TOPK]], base=1, channel_multiplier=1,
                      allow_small_or_imprecise_dtypes=True).then_inc(s_pool, 1)
            pool.wait_ge(s_slot, 1)
            rows = counting_h[:, 0:P].rearrange("p (o c) -> p o c", o=1).broadcast_to([P, NH, P])
            for g in range(NT * TOPK // NH):
                cut = slice(g * NH, (g + 1) * NH)
                pool.tensor_tensor(row_hot[:, cut, :], rows, over(slot_f[:, 0, cut], P), ALU.subtract).then_inc(s_far, 1)


        @block.tensor
        def _(pe):
            pe.wait_ge(s_gate, 16)
            def turn(b, j):
                pe.wait_ge(s_xn, j + 1)
                if not (isinstance(j, int) and j < 2):
                    pe.wait_ge(s_xT, j - 1)
                for c in range(KC):
                    last = pe.transpose(turned[:, b % 2, c * P:(c + 1) * P], xn[:, b, c * P:(c + 1) * P], ident)
                last.then_inc(s_turned, 1)

            def gates(g):
                pe.wait_ge(s_xT, g * GT + GT)
                if not (isinstance(g, int) and g == 0):
                    pe.wait_ge(s_logitT, g)
                for c in range(KC):
                    last = pe.matmul(logitT_p[0:EXPERTS, :], gate_sb[:, c, :], xT[:, c, bass.ds(g * (GT * P), GT * P)],
                                     start=(c == 0), stop=(c == KC - 1))
                last.then_inc(s_gates, 1)

            for b in range(GT):
                turn(b, b)
            with pe.Fori(1, NT // GT) as g:
                for b in range(GT):
                    turn(b, g * GT + b)
                    if b == 0:
                        gates(g - 1)
            gates(NT // GT - 1)
            pe.wait_ge(s_logitT, NT // GT)
            for j in range(NT):
                last = pe.transpose(logit_p[:, j * EXPERTS:(j + 1) * EXPERTS], logitT[:, j * P:(j + 1) * P],
                                    t.cst[0:EXPERTS, CI:CI + EXPERTS])
            last.then_inc(s_logit, 1)
            pe.wait_ge(s_member, 1)
            pe.matmul(before_p[:], tri[:], flat(member_b[:]), start=True, stop=True)
            pe.matmul(total_p[:], ones[:], flat(member_b[:]), start=True, stop=True)
            for j in range(NT):
                last = pe.matmul(tiny[0:EXPERTS, 0:1], member_b[:, j, :], ones[:, 0:1], start=(j == 0), stop=(j == NT - 1))
            last.then_inc(s_before, 1)
            pe.wait_ge(s_tiles, 1)
            pe.matmul(tiny[0:EXPERTS, 8:10], t.cst[0:EXPERTS, CT:CT + EXPERTS], n_f[:, 0:2], start=True,
                      stop=True).then_inc(s_bound, 1)
            pe.wait_ge(s_past, 1)
            one = ones_f[0:EXPERTS, 0:1]
            pe.matmul(tiny[0:1, 16:16 + SLOTS], one, past[:], start=True, stop=True)
            pe.matmul(tiny[0:1, 192:192 + SLOTS], n_f[:, 0:1], past[:], start=True, stop=True)
            pe.matmul(tiny[0:1, 384:384 + EXPERTS + 1], one, served[:], start=True, stop=True)
            pe.matmul(tiny[0:1, 448:448 + EXPERTS + 1], n_f[:, 1:2], served[:], start=True, stop=True).then_inc(s_bound, 1)
            pe.matmul(slot_p[:, 0:SLOTS], zero[:, 0:P], zero[:], start=True, stop=False)
            with pe.Fori(0, NT * TOPK // NH) as i:
                pe.wait_ge(s_row_hot, i + 1)
                for b in range(NH):
                    pe.wait_ge(s_hot, i * NH + (b + 1))
                    pe.matmul(slot_p[:, 0:SLOTS], row_hot[:, bass.ds(i * NH + b, 1), :].rearrange("p a c -> p (a c)"),
                              col_hot[:, b, :], start=False,
                              stop=False).then_inc(s_used, 1)
            pe.matmul(slot_p[:, 0:SLOTS], zero[:, 0:P], zero[:], start=False, stop=True).then_inc(s_slots, 1)

        @block.scalar
        def _(act):
            act.wait_ge(s_var, 1)
            act.activation(root[:], var[:], ACT.Sqrt).then_inc(s_root, 1)
            def copy_xT(b, j):
                act.wait_ge(s_turned, j + 1)
                act.copy(xT[:, :, bass.ds(j * P, P)], turned[:, b, :].rearrange("p (c k) -> p c k", c=KC)).then_inc(s_xT, 1)

            def copy_logitT(g):
                act.wait_ge(s_gates, g + 1)
                act.copy(logitT[:, bass.ds(g * (GT * P), GT * P)], logitT_p[0:EXPERTS, :]).then_inc(s_logitT, 1)

            for b in range(GT):
                copy_xT(b % 2, b)
            with act.Fori(1, NT // GT) as g:
                for b in range(GT):
                    copy_xT(b % 2, g * GT + b)
                    if b == 0:
                        copy_logitT(g - 1)
            copy_logitT(NT // GT - 1)
            act.wait_ge(s_shift, 1)
            act.activation(flat(prob[:]), flat(logit[:]), ACT.Exp).then_inc(s_exp, 1)
            for g in range(NT * TOPK // NH):
                part = flat(row_hot[:, g * NH:(g + 1) * NH, :])
                act.wait_ge(s_far, g + 1)
                act.activation(part, part, ACT.Abs).then_inc(s_abs, 1)
                act.wait_ge(s_abs, g + 1)
                act.activation(part, part, ACT.Relu, bias=ones_f[:, 0:1], scale=-1.0).then_inc(s_row_hot, 1)

        @block.vector
        def _(dve):
            moments(dve, s_v, 0, t.stats, mean[:], var[:], root[:])
            dve.nop().then_inc(s_var, 1)
            dve.wait_ge(s_root, 1)
            rsqrt(dve, s_v, 4, rstd[:], var[:], root[:])

            def norm(b, j):
                dve.tensor_scalar(xn[:, b, :], t.h[:, bass.ds(j, 1), :].rearrange("p a d -> p (a d)"),
                                  mean[:, bass.ds(j, 1)], rstd[:, bass.ds(j, 1)], ALU.subtract,
                                  ALU.mult).then_inc(s_xn, 1)

            for b in range(GT):
                norm(b, b)
            with dve.Fori(1, NT // GT) as g:
                for b in range(GT):
                    dve.wait_ge(s_turned, g * GT + (b + 1 - GT))
                    dve.wait_ge(s_rows[b], g * 16)
                    norm(b, g * GT + b)
            count = [9]

            def link(ins):
                count[0] += 1
                ins.then_inc(s_v, 1)
                dve.wait_ge(s_v, count[0])

            dve.tensor_copy(tri[:], t.cst[:, CT:CT + P])
            dve.memset(ones[:], 1.0)
            dve.memset(ones_f[:], 1.0)
            link(dve.memset(zero_f[:], 0.0))
            dve.tensor_copy(zero[:], zero_f[:])
            dve.wait_ge(s_pool, 1)
            link(dve.tensor_copy(counting_h[:], counting[:]))
            dve.wait_ge(s_logit, 1)
            link(dve.tensor_copy(flat(logit[:]), logit_p[:]))
            link(dve.tensor_reduce(col[:, 0, :], logit[:], AX.X, ALU.max))
            dve.tensor_tensor(logit[:], logit[:], over(col[:, 0, :], EXPERTS), ALU.subtract).then_inc(s_shift, 1)
            dve.wait_ge(s_exp, 1)
            link(dve.tensor_reduce(col[:, 1, :], prob[:], AX.X, ALU.add))
            link(dve.reciprocal(col[:, 1, :], col[:, 1, :]))
            link(dve.tensor_tensor(prob[:], prob[:], over(col[:, 1, :], EXPERTS), ALU.mult))
            for j in range(NT):
                last = dve.max(top[:, j, :], prob[:, j, :])
            link(last)
            for j in range(NT):
                last = dve.max_index(top_at[:, j, :], top[:, j, :], prob[:, j, :])
            link(last)
            link(dve.tensor_reduce(col[:, 2, :], top[:], AX.X, ALU.add))
            link(dve.tensor_scalar(col[:, 2, :], col[:, 2, :], 1e-12, None, ALU.max))
            link(dve.reciprocal(col[:, 2, :], col[:, 2, :]))
            link(dve.tensor_tensor(share[:], top[:], over(col[:, 2, :], TOPK), ALU.mult))
            for k in range(1, TOPK):
                link(dve.tensor_tensor(share[:, :, k], share[:, :, k], share[:, :, k - 1], ALU.add))
            dve.memset(active[:, :, 0], 1.0)
            link(dve.tensor_scalar(active[:, :, 1:TOPK], share[:, :, 0:TOPK - 1], KEEP, None, ALU.is_lt))
            link(dve.tensor_tensor(top[:], top[:], active[:], ALU.mult))
            link(dve.tensor_reduce(col[:, 3, :], top[:], AX.X, ALU.add))
            link(dve.tensor_scalar(col[:, 3, :], col[:, 3, :], 1e-12, None, ALU.max))
            link(dve.reciprocal(col[:, 3, :], col[:, 3, :]))
            dve.tensor_copy(at_f[:], top_at[:])
            link(dve.tensor_scalar(active[:], active[:], -NOWHERE, NOWHERE, ALU.mult, ALU.add))
            link(dve.tensor_tensor(at_f[:], at_f[:], active[:], ALU.add))
            dve.wait_ge(s_pool, 2)
            link(dve.tensor_tensor(picked.rearrange("p j k e -> p (j k) e"),
                                   counting[:, 0:EXPERTS].rearrange("p (o e) -> p o e", o=1).broadcast_to([P, NT * TOPK, EXPERTS]),
                                   over(flat(at_f[:]), EXPERTS), ALU.is_equal))
            link(dve.tensor_reduce(member[:], picked.rearrange("p j k e -> p j e k"), AX.X, ALU.add))
            dve.tensor_copy(member_b[:], member[:]).then_inc(s_member, 1)
            link(dve.tensor_tensor(comb[:], prob[:], member[:], ALU.mult))
            dve.tensor_tensor(comb[:], comb[:], over(col[:, 3, :], EXPERTS), ALU.mult).then_inc(s_comb, 1)
            dve.wait_ge(s_before, 1)
            link(dve.tensor_scalar(n_int[:, 0:1], tiny[0:EXPERTS, 0:1], float(P - 1), None, ALU.add))
            link(dve.tensor_scalar(n_int[:, 1:2], n_int[:, 0:1], 7, None, ALU.arith_shift_right))
            dve.tensor_scalar(n_f[:, 0:1], n_int[:, 1:2], 0, None, ALU.is_gt)
            dve.tensor_copy(n_f[:, 1:2], n_int[:, 1:2]).then_inc(s_tiles, 1)
            link(dve.tensor_copy(tile_count[:], total_p[:].rearrange("p (j e) -> p e j", e=EXPERTS)))
            link(dve.tensor_tensor_scan(flat(upto[:]), ones_f[:], flat(tile_count[:]), 0.0, ALU.mult, ALU.add))
            dve.memset(e_col[:, 0, 0:1], 0.0)
            link(dve.tensor_copy(e_col[:, 0, 1:EXPERTS], upto[:, 0:EXPERTS - 1, NT - 1]))
            link(dve.tensor_tensor(e_col[:, 1, :], upto[:, :, NT - 1], e_col[:, 0, :], ALU.subtract))
            link(dve.tensor_scalar(e_int[:], e_col[:, 1, :], float(P - 1), None, ALU.add))
            link(dve.tensor_scalar(e_int[:], e_int[:], 7, None, ALU.arith_shift_right))
            link(dve.tensor_copy(e_col[:, 2, :], e_int[:]))
            link(dve.tensor_tensor_scan(e_col[:, 3, :], ones_f[:, 0:EXPERTS], e_col[:, 2, :], 0.0, ALU.mult, ALU.add))
            dve.memset(t.bound[:, 0:3], 0)
            link(dve.tensor_tensor(e_col[:, 4, :], e_col[:, 3, :], e_col[:, 2, :], ALU.subtract))
            link(dve.scalar_tensor_tensor(e_col[:, 4, :], e_col[:, 4, :], float(P), e_col[:, 0, :], ALU.mult, ALU.subtract))
            dve.wait_ge(s_bound, 1)
            link(dve.tensor_tensor(n_f[:, 2:4], tiny[0:EXPERTS, 8:10], n_f[:, 0:2], ALU.add))
            dve.tensor_scalar(served[:], counting[0:EXPERTS, 0:EXPERTS + 1], n_f[:, 2:3], None, ALU.is_ge)
            dve.tensor_scalar(past[:], counting[0:EXPERTS, 0:SLOTS], n_f[:, 3:4], None, ALU.is_ge).then_inc(s_past, 1)
            link(dve.tensor_tensor(upto[:], upto[:], tile_count[:], ALU.subtract))
            link(dve.tensor_tensor(upto[:], upto[:], over(e_col[:, 4, :], NT), ALU.add))
            link(dve.tensor_tensor(place[:], upto[:].rearrange("p e j -> p j e"),
                                   before_p[:].rearrange("p (j e) -> p j e", e=EXPERTS), ALU.add))
            link(dve.tensor_tensor(product, picked, place[:].rearrange("p j (o e) -> p j o e", o=1).broadcast_to(
                [P, NT, TOPK, EXPERTS]), ALU.mult))
            link(dve.tensor_reduce(slot[:].rearrange("p (j k) -> p j k", k=TOPK), product, AX.X, ALU.add))
            link(dve.tensor_tensor(slot_i[:, 0, :], slot[:], flat(active[:]), ALU.add))
            dve.tensor_scalar(slot_i[:, 1, :], slot_i[:, 0, :], P - 1, None, ALU.bitwise_and)
            link(dve.tensor_scalar(slot_i[:, 2, :], slot_i[:, 0, :], 7, None, ALU.arith_shift_right))
            link(dve.tensor_copy(slot_f[:], slot_i[:, 1:3, :]))
            dve.nop().then_inc(s_slot, 1)
            dve.wait_ge(s_bound, 2)
            link(dve.tensor_scalar(t.tile_expert[:], tiny[0:1, 16:16 + SLOTS], float(EXPERTS - 1), None, ALU.min))
            link(dve.tensor_scalar(t.tile_turn[:], tiny[0:1, 192:192 + SLOTS], float(EXPERTS - 1), None, ALU.min))
            link(dve.tensor_scalar(t.turn_expert[:], tiny[0:1, 384:384 + EXPERTS], float(EXPERTS - 1), None, ALU.min))
            link(dve.tensor_copy(t.bound[:, 3:4 + EXPERTS], tiny[0:1, 448:449 + EXPERTS]))
            dve.nop().then_inc(s_turns, 1)
            tokens = flat(token[:])
            def one_hots(b, n):
                dve.tensor_scalar(col_hot[:, b, :], counting_h[:, 0:SLOTS], slot_f[:, 1, bass.ds(n, 1)],
                                  tokens[:, bass.ds(n, 1)], ALU.is_equal, ALU.mult).then_inc(s_hot, 1)

            for b in range(NH):
                one_hots(b, b)
            with dve.Fori(1, NT * TOPK // NH) as i:
                for b in range(NH):
                    dve.wait_ge(s_used, (i - 1) * NH + (b + 1))
                    one_hots(b, i * NH + b)
            dve.wait_ge(s_slots, 1)
            link(dve.tensor_copy(held[:], slot_p[:, 0:SLOTS]))
            dve.tensor_scalar(t.gather[:], held[:], 1.0, 0.0, ALU.subtract, ALU.max)
            link(dve.tensor_scalar(empty[:], held[:], 0.0, None, ALU.is_equal))
            link(dve.tensor_scalar(held[:], held[:], 1.0, None, ALU.subtract))
            link(dve.tensor_scalar(zero_f[:], empty[:], float(TOK + 1), None, ALU.mult))
            link(dve.tensor_tensor(held[:], held[:], zero_f[:], ALU.add))
            link(dve.tensor_scalar(empty[:], empty[:], t.cst[:, CP:CP + 1], None, ALU.mult))
            link(dve.tensor_tensor(t.scatter[:], held[:], empty[:], ALU.add))


def experts(nc, t, gate_up, down_a, down_b, xrows, out):
    INNER = 8
    I2 = INTER - P
    with ExitStack() as ctx:
        sb = lambda n, s, d: ctx.enter_context(nc.sbuf_tensor(n, s, d))
        pb = lambda n, s, d: ctx.enter_context(nc.psum_tensor(n, s, d))
        sem = lambda n: ctx.enter_context(nc.semaphore(n))
        w_gu, w_da, w_db, s_w = t.w_gu, t.w_da, t.w_db, t.s_w
        x = sb("e_x", [P, 2, XROW], F32)
        read_at = sb("read_at", [P, 2], I32)
        add_at = sb("add_at", [P, 2], I32)
        weight = sb("e_weight", [P, 2], F32)
        xT = sb("e_xT", [P, 2, D], F32)
        gated = sb("gated", [P, INTER], F32)
        h = sb("e_h", [P, INTER], F32)
        hT = sb("e_hT", [P, 2, P], F32)
        y = sb("e_y", [P, 2, D], F32)
        xT_p = pb("xT_p", [P, 512], F32)
        gu_p = pb("gu_p", [P, 512], F32)
        hT_p = pb("hT_p", [P, 512], F32)
        y_p = pb("y_p", [P, 512], F32)

        s_expert = sem("s_expert")
        s_read_at = sem("s_read_at")
        s_add_at = sem("s_add_at")
        s_x = [sem("s_x0"), sem("s_x1")]
        s_pool_step = sem("s_pool_step")
        s_end = sem("s_end")
        s_xT = sem("e_s_xT")
        s_xT_sb = sem("e_xT_sb")
        s_weight = sem("e_weight_s")
        s_gu = sem("s_gu")
        s_silu = sem("s_silu")
        s_h = sem("e_s_h")
        s_hT = sem("e_s_hT")
        s_hT_sb = sem("e_hT_sb")
        s_y = sem("e_s_y")
        s_y_sb = sem("e_y_sb")
        s_added = [sem("s_added0"), sem("s_added1")]
        block = ctx.enter_context(nc.Block())
        ident = t.cst[:, CI:CI + P]

        def tiles_in_use(eng):
            return eng.value_load(t.bound[0:1, 3 + EXPERTS:4 + EXPERTS], min_val=1, max_val=TILES)

        def is_first(m):
            return isinstance(m, int)

        def steps(eng, body):
            tiles = tiles_in_use(eng)
            for b in (1, 0):
                body(0, b, 2 - b)
            with eng.Fori(0, TILES // (2 * INNER)) as outer:
                with eng.If(outer * (2 * INNER) + 2 < tiles):
                    with eng.Fori(0, INNER) as inner:
                        m = outer * INNER + inner + 1
                        with eng.If(m * 2 < tiles):
                            for b in (1, 0):
                                body(m, b, m * 2 + (2 - b))

        @block.sync
        def _(sp):
            for b in range(NW - 2):
                sp.wait_ge(s_w[b], 48)
                sp.nop().then_inc(s_expert, 1)
            with sp.Fori(1, EXPERTS // NW) as m:
                for b in range(NW):
                    turn = m * NW + b
                    sp.wait_ge(s_w[(b + 2) % NW], (m + (b >= 2)) * 48)
                    sp.nop().then_inc(s_expert, 1)
                    e = turn_expert(sp, t, turn)
                    sp.wait_ge(s_y, sp.value_load(t.bound[0:1, bass.ds(turn, 1)], min_val=1, max_val=TILES))
                    load_expert(sp, t, b, e, gate_up, down_a, down_b)
            for b in range(2, NW):
                sp.wait_ge(s_w[b], 48 * (EXPERTS // NW))
                sp.nop().then_inc(s_expert, 1)
            rounds = (tiles_in_use(sp) + 1) >> 1
            for b in range(2):
                sp.wait_ge(s_added[b], rounds * 16)
                sp.wait_ge(s_x[b], (rounds + (2 - b)) * 16)
            sp.nop().then_inc(s_end, 1)

        @block.gpsimd
        def _(pool):
            def read(b):
                pool.indirect_dma_start(x[:, b, :], None, xrows, bass.IndirectOffsetOnAxis(ap=read_at[:, b:b + 1], axis=0),
                                        bounds_check=TOK - 1, oob_is_err=False).then_inc(s_x[b], 16)

            def add(b):
                pool.indirect_dma_start(out, bass.IndirectOffsetOnAxis(ap=add_at[:, b:b + 1], axis=0), y[:, b, :], None,
                                        bounds_check=TOK + P - 1, oob_is_err=True,
                                        compute_op=ALU.add).then_inc(s_added[b], 16)

            for n in range(3):
                pool.wait_ge(s_read_at, n + 1)
                if n == 2:
                    pool.wait_ge(s_xT, 1)
                    pool.wait_ge(s_weight, 1)
                read(n % 2)

            def body(m, b, i):
                pool.wait_ge(s_read_at, i + 3)
                pool.wait_ge(s_xT, i + 1)
                pool.wait_ge(s_weight, i + 1)
                pool.nop().then_inc(s_pool_step, 1)
                read(b)
                pool.wait_ge(s_add_at, i)
                pool.wait_ge(s_y_sb, i)
                if not (is_first(m) and b):
                    pool.wait_ge(s_added[b], (m + (1 - b)) * 16)
                pool.nop().then_inc(s_pool_step, 1)
                add(1 - b)

            steps(pool, body)

        @block.tensor
        def _(pe):
            def turn_x(b):
                for c in range(KC):
                    last = pe.transpose(xT_p[:, c * P:(c + 1) * P], x[:, b, c * P:(c + 1) * P], ident)
                last.then_inc(s_xT, 1)

            def turn_of(i):
                return pe.value_load(t.tile_turn[0:1, bass.ds(i, 1)], min_val=0, max_val=EXPERTS - 1)

            def multiply(b, turn):
                pe.wait_ge(s_expert, turn + 1)
                at = (turn & (NW - 1)) * (KC * GU)
                for c in range(KC):
                    last = pe.matmul(gu_p[:, 0:GU], xT[:, b, c * P:(c + 1) * P], w_gu[:, bass.ds(at + c * GU, GU)],
                                     start=(c == 0), stop=(c == KC - 1))
                last.then_inc(s_gu, 1)

            def turn_h():
                pe.transpose(hT_p[:, 0:P], h[:, 0:P], ident)
                pe.transpose(hT_p[0:I2, P:2 * P], h[:, P:INTER], ident).then_inc(s_hT, 1)

            pe.wait_ge(s_x[0], 16)
            turn_x(0)
            pe.wait_ge(s_xT_sb, 1)
            multiply(0, turn_of(0))
            pe.wait_ge(s_x[1], 16)
            turn_x(1)

            def body(m, b, i):
                turn = turn_of(i)
                at = (turn_of(i - 1) & (NW - 1)) * D
                pe.wait_ge(s_h, i)
                turn_h()
                pe.wait_ge(s_xT_sb, i + 1)
                multiply(b, turn)
                pe.wait_ge(s_x[1 - b], m * 16 + 32)
                turn_x(1 - b)
                pe.wait_ge(s_hT_sb, i)
                if not (is_first(m) and b):
                    pe.wait_ge(s_y_sb, i - 1)
                pe.matmul(y_p[:], hT[:, 0, :], w_da[:, bass.ds(at, D)], start=True, stop=False)
                pe.matmul(y_p[:], hT[0:I2, 1, :], w_db[:, bass.ds(at, D)], start=False, stop=True).then_inc(s_y, 1)

            steps(pe, body)

        @block.scalar
        def _(act):
            def copy_xT(b):
                act.copy(xT[:, b, :], xT_p[:]).then_inc(s_xT_sb, 1)

            def take_weight(b, i):
                e = act.value_load(t.tile_expert[0:1, bass.ds(i, 1)], min_val=0, max_val=EXPERTS - 1)
                act.copy(weight[:, b:b + 1], x[:, b, bass.ds(e + D, 1)]).then_inc(s_weight, 1)

            def gate_tile():
                act.activation(gated[:], gu_p[:, 0:INTER], ACT.Silu).then_inc(s_silu, 1)

            act.wait_ge(s_xT, 1)
            copy_xT(0)
            take_weight(0, 0)
            act.wait_ge(s_gu, 1)
            gate_tile()
            act.wait_ge(s_xT, 2)
            copy_xT(1)
            take_weight(1, 1)

            def body(m, b, i):
                act.wait_ge(s_gu, i + 1)
                act.wait_ge(s_h, i)
                gate_tile()
                act.wait_ge(s_xT, i + 2)
                copy_xT(1 - b)
                act.wait_ge(s_y, i)
                if not is_first(m):
                    act.wait_ge(s_added[1 - b], m * 16)
                act.activation(y[:, 1 - b, :], y_p[:], ACT.Copy, scale=weight[:, 1 - b:2 - b]).then_inc(s_y_sb, 1)
                act.wait_ge(s_y_sb, i)
                take_weight(1 - b, i + 1)

            steps(act, body)

        @block.vector
        def _(dve):
            def next_read(b, i):
                dve.tensor_copy(read_at[:, b:b + 1], t.gather[:, bass.ds(i, 1)]).then_inc(s_read_at, 1)

            for b in range(2):
                next_read(b, b)
            dve.wait_ge(s_x[0], 16)
            next_read(0, 2)

            def product():
                dve.tensor_tensor(h[:], gated[:], gu_p[:, INTER:GU], ALU.mult).then_inc(s_h, 1)

            def copy_hT():
                dve.tensor_copy(hT[0:I2, 1, :], hT_p[0:I2, P:2 * P])
                dve.tensor_copy(hT[:, 0, :], hT_p[:, 0:P]).then_inc(s_hT_sb, 1)

            dve.wait_ge(s_silu, 1)
            product()

            def body(m, b, i):
                dve.wait_ge(s_hT, i)
                if not (is_first(m) and b):
                    dve.wait_ge(s_y, i - 1)
                copy_hT()
                if not is_first(m):
                    dve.wait_ge(s_added[1 - b], m * 16)
                dve.tensor_copy(add_at[:, 1 - b:2 - b], t.scatter[:, bass.ds(i - 1, 1)]).then_inc(s_add_at, 1)
                dve.wait_ge(s_x[b], (m + (2 - b)) * 16)
                next_read(b, i + 2)
                dve.wait_ge(s_silu, i + 1)
                product()

            steps(dve, body)


def program(nc, ids, hot_ids, hot_w, cold_w, proj, wqkv, wo, gate, gate_up, down_a, down_b, cst, rope, out):
    t = Chip()
    table = nc.dram_tensor("token_table", (VOCAB, 4), I32).ap()
    xrows = nc.dram_tensor("expert_rows", (TOK, XROW), F32).ap()
    with ExitStack() as ctx:
        sb = lambda n, s, d: ctx.enter_context(nc.sbuf_tensor(n, s, d))
        t.h = sb("h", [P, NT + 1, D], F32)
        t.cst = sb("cst", [P, CST_COLS], F32)
        t.stats = sb("ln_stats", [P, NT, 6], F32)
        with ExitStack() as until_routed:
            early = lambda n, s, d: until_routed.enter_context(nc.sbuf_tensor(n, s, d))
            t.ln = early("ln", [P, NT, 2], F32)
            t.wq_hi, t.wq_lo = early("wq_hi", [P, KC, QKV], F32R), early("wq_lo", [P, KC, QKV], F32R)
            t.wo_hi, t.wo_lo = early("wo_hi", [P, KC, D], F32R), early("wo_lo", [P, KC, D], F32R)
            embed(nc, t, ids, hot_ids, hot_w, cold_w, proj, wqkv, wo, cst, table)
            attend(nc, t, rope)
        t.bound = sb("bound", [1, EXPERTS + 4], I32)
        t.tile_expert = sb("tile_expert", [1, SLOTS], I32)
        t.tile_turn = sb("tile_turn", [1, SLOTS], I32)
        t.turn_expert = sb("turn_expert", [1, EXPERTS], I32)
        t.gather = sb("gather", [P, SLOTS], I32)
        t.scatter = sb("scatter", [P, SLOTS], I32)
        t.w_gu = sb("w_gu", [P, NW * KC * GU], F32)
        t.w_da = sb("w_da", [P, NW * D], F32)
        t.w_db = sb("w_db", [INTER - P, NW * D], F32)
        t.s_w = [ctx.enter_context(nc.semaphore(f"s_w{b}")) for b in range(NW)]
        route(nc, t, gate, gate_up, down_a, down_b, xrows, out)
        experts(nc, t, gate_up, down_a, down_b, xrows, out)


def by_partition(w):
    return w.reshape(-1, P, w.shape[-1]).transpose(1, 0, 2)


def kernel(**inputs):
    import concourse.bacc as bacc
    from concourse.bass_utils import run_bass_kernel_spmd

    given = {name: np.asarray(a) for name, a in inputs.items()}
    q_order, k_order = head_order()
    w_gu = given["L0_ffn_gate_up_proj"].transpose(0, 2, 1).reshape(EXPERTS, KC, P, 2 * INTER)
    w_down = given["L0_ffn_down_proj"].transpose(0, 2, 1)
    laid = dict(
        ids=given["x"].reshape(NT, P).T,
        hot_ids=given["L0_tok_hot_token_ids"],
        hot_w=given["L0_tok_hot_emb_w"],
        cold_w=given["L0_tok_cold_emb_w"],
        proj=given["L0_tok_proj_w"].T,
        wqkv=by_partition(np.concatenate([given["L0_attn_wq"][q_order], given["L0_attn_wk"][k_order],
                                          given["L0_attn_wv"]], 0).T),
        wo=by_partition(given["L0_attn_wo"].T),
        gate=by_partition(given["L0_ffn_gate_weight"].T),
        gate_up=w_gu.transpose(0, 2, 1, 3).reshape(EXPERTS, P, KC * 2 * INTER),
        down_a=w_down[:, :P],
        down_b=w_down[:, P:],
        constants=constants(),
        rope=rope_table(),
    )
    nc = bacc.Bacc("TRN2", target_bir_lowering=False, num_devices=1)
    arrays, args = {}, []
    for name, a in laid.items():
        arrays["in_" + name] = np.ascontiguousarray(a)
        args.append(nc.dram_tensor("in_" + name, a.shape, mybir.dt.from_np(a.dtype), kind="ExternalInput").ap())
    args.append(nc.dram_tensor("out_rows", (TOK + P, D), F32, kind="ExternalOutput").ap())
    program(nc, *args)
    r = run_bass_kernel_spmd(nc, [arrays], core_ids=[0])
    return r.results[0]["out_rows"][:TOK].reshape(BATCH, SEQ, D)
```
